# Optimizing a Trainium2 kernel written in Bass

```python
import numpy as np
import jax
import jax.numpy as jnp

def _softmax(x, axis=-1):
    return jax.nn.softmax(x, axis=axis)

def _gelu(x):
    return jax.nn.gelu(x, approximate=True)

def _silu(x):
    return jax.nn.silu(x)

def _sigmoid(x):
    return jax.nn.sigmoid(x)

def _layernorm(x, axis=-1, eps=1e-05):
    m = jnp.mean(x, axis=axis, keepdims=True)
    v = jnp.var(x, axis=axis, keepdims=True)
    return (x - m) / jnp.sqrt(v + eps)

def _scatter_add(tgt, idx, src, axis=0):
    return tgt.at[idx].add(src)

def _segment_sum(src, seg, n):
    return jax.ops.segment_sum(src, seg, n)
kernel_name = 'mk_gnn_resnorm_d4_gnn_r64_961fe4'

def setup_inputs(seed: int=0):
    np.random.seed(seed)
    _w = jnp.asarray

    def _rec_inputs():
        import jax
        import jax.numpy as jnp
        _gk = jax.random.key(seed)
        x = -0.0003713 + 1 * jax.random.normal(jax.random.fold_in(_gk, 1), (50000, 256), jnp.float32)
        src = jax.random.randint(jax.random.fold_in(_gk, 2), (25000,), 0, 50000, jnp.int32)
        dst = jax.random.randint(jax.random.fold_in(_gk, 3), (25000,), 0, 50000, jnp.int32)
        _o = jnp.argsort(dst, stable=True)
        src = src[_o]
        dst = dst[_o]
        edge_attr_64 = -9.77346e-05 + 0.999888 * jax.random.normal(jax.random.fold_in(_gk, 12), (25000, 64), jnp.float32)
        edge_weight = jax.random.uniform(jax.random.fold_in(_gk, 14), (25000,), jnp.float32, 0.0, 0.999999)
        return (x, src, dst, edge_attr_64, edge_weight)
    x, src, dst, edge_attr_64, edge_weight = _rec_inputs()

    def _L0_gnn_setup():
        import jax, jax.numpy as jnp
        import numpy as np
        N_NODES = 50000
        EPS = 1e-12
        key = jax.random.key(seed)
        k1, k2, k3 = jax.random.split(key, 3)
        d_in, d_out, n_edges = (256, 256, 12500)
        input_matrix = jax.random.normal(k1, (N_NODES, d_in), dtype=jnp.float32)
        adjacency_coo_matrix = jax.random.randint(k2, (2, n_edges), 0, N_NODES, dtype=jnp.int64)
        W = jax.random.normal(k3, (2 * d_in, d_out), dtype=jnp.float32) * (1.0 / np.sqrt(2 * d_in))
        b = jnp.zeros((d_out,), dtype=jnp.float32)
        return {'input_matrix': input_matrix, 'adjacency_coo_matrix': adjacency_coo_matrix, 'W': W, 'b': b}
    _L0_gnn_all = _L0_gnn_setup()
    _L0_gnn_in = {k: v for k, v in _L0_gnn_all.items() if k in ('W', 'b')}
    del _L0_gnn_all

    def _L1_gnn_setup():
        import jax, jax.numpy as jnp
        import numpy as np
        ALPHA = 0.2
        key = jax.random.key(seed)
        ks = jax.random.split(key, 6)
        N, E, F_IN, F_OUT, E_DIM = (50000, 12500, 256, 256, 64)
        h = jax.random.normal(ks[0], (N, F_IN), dtype=jnp.float32)
        e_feat = jax.random.normal(ks[1], (E, E_DIM), dtype=jnp.float32)
        W = jax.random.normal(ks[2], (F_OUT, F_IN), dtype=jnp.float32) * (1.0 / np.sqrt(F_IN))
        A = jax.random.normal(ks[3], (1, 2 * F_OUT + E_DIM), dtype=jnp.float32) * 0.05
        src = jax.random.randint(ks[4], (E,), 0, N, dtype=jnp.int32)
        dst = jax.random.randint(ks[5], (E,), 0, N, dtype=jnp.int32)
        return {'h': h, 'e_feat': e_feat, 'W': W, 'A': A, 'src': src, 'dst': dst}
    _L1_gnn_all = _L1_gnn_setup()
    _L1_gnn_in = {k: v for k, v in _L1_gnn_all.items() if k in ('W', 'A')}
    del _L1_gnn_all

    def _L2_gnn_setup():
        import jax, jax.numpy as jnp
        import numpy as np
        N_NODES = 18870
        N_EDGES = 18750
        DIM = 256
        EPS = 1e-05

        def _layer_norm(x, g, b):
            mu = jnp.mean(x, axis=-1, keepdims=True)
            var = jnp.mean(jnp.square(x - mu), axis=-1, keepdims=True)
            return (x - mu) * jax.lax.rsqrt(var + EPS) * g + b

        def _gcn_conv(x, edge_index, edge_weight, W, b):
            n = x.shape[0]
            row, col = (edge_index[0], edge_index[1])
            loop = jnp.arange(n, dtype=row.dtype)
            row = jnp.concatenate([row, loop])
            col = jnp.concatenate([col, loop])
            ew = jnp.concatenate([edge_weight, jnp.ones((n,), dtype=x.dtype)])
            deg = jax.ops.segment_sum(ew, col, num_segments=n)
            dis = jnp.where(deg > 0, jax.lax.rsqrt(jnp.where(deg > 0, deg, 1.0)), 0.0)
            norm = dis[row] * ew * dis[col]
            h = x @ W.T
            msg = h[row] * norm[:, None]
            out = jax.ops.segment_sum(msg, col, num_segments=n)
            return out + b

        def _block(x, edge_index, edge_weight, g, bln, W, b):
            h = _layer_norm(x, g, bln)
            h = _gcn_conv(h, edge_index, edge_weight, W, b)
            h = jax.nn.relu(h)
            return x + h
        key = jax.random.key(seed)
        ks = jax.random.split(key, 8)
        s = 0.05
        return {'x': jax.random.normal(ks[0], (N_NODES, DIM), dtype=jnp.float32), 'edge_index': jax.random.randint(ks[1], (2, N_EDGES), 0, N_NODES, dtype=jnp.int64) if jax.config.jax_enable_x64 else jax.random.randint(ks[1], (2, N_EDGES), 0, N_NODES).astype(jnp.int32), 'edge_weight': jax.random.uniform(ks[2], (N_EDGES,), dtype=jnp.float32), 'ln6_g': jnp.ones((DIM,), jnp.float32), 'ln6_b': jnp.zeros((DIM,), jnp.float32), 'W6': jax.random.normal(ks[3], (DIM, DIM), jnp.float32) * s, 'b6': jnp.zeros((DIM,), jnp.float32), 'ln7_g': jnp.ones((DIM,), jnp.float32), 'ln7_b': jnp.zeros((DIM,), jnp.float32), 'W7': jax.random.normal(ks[4], (DIM, DIM), jnp.float32) * s, 'b7': jnp.zeros((DIM,), jnp.float32), 'Wp': jax.random.normal(ks[5], (DIM, DIM), jnp.float32) * s, 'bp': jnp.zeros((DIM,), jnp.float32)}
    _L2_gnn_all = _L2_gnn_setup()
    _L2_gnn_in = {k: v for k, v in _L2_gnn_all.items() if k in ('ln6_g', 'ln6_b', 'W6', 'b6', 'ln7_g', 'ln7_b', 'W7', 'b7', 'Wp', 'bp')}
    del _L2_gnn_all

    def _L3_gnn_setup():
        import jax, jax.numpy as jnp
        import numpy as np
        N = 50000
        E = 12500
        IN_C = 256
        HID = 64
        HEADS = 4
        NEG_SLOPE = 0.2

        def _gat_conv(x, W, att_src, att_dst, b, src, dst):
            n = x.shape[0]
            h = (x @ W).reshape(n, HEADS, HID)
            a_s = jnp.einsum('nhc,hc->nh', h, att_src)
            a_d = jnp.einsum('nhc,hc->nh', h, att_dst)
            e = jax.nn.leaky_relu(a_s[src] + a_d[dst], NEG_SLOPE)
            m = jax.ops.segment_max(e, dst, num_segments=n)
            ex = jnp.exp(e - m[dst])
            denom = jax.ops.segment_sum(ex, dst, num_segments=n)
            alpha = ex / denom[dst]
            msg = h[src] * alpha[:, :, None]
            out = jax.ops.segment_sum(msg, dst, num_segments=n)
            return out.reshape(n, HEADS * HID) + b
        key = jax.random.key(seed)
        ks = jax.random.split(key, 12)
        x = jax.random.normal(ks[0], (N, IN_C), dtype=jnp.float32)
        edge_index = jax.random.randint(ks[1], (2, E), 0, N, dtype=jnp.int64)
        s1 = 1.0 / np.sqrt(IN_C)
        W1 = jax.random.normal(ks[2], (IN_C, HEADS * HID), dtype=jnp.float32) * s1
        att_src1 = jax.random.normal(ks[3], (HEADS, HID), dtype=jnp.float32) * 0.1
        att_dst1 = jax.random.normal(ks[4], (HEADS, HID), dtype=jnp.float32) * 0.1
        b1 = jnp.zeros((HEADS * HID,), dtype=jnp.float32)
        s2 = 1.0 / np.sqrt(HEADS * HID)
        W2 = jax.random.normal(ks[5], (HEADS * HID, HEADS * HID), dtype=jnp.float32) * s2
        att_src2 = jax.random.normal(ks[6], (HEADS, HID), dtype=jnp.float32) * 0.1
        att_dst2 = jax.random.normal(ks[7], (HEADS, HID), dtype=jnp.float32) * 0.1
        b2 = jnp.zeros((HEADS * HID,), dtype=jnp.float32)
        return {'x': x, 'edge_index': edge_index, 'W1': W1, 'att_src1': att_src1, 'att_dst1': att_dst1, 'b1': b1, 'W2': W2, 'att_src2': att_src2, 'att_dst2': att_dst2, 'b2': b2}
    _L3_gnn_all = _L3_gnn_setup()
    _L3_gnn_in = {k: v for k, v in _L3_gnn_all.items() if k in ('W1', 'att_src1', 'att_dst1', 'b1', 'W2', 'att_src2', 'att_dst2', 'b2')}
    del _L3_gnn_all
    return {'x': x, 'src': src, 'dst': dst, 'edge_attr_64': edge_attr_64, 'edge_weight': edge_weight, 'L0_gnn_W': _L0_gnn_in['W'], 'L0_gnn_b': _L0_gnn_in['b'], 'L1_gnn_W': _L1_gnn_in['W'], 'L1_gnn_A': _L1_gnn_in['A'], 'L2_gnn_ln6_g': _L2_gnn_in['ln6_g'], 'L2_gnn_ln6_b': _L2_gnn_in['ln6_b'], 'L2_gnn_W6': _L2_gnn_in['W6'], 'L2_gnn_b6': _L2_gnn_in['b6'], 'L2_gnn_ln7_g': _L2_gnn_in['ln7_g'], 'L2_gnn_ln7_b': _L2_gnn_in['ln7_b'], 'L2_gnn_W7': _L2_gnn_in['W7'], 'L2_gnn_b7': _L2_gnn_in['b7'], 'L2_gnn_Wp': _L2_gnn_in['Wp'], 'L2_gnn_bp': _L2_gnn_in['bp'], 'L3_gnn_W1': _L3_gnn_in['W1'], 'L3_gnn_att_src1': _L3_gnn_in['att_src1'], 'L3_gnn_att_dst1': _L3_gnn_in['att_dst1'], 'L3_gnn_b1': _L3_gnn_in['b1'], 'L3_gnn_W2': _L3_gnn_in['W2'], 'L3_gnn_att_src2': _L3_gnn_in['att_src2'], 'L3_gnn_att_dst2': _L3_gnn_in['att_dst2'], 'L3_gnn_b2': _L3_gnn_in['b2']}

def reference(x, src, dst, edge_attr_64, edge_weight, L0_gnn_W, L0_gnn_b, L1_gnn_W, L1_gnn_A, L2_gnn_ln6_g, L2_gnn_ln6_b, L2_gnn_W6, L2_gnn_b6, L2_gnn_ln7_g, L2_gnn_ln7_b, L2_gnn_W7, L2_gnn_b7, L2_gnn_Wp, L2_gnn_bp, L3_gnn_W1, L3_gnn_att_src1, L3_gnn_att_dst1, L3_gnn_b1, L3_gnn_W2, L3_gnn_att_src2, L3_gnn_att_dst2, L3_gnn_b2):
    import jax
    import jax.numpy as jnp

    def _L0_gnn_ref(input_matrix, adjacency_coo_matrix, W, b):
        import jax, jax.numpy as jnp
        import numpy as np
        N_NODES = 50000
        EPS = 1e-12
        src = adjacency_coo_matrix[0]
        dst = adjacency_coo_matrix[1]
        neigh_sum = jax.ops.segment_sum(input_matrix[src], dst, num_segments=N_NODES)
        deg = jax.ops.segment_sum(jnp.ones_like(dst, dtype=input_matrix.dtype), dst, num_segments=N_NODES)
        neigh_mean = neigh_sum / jnp.maximum(deg, 1.0)[:, None]
        h = jnp.concatenate([input_matrix, neigh_mean], axis=-1)
        out = jax.nn.relu(h @ W + b)
        norm = jnp.maximum(jnp.linalg.norm(out, axis=-1, keepdims=True), EPS)
        return out / norm

    def _L1_gnn_ref(h, e_feat, W, A, src, dst):
        import jax, jax.numpy as jnp
        import numpy as np
        ALPHA = 0.2
        N = h.shape[0]
        F_OUT = W.shape[0]
        z = h @ W.T
        z_src = z[src]
        z_dst = z[dst]
        a_src, a_dst, a_e = (A[0, :F_OUT], A[0, F_OUT:2 * F_OUT], A[0, 2 * F_OUT:])
        logits = z_src @ a_src + z_dst @ a_dst + e_feat @ a_e
        e = jax.nn.leaky_relu(logits, ALPHA)
        m = jax.ops.segment_max(e, dst, num_segments=N)
        ex = jnp.exp(e - m[dst])
        denom = jax.ops.segment_sum(ex, dst, num_segments=N)
        alpha = ex / denom[dst]
        h_out = jax.ops.segment_sum(alpha[:, None] * z_src, dst, num_segments=N)
        return h_out

    def _L2_gnn_ref(x, edge_index, edge_weight, ln6_g, ln6_b, W6, b6, ln7_g, ln7_b, W7, b7, Wp, bp):
        import jax, jax.numpy as jnp
        import numpy as np
        N_NODES = 18870
        N_EDGES = 18750
        DIM = 256
        EPS = 1e-05

        def _layer_norm(x, g, b):
            mu = jnp.mean(x, axis=-1, keepdims=True)
            var = jnp.mean(jnp.square(x - mu), axis=-1, keepdims=True)
            return (x - mu) * jax.lax.rsqrt(var + EPS) * g + b

        def _gcn_conv(x, edge_index, edge_weight, W, b):
            n = x.shape[0]
            row, col = (edge_index[0], edge_index[1])
            loop = jnp.arange(n, dtype=row.dtype)
            row = jnp.concatenate([row, loop])
            col = jnp.concatenate([col, loop])
            ew = jnp.concatenate([edge_weight, jnp.ones((n,), dtype=x.dtype)])
            deg = jax.ops.segment_sum(ew, col, num_segments=n)
            dis = jnp.where(deg > 0, jax.lax.rsqrt(jnp.where(deg > 0, deg, 1.0)), 0.0)
            norm = dis[row] * ew * dis[col]
            h = x @ W.T
            msg = h[row] * norm[:, None]
            out = jax.ops.segment_sum(msg, col, num_segments=n)
            return out + b

        def _block(x, edge_index, edge_weight, g, bln, W, b):
            h = _layer_norm(x, g, bln)
            h = _gcn_conv(h, edge_index, edge_weight, W, b)
            h = jax.nn.relu(h)
            return x + h
        x = _block(x, edge_index, edge_weight, ln6_g, ln6_b, W6, b6)
        x = _block(x, edge_index, edge_weight, ln7_g, ln7_b, W7, b7)
        return x @ Wp.T + bp

    def _L3_gnn_ref(x, edge_index, W1, att_src1, att_dst1, b1, W2, att_src2, att_dst2, b2):
        import jax, jax.numpy as jnp
        import numpy as np
        N = 50000
        E = 12500
        IN_C = 256
        HID = 64
        HEADS = 4
        NEG_SLOPE = 0.2

        def _gat_conv(x, W, att_src, att_dst, b, src, dst):
            n = x.shape[0]
            h = (x @ W).reshape(n, HEADS, HID)
            a_s = jnp.einsum('nhc,hc->nh', h, att_src)
            a_d = jnp.einsum('nhc,hc->nh', h, att_dst)
            e = jax.nn.leaky_relu(a_s[src] + a_d[dst], NEG_SLOPE)
            m = jax.ops.segment_max(e, dst, num_segments=n)
            ex = jnp.exp(e - m[dst])
            denom = jax.ops.segment_sum(ex, dst, num_segments=n)
            alpha = ex / denom[dst]
            msg = h[src] * alpha[:, :, None]
            out = jax.ops.segment_sum(msg, dst, num_segments=n)
            return out.reshape(n, HEADS * HID) + b
        loop = jnp.arange(N, dtype=edge_index.dtype)
        src = jnp.concatenate([edge_index[0], loop])
        dst = jnp.concatenate([edge_index[1], loop])
        h = _gat_conv(x, W1, att_src1, att_dst1, b1, src, dst)
        h = jax.nn.elu(h)
        h = _gat_conv(h, W2, att_src2, att_dst2, b2, src, dst)
        h = jax.nn.elu(h)
        return h
    edge_index = jnp.stack([src, dst])
    x = _layernorm(x + _L0_gnn_ref(x, edge_index, L0_gnn_W, L0_gnn_b), axis=-1)
    x = _layernorm(x + _L1_gnn_ref(x, edge_attr_64, L1_gnn_W, L1_gnn_A, src, dst), axis=-1)
    x = _layernorm(x + _L2_gnn_ref(x, edge_index, edge_weight, L2_gnn_ln6_g, L2_gnn_ln6_b, L2_gnn_W6, L2_gnn_b6, L2_gnn_ln7_g, L2_gnn_ln7_b, L2_gnn_W7, L2_gnn_b7, L2_gnn_Wp, L2_gnn_bp), axis=-1)
    x = _layernorm(x + _L3_gnn_ref(x, edge_index, L3_gnn_W1, L3_gnn_att_src1, L3_gnn_att_dst1, L3_gnn_b1, L3_gnn_W2, L3_gnn_att_src2, L3_gnn_att_dst2, L3_gnn_b2), axis=-1)
    return x

_drawn_inputs = setup_inputs


def setup_inputs(seed=0):
    import zlib

    import numpy as np

    out = dict(_drawn_inputs(seed))
    spreads = {'L0_gnn_b': (0.0, 0.8),
     'L2_gnn_ln6_g': (1.0, 0.2),
     'L2_gnn_ln6_b': (0.0, 0.1),
     'L2_gnn_b6': (0.0, 0.1),
     'L2_gnn_ln7_g': (1.0, 0.2),
     'L2_gnn_ln7_b': (0.0, 0.1),
     'L2_gnn_b7': (0.0, 0.1),
     'L2_gnn_bp': (0.0, 0.1),
     'L3_gnn_b1': (0.0, 0.1),
     'L3_gnn_b2': (0.0, 0.1)}
    factors = {'L3_gnn_att_dst1': 3.232, 'L3_gnn_att_dst2': 5.97}
    for name, (base, spread) in spreads.items():
        noise = np.random.default_rng([zlib.crc32(name.encode()), seed]).standard_normal(out[name].shape)
        drawn = base * np.exp(spread * noise) if base else spread * noise
        out[name] = jnp.asarray(drawn.astype(out[name].dtype))
    for name, factor in factors.items():
        out[name] = (out[name] * factor).astype(out[name].dtype)
    return out
```

```python
from contextlib import ExitStack

import concourse.bass as bass
from concourse import mybir

F32 = mybir.dt.float32
BF16 = mybir.dt.bfloat16
I32 = mybir.dt.int32
ALU = mybir.AluOpType
ACT = mybir.ActivationFunctionType
AX = mybir.AxisListType

P = 128
D = 256
N = 50000
E = 25000
EDIM = 64
HEADS = 4
HID = D // HEADS

SLOTS = 4
GT = 2
GROUP = GT * P
NGROUPS = -(-N // (GROUP * SLOTS)) * SLOTS
NPAD = NGROUPS * GROUP
NTILES = NPAD // P
NITER = NGROUPS // SLOTS

ETILES = -(-E // (2 * P)) * 2
EPAD = ETILES * P
EROWS = ETILES // 2
HALF = 7
EITER = ETILES // (2 * HALF)
assert EITER * 2 * HALF == ETILES and EROWS <= P and NTILES == 4 * EROWS

SCORES = 2 * HEADS
CW = D + SCORES
NO_EDGES = EPAD
BIG = 1e30
FAR = 1000000
PAD_NODE = 60000
LN_EPS = 1e-5


def build(nc, a, out):
    ctx = ExitStack()
    with ctx:
        def sb(name, shape, dt=F32):
            return ctx.enter_context(nc.sbuf_tensor(name, shape, dt))

        def dram(name, shape, dt=F32):
            return nc.dram_tensor(name, shape, dt).ap()

        g = {}
        for name in ("x1", "x2", "h6", "y6", "h7", "x3", "p1", "p2"):
            g[name] = dram("t_" + name, [NPAD, D])
        g["scores"] = dram("t_scores", [NPAD, SCORES])
        g["pieces"] = dram("t_pieces", [EPAD + 1, CW])
        g["piece_of"] = dram("t_piece_of", [NPAD, 1], I32)
        g["credit"] = dram("t_credit", [P, 16 * 8])

        for name, shape in (("ident", [P, P]), ("iota", [P, P]), ("eps", [P, 1]), ("zero", [P, 8]),
                            ("w0", [P, 4, D]), ("w1T", [P, 2, D]), ("w6T", [P, 2, D]), ("w7T", [P, 2, D]),
                            ("wpT", [P, 2, D]), ("g1w", [P, 2, CW]), ("g2w", [P, 2, CW]),
                            ("vsrc", [P, D]), ("vdst", [P, D]),
                            ("ln6g", [P, GT, D]), ("ln6b", [P, GT, D]), ("ln7g", [P, GT, D]), ("ln7b", [P, GT, D]),
                            ("b6", [P, D]), ("b7", [P, D]), ("gb1", [P, GT, D]), ("gb2", [P, GT, D]),
                            ("rank", [P, ETILES]), ("first", [P, ETILES]), ("ew", [P, ETILES]), ("ee", [P, ETILES]),
                            ("startR", [EROWS, 2 * P]), ("endR", [EROWS, 2 * P]),
                            ("startrow", [HEADS, EROWS]), ("endrow", [HEADS, EROWS]),
                            ("same", [EROWS, 2, 2, EROWS]),
                            ("dis", [P, NTILES])):
            g[name] = sb(name, shape)
        g["ones3"] = sb("ones3", [3, P], BF16)
        g["b0"] = sb("b0", [3, D], BF16)
        g["bp"] = sb("bp", [3, D], BF16)
        g["src"] = sb("srcs", [P, ETILES + 2 * HALF], I32)
        g["dst"] = sb("dsts", [P, ETILES + 2 * HALF], I32)
        g["piece"] = sb("piece", [P, NTILES + GT * SLOTS], I32)
        g["target"] = sb("target", [EROWS, 2], I32)
        g["exs"] = sb("exs", [P, ETILES, HEADS])
        g["exd"] = sb("exd", [P, ETILES, SCORES])

        weights(nc, a, g)
        edge_tables(nc, a, g)
        edge_pass(nc, g, "count", a["x"], 0)
        sage_nodes(nc, g, a["x"])
        edge_scores(nc, g, 1)
        edge_pass(nc, g, "attention", g["x1"], 1)
        attention_nodes(nc, g)
        edge_pass(nc, g, "gcn", g["h6"], 0)
        gcn_nodes(nc, g, last=False)
        edge_pass(nc, g, "gcn", g["h7"], 0)
        gcn_nodes(nc, g, last=True)
        edge_scores(nc, g, HEADS)
        edge_pass(nc, g, "gat", g["p1"], SCORES)
        gat_nodes(nc, g, last=False, out=None)
        edge_scores(nc, g, HEADS)
        edge_pass(nc, g, "gat", g["p2"], SCORES)
        gat_nodes(nc, g, last=True, out=out)


PHASE = [0]


class Phase:

    def __init__(self, nc):
        self.nc = nc
        self.ctx = ExitStack()
        self.sems = []
        PHASE[0] += 1
        self.tag = f"_{PHASE[0]}"

    def __enter__(self):
        self.ctx.__enter__()
        return self

    def __exit__(self, *e):
        self.nc.clear_and_free_semaphores(self.sems)
        self.nc.all_engine_barrier()
        return self.ctx.__exit__(*e)

    def sb(self, name, shape, dt=F32):
        return self.ctx.enter_context(self.nc.sbuf_tensor(name + self.tag, shape, dt))

    def ps(self, name, shape, dt=F32):
        return self.ctx.enter_context(self.nc.psum_tensor(name + self.tag, shape, dt))

    def sem(self, name):
        s = self.nc.alloc_semaphore(name + self.tag)
        self.sems.append(s)
        return s


def chain(eng, sem):
    n = [0]

    def link(ins):
        n[0] += 1
        ins.then_inc(sem, 1)
        eng.wait_ge(sem, n[0])
    return link


def spread(ap, shape):
    return ap.to_broadcast(shape)


def weights(nc, a, g):
    with Phase(nc) as ph:
        raw = {k: ph.sb("raw_" + k, [P, 2, D]) for k in ("w1", "w6", "w7", "wp")}
        acol = ph.sb("acol", [P, 2, 2])
        arow = ph.sb("arow", [P, 2, 2, P])
        att = ph.sb("att", [P, 4, D])
        prod = ph.sb("prod", [P, 2, 4, D])
        bias = ph.sb("bias", [1, 2, D])
        parts = ph.sb("parts", [1, 2, 3, D], BF16)
        rest = ph.sb("rest", [1, 2, 2, D])
        pt = [ph.ps(f"pt{k}", [P, 2 * D]) for k in range(4)]
        pv = ph.ps("pv", [P, 2, D])
        loaded, zeroed, done, transposed, vecs = (ph.sem(n) for n in ("loaded", "zeroed", "done", "transposed", "vecs"))
        moved, split = ph.sem("moved"), ph.sem("split")
        names = (("w1", "L1_gnn_W", "w1T"), ("w6", "L2_gnn_W6", "w6T"), ("w7", "L2_gnn_W7", "w7T"), ("wp", "L2_gnn_Wp", "wpT"))
        loads = [0]
        with nc.Block() as block:
            @block.sync
            def _(sp):
                def load(o, i):
                    sp.dma_start(o, i).then_inc(loaded, 16)
                    loads[0] += 1
                for k, name, _ in names:
                    load(raw[k][:], a[name].rearrange("(c p) k -> p c k", p=P))
                load(g["w0"][:], a["L0_gnn_W"].rearrange("(c p) k -> p c k", p=P))
                load(g["g1w"][:, :, 0:D], a["L3_gnn_W1"].rearrange("(c p) k -> p c k", p=P))
                load(g["g2w"][:, :, 0:D], a["L3_gnn_W2"].rearrange("(c p) k -> p c k", p=P))
                with nc.allow_non_contiguous_dma(reason="512 scattered words, once"):
                    for k in range(2):
                        for c in range(2):
                            load(acol[:, k, c:c + 1], a["L1_gnn_A"][0:1, k * D + c * P:k * D + (c + 1) * P].rearrange("a p -> p a"))
                for k, name in enumerate(("L3_gnn_att_src1", "L3_gnn_att_dst1", "L3_gnn_att_src2", "L3_gnn_att_dst2")):
                    load(att[:, k, :], a[name].rearrange("(a h) c -> a (h c)", a=1).to_broadcast([P, D]))
                for k, name in (("ln6g", "L2_gnn_ln6_g"), ("ln6b", "L2_gnn_ln6_b"), ("ln7g", "L2_gnn_ln7_g"),
                                ("ln7b", "L2_gnn_ln7_b"), ("gb1", "L3_gnn_b1"), ("gb2", "L3_gnn_b2")):
                    for j in range(GT):
                        load(g[k][:, j, :], a[name].rearrange("(a c) -> a c", a=1).to_broadcast([P, D]))
                for k, name in (("b6", "L2_gnn_b6"), ("b7", "L2_gnn_b7")):
                    load(g[k][:], a[name].rearrange("(a c) -> a c", a=1).to_broadcast([P, D]))
                for k, name in enumerate(("L0_gnn_b", "L2_gnn_bp")):
                    load(bias[:, k, :], a[name].rearrange("(a c) -> a c", a=1))
                sp.wait_ge(split, 1)
                for k, name in enumerate(("b0", "bp")):
                    for part in range(3):
                        sp.dma_start(g[name][part:part + 1, :], parts[:, k, part, :]).then_inc(moved, 16)
                sp.wait_ge(moved, 6 * 16)

            @block.gpsimd
            def _(pool):
                pool.memset(g["ident"][:], 0.0).then_inc(zeroed, 1)
                pool.wait_ge(zeroed, 1)
                pool.affine_select(out=g["ident"][:], in_=g["ident"][:], compare_op=ALU.not_equal, fill=1.0, base=0,
                                   pattern=[[-1, P]], channel_multiplier=1).then_inc(zeroed, 1)
                pool.iota(g["iota"][:], [[1, P]], base=0, channel_multiplier=0,
                          allow_small_or_imprecise_dtypes=True).then_inc(zeroed, 1)

            @block.tensor
            def _(pe):
                pe.wait_ge(zeroed, 3)
                pe.wait_ge(loaded, 16 * loads[0])
                for n, (k, _, _) in enumerate(names):
                    for ci in range(2):
                        for co in range(2):
                            last = pe.transpose(pt[n][:, ci * D + co * P:ci * D + (co + 1) * P],
                                                raw[k][:, co, ci * P:(ci + 1) * P], g["ident"][:])
                    last.then_inc(transposed, 1)
                pe.wait_ge(vecs, 1)
                for k in range(2):
                    for c in range(2):
                        last = pe.matmul(pv[:, k, :], arow[:, k, c, :], raw["w1"][:, c, :], start=(c == 0), stop=(c == 1))
                last.then_inc(transposed, 1)

            @block.vector
            def _(dve):
                link = chain(dve, done)
                dve.memset(g["eps"][:], LN_EPS)
                dve.memset(g["ones3"][:], 1.0)
                dve.memset(g["zero"][:], 0.0)
                link(dve.memset(arow[:], 1.0))
                dve.wait_ge(loaded, 16 * loads[0])
                for k in range(2):
                    for c in range(2):
                        last = dve.tensor_scalar(arow[:, k, c, :], arow[:, k, c, :], acol[:, k, c:c + 1], None, ALU.mult)
                last.then_inc(vecs, 1)
                for w, base in ((g["g1w"], 0), (g["g2w"], 2)):
                    for k in range(2):
                        for c in range(2):
                            last = dve.tensor_tensor(prod[:, c, base + k, :], w[:, c, 0:D], att[:, base + k, :], ALU.mult)
                link(last)
                for w, base in ((g["g1w"], 0), (g["g2w"], 2)):
                    for k in range(2):
                        for c in range(2):
                            last = dve.tensor_reduce(w[:, c, D + k * HEADS:D + (k + 1) * HEADS],
                                                     prod[:, c, base + k, :].rearrange("p (h c) -> p h c", h=HEADS),
                                                     AX.X, ALU.add)
                link(last)
                link(dve.tensor_copy(parts[:, :, 0, :], bias[:]))
                link(dve.tensor_tensor(rest[:, :, 0, :], bias[:], parts[:, :, 0, :], ALU.subtract))
                link(dve.tensor_copy(parts[:, :, 1, :], rest[:, :, 0, :]))
                link(dve.tensor_tensor(rest[:, :, 1, :], rest[:, :, 0, :], parts[:, :, 1, :], ALU.subtract))
                dve.tensor_copy(parts[:, :, 2, :], rest[:, :, 1, :]).then_inc(split, 1)
                for n, (_, _, k) in enumerate(names):
                    dve.wait_ge(transposed, n + 1)
                    dve.tensor_copy(g[k][:], pt[n][:].rearrange("p (c k) -> p c k", c=2))
                dve.wait_ge(transposed, len(names) + 1)
                dve.tensor_copy(g["vsrc"][:], pv[:, 0, :])
                dve.tensor_copy(g["vdst"][:], pv[:, 1, :])


def edge_tables(nc, a, g):
    full = E // (2 * P)
    tail = E - full * 2 * P
    with Phase(nc) as ph:
        names = ("src", "dst", "prev", "next")
        ints = {k: ph.sb("i_" + k, [EROWS, 2 * P], I32) for k in names}
        rows = {k: ph.sb("r_" + k, [EROWS, 2 * P]) for k in names}
        ewR = ph.sb("ewR", [EROWS, 2 * P])
        before = ph.sb("before", [EROWS, 2], I32)
        beforef = ph.sb("beforef", [EROWS, 2])
        first, lastf, tstart, rank, ones = (ph.sb(n, [EROWS, 2 * P]) for n in ("firstR", "lastR", "tstart", "rankR", "onesR"))
        anyf = ph.sb("anyf", [EROWS, 2, HEADS])
        anyone = ph.sb("anyone", [EROWS, 2])
        cont, key, rep, node0 = (ph.sb(n, [EROWS, 2]) for n in ("cont", "key", "rep", "node0"))
        idx0 = ph.sb("idx0", [EROWS, 2], I32)
        diag = ph.sb("diag", [EROWS, 2, EROWS])
        fdst = ph.sb("fdst", [P, ETILES], I32)
        rowid = ph.sb("rowid", [P, ETILES], I32)
        rowf = ph.sb("rowf", [P, ETILES])
        tbase = ph.sb("tbase", [P, ETILES])
        attr = [ph.sb(f"attr{k}", [P, ETILES // 4, EDIM]) for k in range(2)]
        aerow = ph.sb("aerow", [P, EDIM])
        idx = ph.sb("idxs", [P, 2 * HALF], I32)
        val = ph.sb("vals", [P, 2 * HALF], I32)
        fill = ph.sb("fill", [EROWS, 4 * P], I32)
        pieceR = ph.sb("pieceR", [EROWS, 4 * P], I32)
        pieceF = ph.sb("pieceF", [EROWS, 4 * P])
        pc = [ph.ps(f"pc{k}", [P, 512]) for k in range(5)]
        prow = ph.ps("prow", [P, 2, P])
        pany = ph.ps("pany", [P, 2, P])
        (ready, loaded, done, turned, filled, idxed, told, read, ptrs, attrd, bases) = (
            ph.sem(n) for n in ("ready", "loaded", "done", "turned", "filled", "idxed", "told", "read",
                                "ptrs", "attrd", "bases"))
        passed = ph.sem("passed")
        attrs = [ph.sem(f"attrs{k}") for k in range(4)]
        scattered = [ph.sem(f"scattered{h}") for h in range(2)]
        q4 = ETILES // 4
        nloads = [0]
        with nc.Block() as block:
            @block.sync
            def _(sp):
                sp.wait_ge(ready, 1)
                nloads[0] = 0

                def load(o, i):
                    sp.dma_start(o, i).then_inc(loaded, 16)
                    nloads[0] += 1
                flat = {"src": a["src"], "dst": a["dst"], "prev": a["dst"], "next": a["dst"]}

                def rowsof(k, lo, n):
                    return flat[k][lo:lo + n * 2 * P].rearrange("(q i) -> q i", i=2 * P)

                def one(k, lo, n):
                    return flat[k][lo:lo + n].rearrange("(q i) -> q i", q=1)
                for k in ("src", "dst"):
                    load(ints[k][0:full, :], rowsof(k, 0, full))
                    load(ints[k][full:full + 1, 0:tail], one(k, full * 2 * P, tail))
                load(ints["prev"][0:1, 1:2 * P], one("prev", 0, 2 * P - 1))
                load(ints["prev"][1:full, :], rowsof("prev", 2 * P - 1, full - 1))
                load(ints["prev"][full:full + 1, 0:tail + 1], one("prev", full * 2 * P - 1, tail + 1))
                load(ints["next"][0:full, :], rowsof("next", 1, full))
                load(ints["next"][full:full + 1, 0:tail - 1], one("next", full * 2 * P + 1, tail - 1))
                load(ewR[0:full, :], a["edge_weight"][0:full * 2 * P].rearrange("(q i) -> q i", i=2 * P))
                load(ewR[full:full + 1, 0:tail], a["edge_weight"][full * 2 * P:E].rearrange("(q i) -> q i", q=1))
                with nc.allow_non_contiguous_dma(reason="97 words, once"):
                    load(before[1:EROWS, 0:1], rowsof("dst", 0, EROWS - 1)[:, P - 1:P])
                load(aerow[:], a["L1_gnn_A"][0:1, 2 * D:2 * D + EDIM].to_broadcast([P, EDIM]))
                sp.dma_start(g["piece_of"].rearrange("(q i) a -> q (i a)", q=EROWS), fill[:]).then_inc(filled, 16)
                for k in range(4):
                    lo = k * q4 * P
                    n = min(q4, (E - lo) // P)
                    if k >= 2:
                        sp.wait_ge(attrd, k - 1)
                    if n < q4:
                        sp.dma_start(attr[k % 2][0:E - lo - n * P, n, :], a["edge_attr_64"][lo + n * P:E, :]).then_inc(attrs[k], 16)
                    sp.dma_start(attr[k % 2][:, 0:n, :],
                                 a["edge_attr_64"][lo:lo + n * P, :].rearrange("(t p) c -> p t c", p=P)).then_inc(attrs[k], 16)
                for h in range(2):
                    sp.wait_ge(scattered[h], EITER * HALF * 16)
                sp.dma_start(pieceR[:], g["piece_of"].rearrange("(q i) a -> q (i a)", q=EROWS)).then_inc(ptrs, 16)

            @block.gpsimd
            def _(pool):
                pool.iota(tbase[:], [[P, ETILES]], base=0, channel_multiplier=0,
                          allow_small_or_imprecise_dtypes=True).then_inc(bases, 1)
                pool.wait_ge(filled, 16)
                with pool.Fori(0, EITER) as i:
                    for h in range(2):
                        pool.wait_ge(idxed, 2 * i + h + 1)
                        carry_wait(pool, passed)
                        for j in range(h * HALF, (h + 1) * HALF):
                            pool.indirect_dma_start(g["piece_of"], bass.IndirectOffsetOnAxis(idx[:, j:j + 1], 0),
                                                    val[:, j:j + 1], None, bounds_check=NPAD - 1,
                                                    oob_is_err=False).then_inc(scattered[h], 16)
                for h in range(2):
                    pool.wait_ge(scattered[h], EITER * HALF * 16)
                for h in range(2):
                    pool.indirect_dma_start(g["target"][:, h:h + 1], None, g["piece_of"],
                                            bass.IndirectOffsetOnAxis(idx0[:, h:h + 1], 0), bounds_check=NPAD - 1,
                                            oob_is_err=False).then_inc(told, 16)
                pool.wait_ge(told, 32)

            @block.tensor
            def _(pe):
                pe.wait_ge(turned, 1)
                for k, r in enumerate((rows["src"], rows["dst"], rank, first, ewR)):
                    for h in range(2):
                        last = pe.transpose(pc[k][:, h * P:h * P + EROWS], r[:, h * P:(h + 1) * P], g["ident"][0:EROWS, 0:EROWS])
                last.then_inc(read, 1)
                for k in range(2):
                    last = pe.matmul(pany[0:HEADS, k, 0:EROWS], anyf[:, k, :], g["ident"][0:EROWS, 0:EROWS], start=True, stop=True)
                for h in range(2):
                    last = pe.matmul(prow[0:EROWS, h, 0:EROWS], ones[:, 0:EROWS], diag[:, h, :], start=True, stop=True)
                last.then_inc(read, 1)
                pe.wait_ge(turned, 2)
                for j in range(4):
                    last = pe.transpose(pc[0][:, j * P:j * P + EROWS], pieceF[:, j * P:(j + 1) * P], g["ident"][0:EROWS, 0:EROWS])
                last.then_inc(read, 1)

            @block.vector
            def _(dve):
                link = chain(dve, done)
                for k, v in (("src", 0), ("dst", PAD_NODE), ("prev", PAD_NODE), ("next", -5)):
                    dve.memset(ints[k][:], v)
                dve.memset(before[:], -1)
                dve.memset(ewR[:], 0.0)
                dve.memset(ones[:], 1.0)
                dve.memset(fill[:], NO_EDGES)
                dve.memset(g["target"][:], FAR)
                dve.memset(g["src"][:], 0)
                dve.memset(g["dst"][:], 0)
                dve.memset(g["piece"][:], NO_EDGES)
                link(dve.memset(attr[1][:, q4 - 1, :], 0.0))
                dve.memset(ints["prev"][0:1, 0:1], -1).then_inc(ready, 1)
                dve.wait_ge(loaded, 16 * nloads[0])
                for k in names:
                    last = dve.tensor_copy(rows[k][:], ints[k][:])
                link(last)
                link(dve.tensor_copy(beforef[:], before[:]))
                link(dve.tensor_copy(beforef[:, 1:2], rows["prev"][:, 0:1]))
                dve.tensor_tensor(first[:], rows["dst"][:], rows["prev"][:], ALU.not_equal)
                link(dve.tensor_tensor(lastf[:], rows["dst"][:], rows["next"][:], ALU.not_equal))
                link(dve.tensor_copy(tstart[:], first[:]))
                link(dve.memset(tstart[:].rearrange("q (h i) -> q h i", h=2)[:, :, 0:1], 1.0))
                for h in range(2):
                    s = slice(h * P, (h + 1) * P)
                    dve.tensor_tensor_scan(rank[:, s], ones[:, s], tstart[:, s], -1.0, ALU.mult, ALU.add)
                dve.tensor_scalar(g["startR"][:], first[:], -BIG, None, ALU.mult)
                dve.tensor_scalar(g["endR"][:], lastf[:], -BIG, None, ALU.mult)
                dve.tensor_reduce(anyone[:, 0:1], first[:], AX.X, ALU.max)
                link(dve.tensor_reduce(anyone[:, 1:2], lastf[:], AX.X, ALU.max))
                for k in range(2):
                    dve.tensor_scalar(anyf[:, k, :], ones[:, 0:HEADS], anyone[:, k:k + 1], -BIG, ALU.mult, ALU.mult)
                heads = first[:].rearrange("q (h i) -> q h i", h=2)[:, :, 0]
                dve.tensor_scalar(cont[:], heads, -1.0, 1.0, ALU.mult, ALU.add)
                link(dve.tensor_copy(node0[:], rows["dst"][:].rearrange("q (h i) -> q h i", h=2)[:, :, 0]))
                link(dve.tensor_tensor(rep[:], beforef[:], node0[:], ALU.not_equal))
                link(dve.tensor_tensor(rep[:], rep[:], cont[:], ALU.mult))
                link(dve.tensor_scalar(key[:], node0[:], 1.0, None, ALU.add))
                link(dve.tensor_tensor(key[:], key[:], cont[:], ALU.mult))
                link(dve.tensor_scalar(key[:], key[:], -1.0, None, ALU.add))
                for h in range(2):
                    dve.tensor_scalar(diag[:, h, :], g["ident"][0:EROWS, 0:EROWS], key[:, h:h + 1], None, ALU.mult)
                link(dve.tensor_scalar(beforef[:], rep[:], -float(FAR), float(FAR), ALU.mult, ALU.add))
                link(dve.tensor_tensor(beforef[:], beforef[:], node0[:], ALU.add))
                dve.tensor_copy(idx0[:], beforef[:]).then_inc(turned, 1)
                dve.wait_ge(read, 1)

                def cols(o, k):
                    for h in range(2):
                        last = dve.tensor_copy(o.rearrange("p (q h) -> p h q", h=2)[:, h, :], pc[k][:, h * P:h * P + EROWS])
                    return last
                cols(g["src"][:, 0:ETILES], 0)
                cols(g["dst"][:, 0:ETILES], 1)
                cols(g["rank"][:], 2)
                cols(g["first"][:], 3)
                link(cols(g["ew"][:], 4))
                link(dve.tensor_scalar(rowf[:], g["first"][:], -float(FAR), float(FAR), ALU.mult, ALU.add))
                link(dve.tensor_tensor(rowf[:], rowf[:], g["dst"][:, 0:ETILES], ALU.add))
                link(dve.tensor_copy(fdst[:], rowf[:]))
                dve.wait_ge(bases, 1)
                link(dve.tensor_tensor(rowf[:], tbase[:], g["rank"][:], ALU.add))
                link(dve.tensor_copy(rowid[:], rowf[:]))
                dve.tensor_copy(idx[:], fdst[:, 0:2 * HALF])
                dve.tensor_copy(val[:], rowid[:, 0:2 * HALF]).then_inc(idxed, 2)
                with dve.Fori(0, EITER - 1) as i:
                    for h in range(2):
                        s = slice(h * HALF, (h + 1) * HALF)
                        nxt = bass.ds((i + 1) * 2 * HALF + h * HALF, HALF)
                        dve.wait_ge(scattered[h], (i + 1) * HALF * 16)
                        dve.tensor_copy(idx[:, s], fdst[:, nxt])
                        dve.tensor_copy(val[:, s], rowid[:, nxt]).then_inc(idxed, 1)
                dve.wait_ge(read, 2)
                dve.tensor_copy(g["startrow"][:], pany[0:HEADS, 0, 0:EROWS])
                dve.tensor_copy(g["endrow"][:], pany[0:HEADS, 1, 0:EROWS])
                for h in range(2):
                    for o in range(2):
                        last = dve.tensor_scalar(g["same"][:, h, o, :], prow[0:EROWS, o, 0:EROWS], key[:, h:h + 1],
                                                 cont[:, h:h + 1], ALU.is_equal, ALU.mult)
                link(last)
                for k in range(4):
                    n = min(q4, (E - k * q4 * P) // P)
                    dve.wait_ge(attrs[k], 32 if n < q4 else 16)
                    t = attr[k % 2]
                    link(dve.tensor_tensor(t[:], t[:], spread(aerow[:].rearrange("p (a c) -> p a c", a=1), [P, q4, EDIM]), ALU.mult))
                    dve.tensor_reduce(g["ee"][:, k * q4:(k + 1) * q4], t[:], AX.X, ALU.add).then_inc(attrd, 1)
                dve.wait_ge(ptrs, 16)
                dve.tensor_copy(pieceF[:], pieceR[:]).then_inc(turned, 1)
                dve.wait_ge(read, 3)
                for j in range(4):
                    last = dve.tensor_copy(g["piece"][:, 0:NTILES].rearrange("p (q j) -> p j q", j=4)[:, j, :],
                                           pc[0][:, j * P:j * P + EROWS])
                link(last)


def edge_pass(nc, g, kind, table, beside):
    last_row = table.shape[0] - 1
    slots = 2 * HALF
    with Phase(nc) as ph:
        rows = ph.sb("rows", [P, slots, CW])
        onehot = ph.sb("onehot", [P, slots, P])
        sums = ph.sb("sums", [P, 2, HALF, CW])
        idx = ph.sb("idxs", [P, slots], I32)
        none = ph.sb("none", [1, CW])
        acc = [ph.ps(f"acc{k}", [P, CW]) for k in range(2)]
        passed = ph.sem("passed")
        gathered = [ph.sem(f"gathered{h}") for h in range(2)]
        stored = [ph.sem(f"stored{h}") for h in range(2)]
        (cleared, idx_ready, hot_ready, multiplied, copied, none_ready, none_stored) = (
            ph.sem(n) for n in ("cleared", "idx_ready", "hot_ready", "multiplied", "copied", "none_ready", "none_stored"))
        out = g["pieces"][0:EPAD, :].rearrange("(t r) c -> r t c", r=P)
        with nc.Block() as block:
            @block.gpsimd
            def _(pool):
                pool.wait_ge(cleared, 1)
                with pool.Fori(0, EITER) as i:
                    for h in range(2):
                        pool.wait_ge(idx_ready, 2 * i + h + 1)
                        carry_wait(pool, passed)
                        for j in range(h * HALF, (h + 1) * HALF):
                            pool.indirect_dma_start(rows[:, j, 0:D], None, table,
                                                    bass.IndirectOffsetOnAxis(idx[:, j:j + 1], 0), bounds_check=last_row,
                                                    oob_is_err=False).then_inc(gathered[h], 16)

            @block.vector
            def _(dve):
                dve.memset(rows[:], 0.0)
                dve.memset(none[:], 0.0).then_inc(cleared, 1)
                dve.wait_ge(cleared, 1)
                if kind in ("count", "attention"):
                    dve.memset(rows[:, :, D:D + 1], 1.0)
                dve.memset(none[:, D:D + max(beside, 1)], 1.0 if beside else 0.0).then_inc(none_ready, 1)
                dve.tensor_copy(idx[:], g["src"][:, 0:slots]).then_inc(idx_ready, 2)
                with dve.Fori(0, EITER) as i:
                    for h in range(2):
                        for j in range(h * HALF, (h + 1) * HALF):
                            t = bass.ds(i * slots + j, 1)
                            rank = g["rank"][:, t]
                            dve.wait_ge(multiplied, i * slots + j + 1)
                            if kind in ("attention", "gcn"):
                                w = g["exs"][:, t, 0] if kind == "attention" else g["ew"][:, t]
                                ins = dve.tensor_scalar(onehot[:, j, :], g["iota"][:], rank, w, ALU.is_equal, ALU.mult)
                            else:
                                if kind == "gat" and j % HALF == 0:
                                    dve.wait_ge(gathered[h], (i + 1) * HALF * 16)
                                if kind == "gat":
                                    row = rows[:, j, 0:D].rearrange("p (h c) -> p h c", h=HEADS)
                                    ex = g["exs"][:, t, :].rearrange("p a h -> p (a h)").unsqueeze(2)
                                    dve.tensor_tensor(row, row, ex.to_broadcast([P, HEADS, HID]), ALU.mult)
                                    dve.tensor_copy(rows[:, j, D:CW], g["exd"][:, t, :].rearrange("p a h -> p (a h)"))
                                else:
                                    dve.tensor_copy(rows[:, j, D + 1:D + 2], g["ew"][:, t])
                                ins = dve.tensor_scalar(onehot[:, j, :], g["iota"][:], rank, None, ALU.is_equal)
                            ins.then_inc(hot_ready, 1)
                    for h in range(2):
                        dve.wait_ge(multiplied, (i + 1) * slots + (h + 1) * HALF)
                        s = slice(h * HALF, (h + 1) * HALF)
                        dve.tensor_copy(idx[:, s], g["src"][:, bass.ds((i + 1) * slots + h * HALF, HALF)]).then_inc(idx_ready, 1)

            @block.tensor
            def _(pe):
                pe.sem_inc(multiplied, slots)
                with pe.Fori(0, EITER) as i:
                    for j in range(slots):
                        if j % HALF == 0:
                            pe.wait_ge(gathered[j // HALF], (i + 1) * HALF * 16)
                        pe.wait_ge(hot_ready, i * slots + j + 1)
                        pe.wait_ge(copied, i * slots + j + 1)
                        pe.matmul(acc[j % 2][:], onehot[:, j, :], rows[:, j, :], start=True, stop=True).then_inc(multiplied, 1)

            @block.scalar
            def _(act):
                act.sem_inc(copied, 2)
                with act.Fori(0, EITER) as i:
                    for h in range(2):
                        act.wait_ge(stored[h], (i + 1) * 16)
                        for j in range(h * HALF, (h + 1) * HALF):
                            act.wait_ge(multiplied, (i + 1) * slots + j + 1)
                            act.activation(sums[:, h, j - h * HALF, :], acc[j % 2][:], ACT.Copy).then_inc(copied, 1)

            @block.sync
            def _(sp):
                for h in range(2):
                    sp.dma_start(g["credit"][:, 8 * h:8 * h + 8], g["zero"][:]).then_inc(stored[h], 16)
                sp.wait_ge(none_ready, 1)
                sp.dma_start(g["pieces"][NO_EDGES:NO_EDGES + 1, :], none[:]).then_inc(none_stored, 16)
                with sp.Fori(0, EITER) as i:
                    for h in range(2):
                        sp.wait_ge(copied, i * slots + (h + 1) * HALF + 2)
                        sp.dma_start(out[:, bass.ds(i * slots + h * HALF, HALF), :], sums[:, h, :, :]).then_inc(stored[h], 16)
                sp.wait_ge(none_stored, 16)
                for h in range(2):
                    sp.wait_ge(stored[h], (EITER + 1) * 16)
    merge_pieces(nc, g)


def merge_pieces(nc, g):
    with Phase(nc) as ph:
        firsts = ph.sb("firsts", [EROWS, 2, CW])
        target = ph.sb("targets", [EROWS, 2, CW])
        sums = [ph.ps(f"sums{h}", [P, CW]) for h in range(2)]
        loaded, cleared, summed, added, got, put = (ph.sem(n) for n in ("loaded", "cleared", "summed", "added", "got", "put"))
        with nc.Block() as block:
            @block.sync
            def _(sp):
                sp.dma_start(firsts[:], g["pieces"][0:EPAD, :].rearrange("(q h r) c -> q h r c", h=2, r=P)[:, :, 0, :]).then_inc(loaded, 16)

            @block.gpsimd
            def _(pool):
                pool.wait_ge(cleared, 1)
                for h in range(2):
                    pool.indirect_dma_start(target[:, h, :], None, g["pieces"], bass.IndirectOffsetOnAxis(g["target"][:, h:h + 1], 0),
                                            bounds_check=EPAD - 1, oob_is_err=False).then_inc(got, 16)
                pool.wait_ge(added, 2)
                for h in range(2):
                    pool.indirect_dma_start(g["pieces"], bass.IndirectOffsetOnAxis(g["target"][:, h:h + 1], 0), target[:, h, :], None,
                                            bounds_check=EPAD - 1, oob_is_err=False).then_inc(put, 16)
                pool.wait_ge(put, 32)

            @block.tensor
            def _(pe):
                pe.wait_ge(loaded, 16)
                for o in range(2):
                    for h in range(2):
                        last = pe.matmul(sums[o][0:EROWS, :], g["same"][:, h, o, :], firsts[:, h, :], start=(h == 0), stop=(h == 1))
                    last.then_inc(summed, 1)

            @block.vector
            def _(dve):
                dve.memset(target[:], 0.0).then_inc(cleared, 1)
                dve.wait_ge(got, 32)
                for o in range(2):
                    dve.wait_ge(summed, o + 1)
                    dve.tensor_tensor(target[:, o, :], target[:, o, :], sums[o][0:EROWS, :], ALU.add).then_inc(added, 1)


def edge_scores(nc, g, heads):
    slots = 2 * HALF
    gat = heads > 1
    with Phase(nc) as ph:
        idx = ph.sb("idxs", [P, 2, slots], I32)
        got = ph.sb("got", [P, 2, slots, SCORES])
        both = ph.sb("both", [P, 2, ETILES, SCORES])
        score = ph.sb("score", [P, heads, ETILES])
        selfs = ph.sb("selfs", [P, heads, ETILES])
        most = ph.sb("most", [P, heads, ETILES])
        scoreR, fwd, bwd, zero = (ph.sb(n, [EROWS, heads, 2 * P]) for n in ("scoreR", "fwd", "bwd", "zeroR"))
        ends = ph.sb("ends", [EROWS, 2, HEADS])
        endrow = ph.sb("endsrow", [HEADS, 2, EROWS])
        carryrow = ph.sb("carryrow", [HEADS, 2, EROWS + 1])
        carry = ph.sb("carry", [EROWS, 2, HEADS])
        pr = [ph.ps(f"pr{k}", [P, 2, 2 * P]) for k in range(2)]
        pe_rows = ph.ps("perows", [P, 2, P])
        pcar = ph.ps("pcar", [P, 2, HEADS])
        pcols = [ph.ps(f"pcols{k}", [P, 2, 2 * P]) for k in range(2)]
        passed = ph.sem("passed")
        gathered = [ph.sem(f"gathered{h}") for h in range(2)]
        idx_ready, done, scored, turned, exped, act_done = (
            ph.sem(n) for n in ("idx_ready", "done", "scored", "turned", "exped", "act_done"))
        per = EITER * 4
        with nc.Block() as block:
            @block.gpsimd
            def _(pool):
                with pool.Fori(0, EITER) as i:
                    for h in range(2):
                        pool.wait_ge(idx_ready, 2 * i + h + 1)
                        carry_wait(pool, passed)
                        for j in range(h * HALF, (h + 1) * HALF):
                            for k in range(2):
                                pool.indirect_dma_start(got[:, k, j, :], None, g["scores"],
                                                        bass.IndirectOffsetOnAxis(idx[:, k, j:j + 1], 0), bounds_check=NPAD - 1,
                                                        oob_is_err=False).then_inc(gathered[h], 16)

            @block.vector
            def _(dve):
                link = chain(dve, done)
                for k, name in enumerate(("src", "dst")):
                    last = dve.tensor_copy(idx[:, k, :], g[name][:, 0:slots])
                last.then_inc(idx_ready, 2)
                dve.memset(zero[:], 0.0)
                dve.memset(carryrow[:], -BIG)
                with dve.Fori(0, EITER) as i:
                    for h in range(2):
                        s = slice(h * HALF, (h + 1) * HALF)
                        dve.wait_ge(gathered[h], (i + 1) * 2 * HALF * 16)
                        for k in range(2):
                            dve.tensor_copy(both[:, k, bass.ds(i * slots + h * HALF, HALF), :], got[:, k, s, :])
                        for k, name in enumerate(("src", "dst")):
                            last = dve.tensor_copy(idx[:, k, s], g[name][:, bass.ds((i + 1) * slots + h * HALF, HALF)])
                        last.then_inc(idx_ready, 1)
                dve.wait_ge(idx_ready, 2 * EITER + 2)
                for h in range(heads):
                    last = dve.tensor_tensor(score[:, h, :], both[:, 0, :, h], both[:, 1, :, HEADS + h], ALU.add)
                link(last)
                if gat:
                    for h in range(heads):
                        last = dve.tensor_tensor(selfs[:, h, :], both[:, 1, :, h], both[:, 1, :, HEADS + h], ALU.add)
                    link(last)
                    link(dve.scalar_tensor_tensor(selfs[:], selfs[:], 0.2, selfs[:], ALU.mult, ALU.max))
                else:
                    link(dve.tensor_tensor(score[:, 0, :], score[:, 0, :], g["ee"][:], ALU.add))
                dve.scalar_tensor_tensor(score[:], score[:], 0.2, score[:], ALU.mult, ALU.max).then_inc(scored, 1)
                dve.wait_ge(turned, 1)
                for h in range(heads):
                    last = dve.tensor_copy(scoreR[:, h, :], pr[h // 2][0:EROWS, h % 2, :])
                link(last)

                def scans(start):
                    for h in range(heads):
                        dve.tensor_tensor_scan(fwd[:, h, :], g["startR"][:], scoreR[:, h, :],
                                               -BIG if start is None else start[:, 0, h:h + 1], ALU.add, ALU.max)
                        last = dve.tensor_tensor_scan(bwd[:, h, ::-1], g["endR"][:, ::-1], scoreR[:, h, ::-1],
                                                      -BIG if start is None else start[:, 1, h:h + 1], ALU.add, ALU.max)
                    link(last)
                scans(None)
                dve.tensor_copy(ends[:, 0, 0:heads], fwd[:, :, 2 * P - 1])
                dve.tensor_copy(ends[:, 1, 0:heads], bwd[:, :, 0]).then_inc(scored, 1)
                dve.wait_ge(turned, 2)
                link(dve.tensor_copy(endrow[0:heads, :, :], pe_rows[0:heads, :, 0:EROWS]))
                dve.tensor_tensor_scan(carryrow[0:heads, 0, 1:EROWS + 1], g["startrow"][0:heads, :], endrow[0:heads, 0, :],
                                       -BIG, ALU.add, ALU.max)
                rev = slice(EROWS - 1, None, -1)
                dve.tensor_tensor_scan(carryrow[0:heads, 1, rev], g["endrow"][0:heads, ::-1], endrow[0:heads, 1, ::-1],
                                       -BIG, ALU.add, ALU.max).then_inc(scored, 1)
                dve.wait_ge(turned, 3)
                link(dve.tensor_copy(carry[:, :, 0:heads], pcar[0:EROWS, :, 0:heads]))
                scans(carry)
                dve.tensor_tensor(fwd[:], fwd[:], bwd[:], ALU.max).then_inc(scored, 1)
                dve.wait_ge(turned, 4)
                for h in range(heads):
                    last = dve.tensor_copy(most[:, h, :].rearrange("p (q a) -> p a q", a=2),
                                           pcols[h // 2][:, h % 2, :].rearrange("p (a q) -> p a q", a=2)[:, :, 0:EROWS])
                link(last)
                if gat:
                    link(dve.tensor_tensor(most[:], most[:], selfs[:], ALU.max))
                    dve.tensor_tensor(selfs[:], selfs[:], most[:], ALU.subtract)
                dve.tensor_tensor(score[:], score[:], most[:], ALU.subtract).then_inc(scored, 1)
                dve.wait_ge(exped, 1)
                if gat:
                    for h in range(heads):
                        last = dve.tensor_tensor(selfs[:, h, :], selfs[:, h, :], g["first"][:], ALU.mult)
                    link(last)
                    for h in range(heads):
                        dve.tensor_copy(g["exd"][:, :, HEADS + h], selfs[:, h, :])
                        dve.tensor_tensor(g["exd"][:, :, h], selfs[:, h, :], score[:, h, :], ALU.add)
                for h in range(heads):
                    last = dve.tensor_copy(g["exs"][:, :, h], score[:, h, :])
                link(last)

            @block.tensor
            def _(pe):
                ident = g["ident"]
                pe.wait_ge(scored, 1)
                for h in range(heads):
                    for a in range(2):
                        last = pe.transpose(pr[h // 2][0:EROWS, h % 2, a * P:(a + 1) * P],
                                            score[:, h, :].rearrange("p (q a) -> p a q", a=2)[:, a, :], ident[:])
                last.then_inc(turned, 1)
                pe.wait_ge(scored, 2)
                for k in range(2):
                    last = pe.transpose(pe_rows[0:heads, k, 0:EROWS], ends[:, k, 0:heads], ident[0:EROWS, 0:EROWS])
                last.then_inc(turned, 1)
                pe.wait_ge(scored, 3)
                for k in range(2):
                    last = pe.transpose(pcar[0:EROWS, k, 0:heads], carryrow[0:heads, k, k:k + EROWS], ident[0:heads, 0:heads])
                last.then_inc(turned, 1)
                pe.wait_ge(scored, 4)
                for h in range(heads):
                    for a in range(2):
                        last = pe.transpose(pcols[h // 2][:, h % 2, a * P:a * P + EROWS], fwd[:, h, a * P:(a + 1) * P],
                                            ident[0:EROWS, 0:EROWS])
                last.then_inc(turned, 1)

            @block.scalar
            def _(act):
                act.wait_ge(scored, 5)
                if gat:
                    act.activation(selfs[:], selfs[:], ACT.Exp)
                act.activation(score[:], score[:], ACT.Exp).then_inc(exped, 1)


def in_turn(stages):
    last = max(lag for lag, _ in stages)
    for step in range(SLOTS + last):
        for lag, f in stages:
            if 0 <= step - lag < SLOTS:
                f(step - lag)


class Nodes:

    def __init__(self, nc, ph, g, loads, stores, signals):
        self.nc, self.ph, self.g = nc, ph, g
        self.in_bufs = {k: ph.sb(k, [P, SLOTS, GT, D]) for k, _ in loads}
        self.loads, self.stores = loads, stores
        self.pieces = ph.sb("cb", [P, SLOTS, GT, CW])
        self.idx = ph.sb("idxs", [P, SLOTS * GT], I32)
        self.loaded = [ph.sem(f"loaded{s}") for s in range(SLOTS)]
        self.got = [ph.sem(f"got{s}") for s in range(SLOTS)]
        self.stored = [ph.sem(f"stored{s}") for s in range(SLOTS)]
        self.idx_ready = ph.sem("idx_ready")
        self.step = ph.sem("vector_step")
        self.passed, self.passed_v = ph.sem("passed"), ph.sem("passed_v")
        self.sig = {k: ph.sem(k) for k in signals}

    def start(self, eng, *signals):
        for k in signals:
            eng.sem_inc(self.sig[k], SLOTS)

    def done(self, ins, signal):
        ins.then_inc(self.sig[signal], 1)

    def need(self, eng, signal, i, s, back=0):
        eng.wait_ge(self.sig[signal], i * SLOTS + (s + 1 + SLOTS - back))

    def need_loads(self, eng, i, s):
        eng.wait_ge(self.loaded[s], (i + 1) * (16 * len(self.loads)))

    def need_pieces(self, eng, i, s):
        eng.wait_ge(self.got[s], (i + 1) * (16 * GT))

    def need_stores(self, eng, i, s):
        eng.wait_ge(self.stored[s], (i + 1) * (16 * len(self.stores)))

    def gather(self, pool):
        with pool.Fori(0, NITER) as i:
            for s in range(SLOTS):
                pool.wait_ge(self.idx_ready, i * SLOTS + s + 1)
                carry_wait(pool, self.passed)
                for j in range(GT):
                    pool.indirect_dma_start(self.pieces[:, s, j, :], None, self.g["pieces"],
                                            bass.IndirectOffsetOnAxis(self.idx[:, s * GT + j:s * GT + j + 1], 0),
                                            bounds_check=EPAD, oob_is_err=False).then_inc(self.got[s], 16)

    def first_indices(self, dve):
        dve.tensor_copy(self.idx[:], self.g["piece"][:, 0:SLOTS * GT]).then_inc(self.idx_ready, SLOTS)

    def next_indices(self, dve, i, s):
        dve.tensor_copy(self.idx[:, s * GT:(s + 1) * GT],
                        self.g["piece"][:, bass.ds((i + 1) * (SLOTS * GT) + s * GT, GT)]).then_inc(self.idx_ready, 1)

    def start_stores(self, sp):
        for s in range(SLOTS):
            for k in range(len(self.stores)):
                c = (s * len(self.stores) + k) * 8
                sp.dma_start(self.g["credit"][:, c:c + 8], self.g["zero"][:]).then_inc(self.stored[s], 16)

    def traffic(self, sp, free, ready):
        self.start_stores(sp)

        def load(i, s, wait=True):
            if wait:
                for k in free:
                    self.need(sp, k, i, s, back=SLOTS)
            for k, table in self.loads:
                self.move(sp, i, s, table, self.in_bufs[k][:, s, :, :], self.loaded[s], load=True)

        def store(i, s):
            self.need(sp, ready, i, s)
            for buf, table in self.stores:
                self.move(sp, i, s, table, buf[:, s, :, :], self.stored[s], load=False)

        def round(i):
            in_turn([(0, lambda s: load(i + 1, s)), (1, lambda s: store(i, s))])
        for s in range(SLOTS):
            load(0, s, wait=False)
        with sp.Fori(0, NITER - 2) as i:
            round(i)
        round(NITER - 2)
        for s in range(SLOTS):
            store(NITER - 1, s)
        for s in range(SLOTS):
            sp.wait_ge(self.stored[s], (NITER + 1) * (16 * len(self.stores)))

    @staticmethod
    def partial(table):
        return table.shape[0] != NPAD

    def move(self, sp, i, s, table, buf, sem, load):
        if isinstance(i, int) and self.partial(table) and (i * SLOTS + s + 1) * GROUP > N:
            lo = (i * SLOTS + s) * GROUP
            assert 0 < N - lo <= P
            dram, chip = table[lo:N, :], buf[0:N - lo, 0, :]
        else:
            dram = table[bass.ds(i * (SLOTS * GROUP) + s * GROUP, GROUP), :].rearrange("(j p) c -> p j c", p=P)
            chip = buf
        sp.dma_start(chip if load else dram, dram if load else chip).then_inc(sem, 16)


def vector_steps(eng, sem, i, per_round):
    n = [0]

    def link(ins):
        n[0] += 1
        ins.then_inc(sem, 1)
        eng.wait_ge(sem, i * per_round + n[0])

    def close():
        assert n[0] == per_round, n[0]
    return link, close


def turn(pe, bank, x, ident):
    for c in range(2):
        for j in range(GT):
            last = pe.transpose(bank[:, (c * GT + j) * P:(c * GT + j + 1) * P], x[:, j, c * P:(c + 1) * P], ident[:])
    return last


def times(pe, bank, xT, w, lo, hi, first=True, last=True):
    for j in range(GT):
        for c in range(2):
            ins = pe.matmul(bank[:, j, 0:hi - lo], xT[:, (c * GT + j) * P:(c * GT + j + 1) * P], w[:, c, lo:hi],
                            start=first and c == 0, stop=last and c == 1)
    return ins


def carry_wait(eng, sem):
    eng.sem_inc(sem, 1)


def stats(dve, link, y, st, mv, finish, sem):
    for j in range(GT):
        last = dve.bn_stats(st[:, j, :], y[:, j, :])
    link(last)
    carry_wait(dve, sem)
    for j in range(GT):
        last = dve.bn_aggr(mv[:, j, :], st[:, j, :])
    finish(last)


def normalise(dve, link, out, y, mv, std, rstd):
    link(dve.reciprocal(rstd, std))
    for j in range(GT):
        last = dve.tensor_scalar(out[:, j, :], y[:, j, :], mv[:, j, 0:1], rstd[:, j:j + 1], ALU.subtract, ALU.mult)
    return last


def sage_nodes(nc, g, x):
    with Phase(nc) as ph:
        x1 = ph.sb("x1", [P, SLOTS, GT, D])
        sc = ph.sb("sc", [P, SLOTS, GT, SCORES])
        n = Nodes(nc, ph, g, [("x", x)], [(x1, g["x1"]), (sc, g["scores"])],
                  ("mean", "turned", "copied", "product", "relu", "squares", "norm", "y", "std", "x1", "out"))
        xb, cb = n.in_bufs["x"], n.pieces
        small = ph.sb("small", [P, SLOTS, 4, GT])
        mean = ph.sb("mean", [P, SLOTS, GT, D])
        xT, mT = (ph.sb(k, [P, SLOTS, 2 * GT * P]) for k in ("xT", "mT"))
        relu, y = (ph.sb(k, [P, SLOTS, GT, D]) for k in ("relu", "y"))
        junk = ph.sb("junk", [P, SLOTS, GT, 2, D])
        sq, norm = (ph.sb(k, [P, SLOTS, GT]) for k in ("sq", "norm"))
        inv, std, rstd = (ph.sb(k, [P, SLOTS, GT]) for k in ("inv", "std", "rstd"))
        st = ph.sb("st", [P, SLOTS, GT, 6])
        mv = ph.sb("mv", [P, SLOTS, GT, 2])
        px = [ph.ps(f"px{k}", [P, 2 * GT * P]) for k in range(2)]
        pm = [ph.ps(f"pm{k}", [P, 2 * GT * P]) for k in range(2)]
        po = [ph.ps(f"po{k}", [P, GT, D]) for k in range(2)]
        with nc.Block() as block:
            @block.sync
            def _(sp):
                n.traffic(sp, ("turned", "y"), "out")

            @block.gpsimd
            def _(pool):
                n.gather(pool)

            @block.tensor
            def _(pe):
                n.start(pe, "turned", "product")
                with pe.Fori(0, NITER) as i:
                    def transposes(s):
                        n.need_loads(pe, i, s)
                        n.need(pe, "copied", i, s, back=2)
                        turn(pe, px[s % 2], xb[:, s], g["ident"])
                        n.need(pe, "mean", i, s)
                        n.done(turn(pe, pm[s % 2], mean[:, s], g["ident"]), "turned")

                    def products(s):
                        n.need(pe, "copied", i, s)
                        n.need(pe, "relu", i, s, back=2)
                        for j in range(GT):
                            pe.matmul(po[s % 2][:, j, :], g["ones3"][:], g["b0"][:], start=True, stop=False)
                            for k in range(4):
                                t = (xT, mT)[k // 2]
                                lo = ((k % 2) * GT + j) * P
                                last = pe.matmul(po[s % 2][:, j, :], t[:, s, lo:lo + P], g["w0"][:, k, :], start=False, stop=(k == 3))
                        n.done(last, "product")
                    in_turn([(0, transposes), (1, products)])

            @block.scalar
            def _(act):
                n.start(act, "copied", "relu", "squares", "norm", "std")
                with act.Fori(0, NITER) as i:
                    def copies(s):
                        n.need(act, "turned", i, s)
                        n.need(act, "product", i, s, back=SLOTS)
                        act.activation(xT[:, s, :], px[s % 2][:], ACT.Copy)
                        n.done(act.activation(mT[:, s, :], pm[s % 2][:], ACT.Copy), "copied")

                    def relus(s):
                        n.need(act, "product", i, s)
                        n.need(act, "x1", i, s, back=SLOTS)
                        n.done(act.activation(relu[:, s], po[s % 2][:], ACT.Relu), "relu")
                        n.need(act, "relu", i, s)
                        for j in range(GT):
                            last = act.activation(y[:, s, j, :], relu[:, s, j, :], ACT.Square, accum_out=sq[:, s, j:j + 1])
                        n.done(last, "squares")
                        n.need(act, "squares", i, s)
                        n.done(act.activation(norm[:, s, :], sq[:, s, :], ACT.Sqrt), "norm")

                    def stds(s):
                        n.need(act, "y", i, s)
                        n.need(act, "out", i, s, back=SLOTS)
                        n.done(act.activation(std[:, s, :], mv[:, s, :, 1], ACT.Sqrt, bias=g["eps"][:]), "std")
                    in_turn([(0, copies), (1, relus), (2, stds)])

            @block.vector
            def _(dve):
                n.start(dve, "mean", "y", "x1", "out")
                n.first_indices(dve)
                dve.memset(sc[:], 0.0)
                with dve.Fori(0, NITER) as i:
                    link, close = vector_steps(dve, n.step, i, SLOTS * 7)

                    def means(s):
                        n.need_pieces(dve, i, s)
                        n.need(dve, "turned", i, s, back=SLOTS)
                        link(dve.tensor_scalar(small[:, s, 0, :], cb[:, s, :, D], 1.0, None, ALU.max))
                        dve.tensor_scalar(g["dis"][:, bass.ds(i * (SLOTS * GT) + s * GT, GT)], cb[:, s, :, D + 1], 1.0, None, ALU.add)
                        link(dve.reciprocal(small[:, s, 1, :], small[:, s, 0, :]))
                        for j in range(GT):
                            last = dve.tensor_scalar(mean[:, s, j, :], cb[:, s, j, 0:D], small[:, s, 1, j:j + 1], None, ALU.mult)
                        n.done(last, "mean")
                        n.next_indices(dve, i, s)

                    def ys(s):
                        n.need(dve, "norm", i, s)
                        n.need_loads(dve, i, s)
                        link(dve.tensor_scalar(small[:, s, 2, :], norm[:, s, :], 1e-12, None, ALU.max))
                        link(dve.reciprocal(inv[:, s, :], small[:, s, 2, :]))
                        for j in range(GT):
                            last = dve.scalar_tensor_tensor(y[:, s, j, :], relu[:, s, j, :], inv[:, s, j:j + 1], xb[:, s, j, :], ALU.mult, ALU.add)
                        link(last)
                        stats(dve, link, y[:, s], st[:, s], mv[:, s], lambda ins: n.done(ins, "y"), n.passed_v)

                    def outs(s):
                        n.need(dve, "std", i, s)
                        n.need_stores(dve, i, s)
                        n.done(normalise(dve, link, x1[:, s], y[:, s], mv[:, s], std[:, s, :], rstd[:, s]), "x1")
                        n.need(dve, "x1", i, s)
                        for j in range(GT):
                            for k, v in enumerate(("vsrc", "vdst")):
                                last = dve.tensor_tensor_reduce(junk[:, s, j, k, :], x1[:, s, j, :], g[v][:], 1.0, 0.0, ALU.mult, ALU.add,
                                                                  sc[:, s, j, k * HEADS:k * HEADS + 1])
                        n.done(last, "out")
                    in_turn([(0, means), (2, ys), (3, outs)])
                    close()
    with Phase(nc) as ph:
        root, made = ph.sem("root"), ph.sem("made")
        with nc.Block() as block:
            @block.scalar
            def _(act):
                act.activation(g["dis"][:], g["dis"][:], ACT.Sqrt).then_inc(root, 1)

            @block.vector
            def _(dve):
                dve.wait_ge(root, 1)
                dve.reciprocal(g["dis"][:], g["dis"][:]).then_inc(made, 1)
                dve.wait_ge(made, 1)




def attention_nodes(nc, g):
    with Phase(nc) as ph:
        x2, h = ph.sb("x2", [P, SLOTS, GT, D]), ph.sb("h", [P, SLOTS, GT, D])
        n = Nodes(nc, ph, g, [("x", g["x1"])], [(x2, g["x2"]), (h, g["h6"])],
                  ("agg", "turned", "copied", "product", "y", "std", "x2", "y2", "std2", "z", "out"))
        xb, cb = n.in_bufs["x"], n.pieces
        small = ph.sb("small", [P, SLOTS, 2, GT])
        agg, y, z = (ph.sb(k, [P, SLOTS, GT, D]) for k in ("agg", "y", "z"))
        aT = ph.sb("aT", [P, SLOTS, 2 * GT * P])
        std, rstd = (ph.sb(k, [P, SLOTS, 2, GT]) for k in ("std", "rstd"))
        st = ph.sb("st", [P, SLOTS, GT, 6])
        mv = ph.sb("mv", [P, SLOTS, 2, GT, 2])
        pa = [ph.ps(f"pa{k}", [P, 2 * GT * P]) for k in range(2)]
        po = [ph.ps(f"po{k}", [P, GT, D]) for k in range(2)]
        with nc.Block() as block:
            @block.sync
            def _(sp):
                n.traffic(sp, ("y",), "out")

            @block.gpsimd
            def _(pool):
                n.gather(pool)

            @block.tensor
            def _(pe):
                n.start(pe, "turned", "product")
                with pe.Fori(0, NITER) as i:
                    def transposes(s):
                        n.need(pe, "copied", i, s, back=2)
                        n.need(pe, "agg", i, s)
                        n.done(turn(pe, pa[s % 2], agg[:, s], g["ident"]), "turned")

                    def products(s):
                        n.need(pe, "copied", i, s)
                        n.need(pe, "y", i, s, back=2)
                        n.done(times(pe, po[s % 2], aT[:, s], g["w1T"], 0, D), "product")
                    in_turn([(0, transposes), (1, products)])

            @block.scalar
            def _(act):
                n.start(act, "copied", "std", "std2", "out")
                with act.Fori(0, NITER) as i:
                    def copies(s):
                        n.need(act, "turned", i, s)
                        n.need(act, "product", i, s, back=SLOTS)
                        n.done(act.activation(aT[:, s, :], pa[s % 2][:], ACT.Copy), "copied")

                    def stds(k, signal, before):
                        def f(s):
                            n.need(act, before, i, s)
                            n.need(act, "z", i, s, back=SLOTS)
                            n.done(act.activation(std[:, s, k, :], mv[:, s, k, :, 1], ACT.Sqrt, bias=g["eps"][:]), signal)
                        return f

                    def scales(s):
                        n.need(act, "z", i, s)
                        n.need_stores(act, i, s)
                        for j in range(GT):
                            last = act.activation(h[:, s, j, :], z[:, s, j, :], ACT.Copy,
                                                  scale=g["dis"][:, bass.ds(i * (SLOTS * GT) + (s * GT + j), 1)])
                        n.done(last, "out")
                    in_turn([(0, copies), (1, stds(0, "std", "y")), (2, stds(1, "std2", "y2")), (3, scales)])

            @block.vector
            def _(dve):
                n.start(dve, "agg", "y", "x2", "y2", "z")
                n.first_indices(dve)
                with dve.Fori(0, NITER) as i:
                    link, close = vector_steps(dve, n.step, i, SLOTS * 10)

                    def aggs(s):
                        n.need_pieces(dve, i, s)
                        n.need(dve, "turned", i, s, back=SLOTS)
                        link(dve.tensor_scalar(small[:, s, 0, :], cb[:, s, :, D], 0.5, None, ALU.max))
                        link(dve.reciprocal(small[:, s, 1, :], small[:, s, 0, :]))
                        for j in range(GT):
                            last = dve.tensor_scalar(agg[:, s, j, :], cb[:, s, j, 0:D], small[:, s, 1, j:j + 1], None, ALU.mult)
                        n.done(last, "agg")
                        n.next_indices(dve, i, s)

                    def ys(s):
                        n.need(dve, "product", i, s)
                        n.need_loads(dve, i, s)
                        link(dve.tensor_tensor(y[:, s], po[s % 2][:], xb[:, s], ALU.add))
                        stats(dve, link, y[:, s], st[:, s], mv[:, s, 0], lambda ins: n.done(ins, "y"), n.passed_v)

                    def x2s(s):
                        n.need(dve, "std", i, s)
                        n.need_stores(dve, i, s)
                        link(normalise(dve, link, x2[:, s], y[:, s], mv[:, s, 0], std[:, s, 0, :], rstd[:, s, 0]))
                        stats(dve, link, x2[:, s], st[:, s], mv[:, s, 1], lambda ins: n.done(ins, "y2"), n.passed_v)

                    def zs(s):
                        n.need(dve, "std2", i, s)
                        affine(dve, link, n, i, s, z[:, s], x2[:, s], mv[:, s, 1], std[:, s, 1, :], rstd[:, s, 1], g["ln6g"], g["ln6b"])
                    in_turn([(0, aggs), (1, ys), (2, x2s), (3, zs)])
                    close()


def affine(dve, link, n, i, s, z, x, mv, std, rstd, gain, shift):
    n.need(dve, "out", i, s, back=SLOTS)
    link(normalise(dve, link, z, x, mv, std, rstd))
    link(dve.tensor_tensor(z, z, gain[:], ALU.mult))
    n.done(dve.tensor_tensor(z, z, shift[:], ALU.add), "z")


def gcn_nodes(nc, g, last):
    with Phase(nc) as ph:
        w, bias = (g["w7T"], g["b7"]) if last else (g["w6T"], g["b6"])
        o1, o2 = ph.sb("o1", [P, SLOTS, GT, D]), ph.sb("o2", [P, SLOTS, GT, D])
        sc = ph.sb("sc", [P, SLOTS, GT, SCORES])
        if last:
            loads = [("h", g["h7"]), ("x", g["y6"]), ("x2", g["x2"])]
            stores = [(o1, g["x3"]), (o2, g["p1"]), (sc, g["scores"])]
        else:
            loads = [("h", g["h6"]), ("x", g["x2"])]
            stores = [(o1, g["y6"]), (o2, g["h7"])]
        n = Nodes(nc, ph, g, loads, stores,
                  ("agg", "turned", "copied", "product", "y", "turned2", "copied2", "product2", "v", "std", "z", "x3",
                   "turned3", "copied3", "product3", "out"))
        hb, xb, cb = n.in_bufs["h"], n.in_bufs["x"], n.pieces
        agg, t = (ph.sb(k, [P, SLOTS, GT, D]) for k in ("agg", "t"))
        y = ph.sb("y", [P, SLOTS, GT, D]) if last else o1
        z = ph.sb("z", [P, SLOTS, GT, D])
        aT = ph.sb("aT", [P, SLOTS, 2 * GT * P])
        yT = ph.sb("yT", [P, SLOTS, 2 * GT * P]) if last else None
        std, rstd = (ph.sb(k, [P, SLOTS, GT]) for k in ("std", "rstd"))
        st = ph.sb("st", [P, SLOTS, GT, 6])
        mv = ph.sb("mv", [P, SLOTS, GT, 2])
        pa, po = ph.ps("pa", [P, 2 * GT * P]), ph.ps("po", [P, GT, D])
        if last:
            py, po2, px, po3 = ph.ps("py", [P, 2 * GT * P]), ph.ps("po2", [P, GT, D]), ph.ps("px", [P, 2 * GT * P]), ph.ps("po3", [P, GT, D])
            psc = ph.ps("psc", [P, GT, SCORES])
        with nc.Block() as block:
            @block.sync
            def _(sp):
                n.traffic(sp, ("v",) if last else ("y",), "out")

            @block.gpsimd
            def _(pool):
                n.gather(pool)

            @block.tensor
            def _(pe):
                n.start(pe, "turned", "product", "turned2", "product2", "turned3", "product3")
                with pe.Fori(0, NITER) as i:
                    def transposes(s):
                        n.need(pe, "copied", i, s, back=1)
                        n.need(pe, "agg", i, s)
                        n.done(turn(pe, pa, agg[:, s], g["ident"]), "turned")

                    def products(s):
                        n.need(pe, "copied", i, s)
                        n.need(pe, "y", i, s, back=1)
                        n.done(times(pe, po, aT[:, s], w, 0, D), "product")

                    def transposes2(s):
                        n.need(pe, "copied2", i, s, back=1)
                        n.need(pe, "y", i, s)
                        n.done(turn(pe, py, y[:, s], g["ident"]), "turned2")

                    def products2(s):
                        n.need(pe, "copied2", i, s)
                        n.need(pe, "v", i, s, back=1)
                        for j in range(GT):
                            pe.matmul(po2[:, j, :], g["ones3"][:], g["bp"][:], start=True, stop=False)
                            for c in range(2):
                                ins = pe.matmul(po2[:, j, :], yT[:, s, (c * GT + j) * P:(c * GT + j + 1) * P], g["wpT"][:, c, :],
                                                start=False, stop=(c == 1))
                        n.done(ins, "product2")

                    def transposes3(s):
                        n.need(pe, "copied3", i, s, back=1)
                        n.need(pe, "x3", i, s)
                        n.done(turn(pe, px, o1[:, s], g["ident"]), "turned3")

                    def products3(s):
                        n.need(pe, "copied3", i, s)
                        n.need(pe, "out", i, s, back=1)
                        times(pe, po3, aT[:, s], g["g1w"], 0, D)
                        n.done(times(pe, psc, aT[:, s], g["g1w"], D, CW), "product3")
                    in_turn([(0, transposes), (1, products)] +
                            ([(2, transposes2), (3, products2), (4, transposes3), (5, products3)] if last else []))

            @block.scalar
            def _(act):
                n.start(act, "copied", "copied2", "copied3", "std", "out")
                with act.Fori(0, NITER) as i:
                    def copies(s):
                        n.need(act, "turned", i, s)
                        n.need(act, "product", i, s, back=SLOTS)
                        if last:
                            n.need(act, "product3", i, s, back=SLOTS)
                        n.done(act.activation(aT[:, s, :], pa[:], ACT.Copy), "copied")

                    def copies2(s):
                        n.need(act, "turned2", i, s)
                        n.need(act, "product2", i, s, back=SLOTS)
                        n.done(act.activation(yT[:, s, :], py[:], ACT.Copy), "copied2")

                    def copies3(s):
                        n.need(act, "turned3", i, s)
                        n.done(act.activation(aT[:, s, :], px[:], ACT.Copy), "copied3")

                    def stds(s):
                        n.need(act, "v" if last else "y", i, s)
                        n.need(act, "x3" if last else "z", i, s, back=SLOTS)
                        n.done(act.activation(std[:, s, :], mv[:, s, :, 1], ACT.Sqrt, bias=g["eps"][:]), "std")

                    def scales(s):
                        n.need(act, "z", i, s)
                        n.need_stores(act, i, s)
                        for j in range(GT):
                            ins = act.activation(o2[:, s, j, :], z[:, s, j, :], ACT.Copy,
                                                 scale=g["dis"][:, bass.ds(i * (SLOTS * GT) + (s * GT + j), 1)])
                        n.done(ins, "out")

                    def rows(s):
                        n.need(act, "product3", i, s)
                        n.need_stores(act, i, s)
                        act.activation(o2[:, s], po3[:], ACT.Copy)
                        n.done(act.activation(sc[:, s], psc[:], ACT.Copy), "out")
                    if last:
                        in_turn([(0, copies), (2, copies2), (3, stds), (4, copies3), (5, rows)])
                    else:
                        in_turn([(0, copies), (1, stds), (2, scales)])

            @block.vector
            def _(dve):
                n.start(dve, "agg", "y", "v", "z", "x3")
                n.first_indices(dve)
                with dve.Fori(0, NITER) as i:
                    link, close = vector_steps(dve, n.step, i, SLOTS * (4 if last else 6))

                    def aggs(s):
                        n.need_pieces(dve, i, s)
                        n.need_loads(dve, i, s)
                        n.need(dve, "turned", i, s, back=SLOTS)
                        n.done(dve.tensor_tensor(agg[:, s], cb[:, s, :, 0:D], hb[:, s], ALU.add), "agg")
                        n.next_indices(dve, i, s)

                    def ys(s):
                        n.need(dve, "product", i, s)
                        if last:
                            n.need(dve, "turned2", i, s, back=SLOTS)
                        else:
                            n.need_stores(dve, i, s)
                        for j in range(GT):
                            ins = dve.scalar_tensor_tensor(t[:, s, j, :], po[:, j, :], g["dis"][:, bass.ds(i * (SLOTS * GT) + (s * GT + j), 1)],
                                                           bias[:], ALU.mult, ALU.add)
                        link(ins)
                        ins = dve.scalar_tensor_tensor(y[:, s], t[:, s], 0.0, xb[:, s], ALU.max, ALU.add)
                        if last:
                            n.done(ins, "y")
                        else:
                            link(ins)
                            stats(dve, link, y[:, s], st[:, s], mv[:, s], lambda k: n.done(k, "y"), n.passed_v)

                    def zs(s):
                        n.need(dve, "std", i, s)
                        affine(dve, link, n, i, s, z[:, s], y[:, s], mv[:, s], std[:, s, :], rstd[:, s], g["ln7g"], g["ln7b"])

                    def vs(s):
                        n.need(dve, "product2", i, s)
                        link(dve.tensor_tensor(z[:, s], po2[:], n.in_bufs["x2"][:, s], ALU.add))
                        stats(dve, link, z[:, s], st[:, s], mv[:, s], lambda k: n.done(k, "v"), n.passed_v)

                    def x3s(s):
                        n.need(dve, "std", i, s)
                        n.need_stores(dve, i, s)
                        n.need(dve, "turned3", i, s, back=SLOTS)
                        n.done(normalise(dve, link, o1[:, s], z[:, s], mv[:, s], std[:, s, :], rstd[:, s]), "x3")
                    if last:
                        in_turn([(0, aggs), (1, ys), (3, vs), (4, x3s)])
                    else:
                        in_turn([(0, aggs), (1, ys), (2, zs)])
                    close()


def gat_nodes(nc, g, last, out):
    with Phase(nc) as ph:
        bias = g["gb2"] if last else g["gb1"]
        o = ph.sb("o", [P, SLOTS, GT, D])
        sc = ph.sb("sc", [P, SLOTS, GT, SCORES])
        if last:
            loads, stores = [("p", g["p2"]), ("x3", g["x3"])], [(o, out)]
        else:
            loads, stores = [("p", g["p1"])], [(o, g["p2"]), (sc, g["scores"])]
        n = Nodes(nc, ph, g, loads, stores,
                  ("low", "ex", "v", "turned", "copied", "product", "y", "std", "out"))
        pb, cb = n.in_bufs["p"], n.pieces
        rden = ph.sb("rden", [P, SLOTS, GT, HEADS])
        u, low, v = (ph.sb(k, [P, SLOTS, GT, D]) for k in ("u", "low", "v"))
        vT = ph.sb("vT", [P, SLOTS, 2 * GT * P])
        minus = ph.sb("minus", [P, 1])
        std, rstd = (ph.sb(k, [P, SLOTS, GT]) for k in ("std", "rstd"))
        st = ph.sb("st", [P, SLOTS, GT, 6])
        mv = ph.sb("mv", [P, SLOTS, GT, 2])
        pv = [ph.ps(f"pv{k}", [P, 2 * GT * P]) for k in range(2)]
        po = [ph.ps(f"po{k}", [P, GT, D]) for k in range(2)]
        psc = [ph.ps(f"psc{k}", [P, GT, SCORES]) for k in range(2)]
        minus_ready = ph.sem("minus_ready")

        def heads(x):
            return x.rearrange("p j (h c) -> p j h c", h=HEADS)

        def per_head(x):
            return x.unsqueeze(3).to_broadcast([P, GT, HEADS, HID])
        with nc.Block() as block:
            @block.sync
            def _(sp):
                n.traffic(sp, ("y",) if last else ("low",), "out")

            @block.gpsimd
            def _(pool):
                n.gather(pool)

            @block.tensor
            def _(pe):
                n.start(pe, "turned", "product")
                if not last:
                    with pe.Fori(0, NITER) as i:
                        def transposes(s):
                            n.need(pe, "copied", i, s, back=2)
                            n.need(pe, "v", i, s)
                            n.done(turn(pe, pv[s % 2], v[:, s], g["ident"]), "turned")

                        def products(s):
                            n.need(pe, "copied", i, s)
                            n.need(pe, "out", i, s, back=2)
                            times(pe, po[s % 2], vT[:, s], g["g2w"], 0, D)
                            n.done(times(pe, psc[s % 2], vT[:, s], g["g2w"], D, CW), "product")
                        in_turn([(0, transposes), (1, products)])

            @block.scalar
            def _(act):
                n.start(act, "ex", "copied", "std")
                if not last:
                    n.start(act, "out")
                    act.wait_ge(minus_ready, 1)
                with act.Fori(0, NITER) as i:
                    def exps(s):
                        n.need(act, "low", i, s)
                        n.done(act.activation(low[:, s], low[:, s], ACT.Exp), "ex")

                    def copies(s):
                        n.need(act, "turned", i, s)
                        n.need(act, "product", i, s, back=SLOTS)
                        n.done(act.activation(vT[:, s, :], pv[s % 2][:], ACT.Identity, bias=minus[:]), "copied")

                    def rows(s):
                        n.need(act, "product", i, s)
                        n.need_stores(act, i, s)
                        act.activation(o[:, s], po[s % 2][:], ACT.Copy)
                        n.done(act.activation(sc[:, s], psc[s % 2][:], ACT.Copy), "out")

                    def stds(s):
                        n.need(act, "y", i, s)
                        n.need(act, "out", i, s, back=SLOTS)
                        n.done(act.activation(std[:, s, :], mv[:, s, :, 1], ACT.Sqrt, bias=g["eps"][:]), "std")
                    if last:
                        in_turn([(0, exps), (SLOTS, stds)])
                    else:
                        in_turn([(0, exps), (1, copies), (2, rows)])

            @block.vector
            def _(dve):
                n.start(dve, "low", "v", "y")
                if last:
                    n.start(dve, "out")
                dve.memset(minus[:], -1.0).then_inc(minus_ready, 1)
                n.first_indices(dve)
                with dve.Fori(0, NITER) as i:
                    link, close = vector_steps(dve, n.step, i, SLOTS * (7 if last else 4))

                    def lows(s):
                        n.need_pieces(dve, i, s)
                        n.need_loads(dve, i, s)
                        dve.reciprocal(rden[:, s], cb[:, s, :, D:D + HEADS])
                        link(dve.tensor_tensor(heads(u[:, s]), heads(pb[:, s]), per_head(cb[:, s, :, D + HEADS:CW]), ALU.mult))
                        link(dve.tensor_tensor(u[:, s], u[:, s], cb[:, s, :, 0:D], ALU.add))
                        n.next_indices(dve, i, s)
                        link(dve.tensor_tensor(heads(u[:, s]), heads(u[:, s]), per_head(rden[:, s]), ALU.mult))
                        link(dve.tensor_tensor(u[:, s], u[:, s], bias[:], ALU.add))
                        n.done(dve.tensor_scalar(low[:, s], u[:, s], 0.0, None, ALU.min), "low")

                    def vs(s):
                        n.need(dve, "ex", i, s)
                        if not last:
                            n.need(dve, "turned", i, s, back=SLOTS)
                        ins = dve.scalar_tensor_tensor(v[:, s], u[:, s], 0.0, low[:, s], ALU.max, ALU.add)
                        if not last:
                            n.done(ins, "v")
                            return
                        link(ins)
                        link(dve.scalar_tensor_tensor(u[:, s], v[:, s], -1.0, n.in_bufs["x3"][:, s], ALU.add, ALU.add))
                        stats(dve, lambda k: (n.done(k, "v"), n.need(dve, "v", i, s)), u[:, s], st[:, s], mv[:, s], lambda k: n.done(k, "y"), n.passed_v)

                    def outs(s):
                        n.need(dve, "std", i, s)
                        n.need_stores(dve, i, s)
                        n.done(normalise(dve, link, o[:, s], u[:, s], mv[:, s], std[:, s, :], rstd[:, s]), "out")
                    in_turn([(0, lows), (1, vs)] + ([(SLOTS, outs)] if last else []))
                    close()


_INS = ["x", "src", "dst", "edge_attr_64", "edge_weight", "L0_gnn_W", "L0_gnn_b", "L1_gnn_W", "L1_gnn_A", "L2_gnn_ln6_g",
        "L2_gnn_ln6_b", "L2_gnn_W6", "L2_gnn_b6", "L2_gnn_ln7_g", "L2_gnn_ln7_b", "L2_gnn_W7", "L2_gnn_b7", "L2_gnn_Wp",
        "L2_gnn_bp", "L3_gnn_W1", "L3_gnn_att_src1", "L3_gnn_att_dst1", "L3_gnn_b1", "L3_gnn_W2", "L3_gnn_att_src2",
        "L3_gnn_att_dst2", "L3_gnn_b2"]
_OUTS = [((50000, 256), "float32")]


def kernel(**inputs):
    import numpy as _np
    import concourse.bacc as _bacc
    from concourse import mybir as _mybir
    from concourse.bass_utils import run_bass_kernel_spmd as _run

    nc = _bacc.Bacc("TRN2", target_bir_lowering=False, num_devices=1)
    arrays, args = {}, {}
    for name in _INS:
        a = _np.ascontiguousarray(inputs[name])
        arrays[f"in_{name}_dram"] = a
        args[name] = nc.dram_tensor(f"in_{name}_dram", a.shape, _mybir.dt.from_np(a.dtype), kind="ExternalInput").ap()
    shape, dtype = _OUTS[0]
    out = nc.dram_tensor("out_0_dram", shape, _mybir.dt.from_np(_np.dtype(dtype)), kind="ExternalOutput").ap()
    build(nc, args, out)
    r = _run(nc, [arrays], core_ids=[0])
    return r.results[0]["out_0_dram"]
```

```python
from contextlib import ExitStack

import concourse.bass as bass
from concourse import mybir

F32 = mybir.dt.float32
BF16 = mybir.dt.bfloat16
I32 = mybir.dt.int32
ALU = mybir.AluOpType
ACT = mybir.ActivationFunctionType
AX = mybir.AxisListType

P = 128
D = 256
N = 50000
E = 25000
EDIM = 64
HEADS = 4
HID = D // HEADS

CREDIT = 16
SLOTS = 4
GT = 2
GROUP = GT * P
NGROUPS = -(-N // (GROUP * SLOTS)) * SLOTS
NPAD = NGROUPS * GROUP
NTILES = NPAD // P
NITER = NGROUPS // SLOTS

ETILES = -(-E // (2 * P)) * 2
EPAD = ETILES * P
EROWS = ETILES // 2
HALF = 7
EITER = ETILES // (2 * HALF)
assert EITER * 2 * HALF == ETILES and EROWS <= P and NTILES == 4 * EROWS

SCORES = 2 * HEADS
CW = D + SCORES
NO_EDGES = EPAD
BIG = 1e30
FAR = 1000000
PAD_NODE = 60000
LN_EPS = 1e-5


def build(nc, a, out):
    ctx = ExitStack()
    with ctx:
        def sb(name, shape, dt=F32):
            return ctx.enter_context(nc.sbuf_tensor(name, shape, dt))

        def dram(name, shape, dt=F32):
            return nc.dram_tensor(name, shape, dt).ap()

        g = {}
        for name in ("x1", "x2", "h6", "y6", "h7", "x3", "p1", "p2"):
            g[name] = dram("t_" + name, [NPAD, D])
        g["scores"] = dram("t_scores", [NPAD, SCORES])
        g["pieces"] = dram("t_pieces", [EPAD + 1, CW])
        g["piece_of"] = dram("t_piece_of", [NPAD, 1], I32)
        g["credit"] = dram("t_credit", [P, 16 * 8])

        for name, shape in (("ident", [P, P]), ("iota", [P, P]), ("eps", [P, 1]), ("zero", [P, 8]),
                            ("w0", [P, 4, D]), ("w1T", [P, 2, D]), ("w6T", [P, 2, D]), ("w7T", [P, 2, D]),
                            ("wpT", [P, 2, D]), ("g1w", [P, 2, CW]), ("g2w", [P, 2, CW]),
                            ("vsrc", [P, D]), ("vdst", [P, D]),
                            ("ln6g", [P, GT, D]), ("ln6b", [P, GT, D]), ("ln7g", [P, GT, D]), ("ln7b", [P, GT, D]),
                            ("b6", [P, D]), ("b7", [P, D]), ("gb1", [P, GT, D]), ("gb2", [P, GT, D]),
                            ("rank", [P, ETILES]), ("first", [P, ETILES]), ("ew", [P, ETILES]), ("ee", [P, ETILES]),
                            ("startR", [EROWS, 2 * P]), ("endR", [EROWS, 2 * P]),
                            ("startrow", [HEADS, EROWS]), ("endrow", [HEADS, EROWS]),
                            ("same", [EROWS, 2, 2, EROWS]),
                            ("dis", [P, NTILES])):
            g[name] = sb(name, shape)
        g["ones3"] = sb("ones3", [3, P], BF16)
        g["b0"] = sb("b0", [3, D], BF16)
        g["bp"] = sb("bp", [3, D], BF16)
        g["src"] = sb("srcs", [P, ETILES + 2 * HALF], I32)
        g["dst"] = sb("dsts", [P, ETILES + 2 * HALF], I32)
        g["piece"] = sb("piece", [P, NTILES + GT * SLOTS], I32)
        g["target"] = sb("target", [EROWS, 2], I32)
        g["exs"] = sb("exs", [P, ETILES, HEADS])
        g["exd"] = sb("exd", [P, ETILES, SCORES])

        weights(nc, a, g)
        edge_tables(nc, a, g)
        edge_pass(nc, g, "count", a["x"], 0)
        sage_nodes(nc, g, a["x"])
        edge_scores(nc, g, 1)
        edge_pass(nc, g, "attention", g["x1"], 1)
        attention_nodes(nc, g)
        edge_pass(nc, g, "gcn", g["h6"], 0)
        gcn_nodes(nc, g, last=False)
        edge_pass(nc, g, "gcn", g["h7"], 0)
        gcn_nodes(nc, g, last=True)
        edge_scores(nc, g, HEADS)
        edge_pass(nc, g, "gat", g["p1"], SCORES)
        gat_nodes(nc, g, last=False, out=None)
        edge_scores(nc, g, HEADS)
        edge_pass(nc, g, "gat", g["p2"], SCORES)
        gat_nodes(nc, g, last=True, out=out)


PHASE = [0]


class Phase:

    def __init__(self, nc):
        self.nc = nc
        self.ctx = ExitStack()
        self.sems = []
        PHASE[0] += 1
        self.tag = f"_{PHASE[0]}"

    def __enter__(self):
        self.ctx.__enter__()
        return self

    def __exit__(self, *e):
        self.nc.clear_and_free_semaphores(self.sems)
        self.nc.all_engine_barrier()
        return self.ctx.__exit__(*e)

    def sb(self, name, shape, dt=F32):
        return self.ctx.enter_context(self.nc.sbuf_tensor(name + self.tag, shape, dt))

    def ps(self, name, shape, dt=F32):
        return self.ctx.enter_context(self.nc.psum_tensor(name + self.tag, shape, dt))

    def sem(self, name):
        s = self.nc.alloc_semaphore(name + self.tag)
        self.sems.append(s)
        return s


def chain(eng, sem):
    n = [0]

    def link(ins):
        n[0] += 1
        ins.then_inc(sem, 1)
        eng.wait_ge(sem, n[0])
    return link


def spread(ap, shape):
    return ap.to_broadcast(shape)


def weights(nc, a, g):
    with Phase(nc) as ph:
        raw = {k: ph.sb("raw_" + k, [P, 2, D]) for k in ("w1", "w6", "w7", "wp")}
        acol = ph.sb("acol", [P, 2, 2])
        arow = ph.sb("arow", [P, 2, 2, P])
        att = ph.sb("att", [P, 4, D])
        prod = ph.sb("prod", [P, 2, 4, D])
        bias = ph.sb("bias", [1, 2, D])
        parts = ph.sb("parts", [1, 2, 3, D], BF16)
        rest = ph.sb("rest", [1, 2, 2, D])
        pt = [ph.ps(f"pt{k}", [P, 2 * D]) for k in range(4)]
        pv = ph.ps("pv", [P, 2, D])
        loaded, zeroed, done, transposed, vecs = (ph.sem(n) for n in ("loaded", "zeroed", "done", "transposed", "vecs"))
        moved, split = ph.sem("moved"), ph.sem("split")
        names = (("w1", "L1_gnn_W", "w1T"), ("w6", "L2_gnn_W6", "w6T"), ("w7", "L2_gnn_W7", "w7T"), ("wp", "L2_gnn_Wp", "wpT"))
        loads = [0]
        with nc.Block() as block:
            @block.sync
            def _(sp):
                def load(o, i):
                    sp.dma_start(o, i).then_inc(loaded, 16)
                    loads[0] += 1
                for k, name, _ in names:
                    load(raw[k][:], a[name].rearrange("(c p) k -> p c k", p=P))
                load(g["w0"][:], a["L0_gnn_W"].rearrange("(c p) k -> p c k", p=P))
                load(g["g1w"][:, :, 0:D], a["L3_gnn_W1"].rearrange("(c p) k -> p c k", p=P))
                load(g["g2w"][:, :, 0:D], a["L3_gnn_W2"].rearrange("(c p) k -> p c k", p=P))
                with nc.allow_non_contiguous_dma(reason="512 scattered words, once"):
                    for k in range(2):
                        for c in range(2):
                            load(acol[:, k, c:c + 1], a["L1_gnn_A"][0:1, k * D + c * P:k * D + (c + 1) * P].rearrange("a p -> p a"))
                for k, name in enumerate(("L3_gnn_att_src1", "L3_gnn_att_dst1", "L3_gnn_att_src2", "L3_gnn_att_dst2")):
                    load(att[:, k, :], a[name].rearrange("(a h) c -> a (h c)", a=1).to_broadcast([P, D]))
                for k, name in (("ln6g", "L2_gnn_ln6_g"), ("ln6b", "L2_gnn_ln6_b"), ("ln7g", "L2_gnn_ln7_g"),
                                ("ln7b", "L2_gnn_ln7_b"), ("gb1", "L3_gnn_b1"), ("gb2", "L3_gnn_b2")):
                    for j in range(GT):
                        load(g[k][:, j, :], a[name].rearrange("(a c) -> a c", a=1).to_broadcast([P, D]))
                for k, name in (("b6", "L2_gnn_b6"), ("b7", "L2_gnn_b7")):
                    load(g[k][:], a[name].rearrange("(a c) -> a c", a=1).to_broadcast([P, D]))
                for k, name in enumerate(("L0_gnn_b", "L2_gnn_bp")):
                    load(bias[:, k, :], a[name].rearrange("(a c) -> a c", a=1))
                sp.wait_ge(split, 1)
                for k, name in enumerate(("b0", "bp")):
                    for part in range(3):
                        sp.dma_start(g[name][part:part + 1, :], parts[:, k, part, :]).then_inc(moved, 16)
                sp.wait_ge(moved, 6 * 16)

            @block.gpsimd
            def _(pool):
                pool.memset(g["ident"][:], 0.0).then_inc(zeroed, 1)
                pool.wait_ge(zeroed, 1)
                pool.affine_select(out=g["ident"][:], in_=g["ident"][:], compare_op=ALU.not_equal, fill=1.0, base=0,
                                   pattern=[[-1, P]], channel_multiplier=1).then_inc(zeroed, 1)
                pool.iota(g["iota"][:], [[1, P]], base=0, channel_multiplier=0,
                          allow_small_or_imprecise_dtypes=True).then_inc(zeroed, 1)

            @block.tensor
            def _(pe):
                pe.wait_ge(zeroed, 3)
                pe.wait_ge(loaded, 16 * loads[0])
                for n, (k, _, _) in enumerate(names):
                    for ci in range(2):
                        for co in range(2):
                            last = pe.transpose(pt[n][:, ci * D + co * P:ci * D + (co + 1) * P],
                                                raw[k][:, co, ci * P:(ci + 1) * P], g["ident"][:])
                    last.then_inc(transposed, 1)
                pe.wait_ge(vecs, 1)
                for k in range(2):
                    for c in range(2):
                        last = pe.matmul(pv[:, k, :], arow[:, k, c, :], raw["w1"][:, c, :], start=(c == 0), stop=(c == 1))
                last.then_inc(transposed, 1)

            @block.vector
            def _(dve):
                link = chain(dve, done)
                dve.memset(g["eps"][:], LN_EPS)
                dve.memset(g["ones3"][:], 1.0)
                dve.memset(g["zero"][:], 0.0)
                link(dve.memset(arow[:], 1.0))
                dve.wait_ge(loaded, 16 * loads[0])
                for k in range(2):
                    for c in range(2):
                        last = dve.tensor_scalar(arow[:, k, c, :], arow[:, k, c, :], acol[:, k, c:c + 1], None, ALU.mult)
                last.then_inc(vecs, 1)
                for w, base in ((g["g1w"], 0), (g["g2w"], 2)):
                    for k in range(2):
                        for c in range(2):
                            last = dve.tensor_tensor(prod[:, c, base + k, :], w[:, c, 0:D], att[:, base + k, :], ALU.mult)
                link(last)
                for w, base in ((g["g1w"], 0), (g["g2w"], 2)):
                    for k in range(2):
                        for c in range(2):
                            last = dve.tensor_reduce(w[:, c, D + k * HEADS:D + (k + 1) * HEADS],
                                                     prod[:, c, base + k, :].rearrange("p (h c) -> p h c", h=HEADS),
                                                     AX.X, ALU.add)
                link(last)
                link(dve.tensor_copy(parts[:, :, 0, :], bias[:]))
                link(dve.tensor_tensor(rest[:, :, 0, :], bias[:], parts[:, :, 0, :], ALU.subtract))
                link(dve.tensor_copy(parts[:, :, 1, :], rest[:, :, 0, :]))
                link(dve.tensor_tensor(rest[:, :, 1, :], rest[:, :, 0, :], parts[:, :, 1, :], ALU.subtract))
                dve.tensor_copy(parts[:, :, 2, :], rest[:, :, 1, :]).then_inc(split, 1)
                for n, (_, _, k) in enumerate(names):
                    dve.wait_ge(transposed, n + 1)
                    dve.tensor_copy(g[k][:], pt[n][:].rearrange("p (c k) -> p c k", c=2))
                dve.wait_ge(transposed, len(names) + 1)
                dve.tensor_copy(g["vsrc"][:], pv[:, 0, :])
                dve.tensor_copy(g["vdst"][:], pv[:, 1, :])


def edge_tables(nc, a, g):
    full = E // (2 * P)
    tail = E - full * 2 * P
    with Phase(nc) as ph:
        names = ("src", "dst", "prev", "next")
        ints = {k: ph.sb("i_" + k, [EROWS, 2 * P], I32) for k in names}
        rows = {k: ph.sb("r_" + k, [EROWS, 2 * P]) for k in names}
        ewR = ph.sb("ewR", [EROWS, 2 * P])
        before = ph.sb("before", [EROWS, 2], I32)
        beforef = ph.sb("beforef", [EROWS, 2])
        first, lastf, tstart, rank, ones = (ph.sb(n, [EROWS, 2 * P]) for n in ("firstR", "lastR", "tstart", "rankR", "onesR"))
        anyf = ph.sb("anyf", [EROWS, 2, HEADS])
        anyone = ph.sb("anyone", [EROWS, 2])
        cont, key, rep, node0 = (ph.sb(n, [EROWS, 2]) for n in ("cont", "key", "rep", "node0"))
        idx0 = ph.sb("idx0", [EROWS, 2], I32)
        diag = ph.sb("diag", [EROWS, 2, EROWS])
        fdst = ph.sb("fdst", [P, ETILES], I32)
        rowid = ph.sb("rowid", [P, ETILES], I32)
        rowf = ph.sb("rowf", [P, ETILES])
        tbase = ph.sb("tbase", [P, ETILES])
        attr = [ph.sb(f"attr{k}", [P, ETILES // 4, EDIM]) for k in range(2)]
        aerow = ph.sb("aerow", [P, EDIM])
        idx = ph.sb("idxs", [P, 2 * HALF], I32)
        val = ph.sb("vals", [P, 2 * HALF], I32)
        fill = ph.sb("fill", [EROWS, 4 * P], I32)
        pieceR = ph.sb("pieceR", [EROWS, 4 * P], I32)
        pieceF = ph.sb("pieceF", [EROWS, 4 * P])
        pc = [ph.ps(f"pc{k}", [P, 512]) for k in range(5)]
        prow = ph.ps("prow", [P, 2, P])
        pany = ph.ps("pany", [P, 2, P])
        (ready, loaded, done, turned, filled, idxed, told, read, ptrs, attrd, bases) = (
            ph.sem(n) for n in ("ready", "loaded", "done", "turned", "filled", "idxed", "told", "read",
                                "ptrs", "attrd", "bases"))
        passed = ph.sem("passed")
        attrs = [ph.sem(f"attrs{k}") for k in range(4)]
        scattered = [ph.sem(f"scattered{h}") for h in range(2)]
        q4 = ETILES // 4
        nloads = [0]
        with nc.Block() as block:
            @block.sync
            def _(sp):
                sp.wait_ge(ready, 1)
                nloads[0] = 0

                def load(o, i):
                    sp.dma_start(o, i).then_inc(loaded, 16)
                    nloads[0] += 1
                flat = {"src": a["src"], "dst": a["dst"], "prev": a["dst"], "next": a["dst"]}

                def rowsof(k, lo, n):
                    return flat[k][lo:lo + n * 2 * P].rearrange("(q i) -> q i", i=2 * P)

                def one(k, lo, n):
                    return flat[k][lo:lo + n].rearrange("(q i) -> q i", q=1)
                for k in ("src", "dst"):
                    load(ints[k][0:full, :], rowsof(k, 0, full))
                    load(ints[k][full:full + 1, 0:tail], one(k, full * 2 * P, tail))
                load(ints["prev"][0:1, 1:2 * P], one("prev", 0, 2 * P - 1))
                load(ints["prev"][1:full, :], rowsof("prev", 2 * P - 1, full - 1))
                load(ints["prev"][full:full + 1, 0:tail + 1], one("prev", full * 2 * P - 1, tail + 1))
                load(ints["next"][0:full, :], rowsof("next", 1, full))
                load(ints["next"][full:full + 1, 0:tail - 1], one("next", full * 2 * P + 1, tail - 1))
                load(ewR[0:full, :], a["edge_weight"][0:full * 2 * P].rearrange("(q i) -> q i", i=2 * P))
                load(ewR[full:full + 1, 0:tail], a["edge_weight"][full * 2 * P:E].rearrange("(q i) -> q i", q=1))
                with nc.allow_non_contiguous_dma(reason="97 words, once"):
                    load(before[1:EROWS, 0:1], rowsof("dst", 0, EROWS - 1)[:, P - 1:P])
                load(aerow[:], a["L1_gnn_A"][0:1, 2 * D:2 * D + EDIM].to_broadcast([P, EDIM]))
                sp.dma_start(g["piece_of"].rearrange("(q i) a -> q (i a)", q=EROWS), fill[:]).then_inc(filled, 16)
                for k in range(4):
                    lo = k * q4 * P
                    n = min(q4, (E - lo) // P)
                    if k >= 2:
                        sp.wait_ge(attrd, k - 1)
                    if n < q4:
                        sp.dma_start(attr[k % 2][0:E - lo - n * P, n, :], a["edge_attr_64"][lo + n * P:E, :]).then_inc(attrs[k], 16)
                    sp.dma_start(attr[k % 2][:, 0:n, :],
                                 a["edge_attr_64"][lo:lo + n * P, :].rearrange("(t p) c -> p t c", p=P)).then_inc(attrs[k], 16)
                for h in range(2):
                    sp.wait_ge(scattered[h], EITER * HALF * 16)
                sp.dma_start(pieceR[:], g["piece_of"].rearrange("(q i) a -> q (i a)", q=EROWS)).then_inc(ptrs, 16)

            @block.gpsimd
            def _(pool):
                pool.iota(tbase[:], [[P, ETILES]], base=0, channel_multiplier=0,
                          allow_small_or_imprecise_dtypes=True).then_inc(bases, 1)
                pool.wait_ge(filled, 16)
                with pool.Fori(0, EITER) as i:
                    for h in range(2):
                        pool.wait_ge(idxed, 2 * i + h + 1)
                        carry_wait(pool, passed)
                        for j in range(h * HALF, (h + 1) * HALF):
                            pool.indirect_dma_start(g["piece_of"], bass.IndirectOffsetOnAxis(idx[:, j:j + 1], 0),
                                                    val[:, j:j + 1], None, bounds_check=NPAD - 1,
                                                    oob_is_err=False).then_inc(scattered[h], 16)
                for h in range(2):
                    pool.wait_ge(scattered[h], EITER * HALF * 16)
                for h in range(2):
                    pool.indirect_dma_start(g["target"][:, h:h + 1], None, g["piece_of"],
                                            bass.IndirectOffsetOnAxis(idx0[:, h:h + 1], 0), bounds_check=NPAD - 1,
                                            oob_is_err=False).then_inc(told, 16)
                pool.wait_ge(told, 32)

            @block.tensor
            def _(pe):
                pe.wait_ge(turned, 1)
                for k, r in enumerate((rows["src"], rows["dst"], rank, first, ewR)):
                    for h in range(2):
                        last = pe.transpose(pc[k][:, h * P:h * P + EROWS], r[:, h * P:(h + 1) * P], g["ident"][0:EROWS, 0:EROWS])
                last.then_inc(read, 1)
                for k in range(2):
                    last = pe.matmul(pany[0:HEADS, k, 0:EROWS], anyf[:, k, :], g["ident"][0:EROWS, 0:EROWS], start=True, stop=True)
                for h in range(2):
                    last = pe.matmul(prow[0:EROWS, h, 0:EROWS], ones[:, 0:EROWS], diag[:, h, :], start=True, stop=True)
                last.then_inc(read, 1)
                pe.wait_ge(turned, 2)
                for j in range(4):
                    last = pe.transpose(pc[0][:, j * P:j * P + EROWS], pieceF[:, j * P:(j + 1) * P], g["ident"][0:EROWS, 0:EROWS])
                last.then_inc(read, 1)

            @block.vector
            def _(dve):
                link = chain(dve, done)
                for k, v in (("src", 0), ("dst", PAD_NODE), ("prev", PAD_NODE), ("next", -5)):
                    dve.memset(ints[k][:], v)
                dve.memset(before[:], -1)
                dve.memset(ewR[:], 0.0)
                dve.memset(ones[:], 1.0)
                dve.memset(fill[:], NO_EDGES)
                dve.memset(g["target"][:], FAR)
                dve.memset(g["src"][:], 0)
                dve.memset(g["dst"][:], 0)
                dve.memset(g["piece"][:], NO_EDGES)
                link(dve.memset(attr[1][:, q4 - 1, :], 0.0))
                dve.memset(ints["prev"][0:1, 0:1], -1).then_inc(ready, 1)
                dve.wait_ge(loaded, 16 * nloads[0])
                for k in names:
                    last = dve.tensor_copy(rows[k][:], ints[k][:])
                link(last)
                link(dve.tensor_copy(beforef[:], before[:]))
                link(dve.tensor_copy(beforef[:, 1:2], rows["prev"][:, 0:1]))
                dve.tensor_tensor(first[:], rows["dst"][:], rows["prev"][:], ALU.not_equal)
                link(dve.tensor_tensor(lastf[:], rows["dst"][:], rows["next"][:], ALU.not_equal))
                link(dve.tensor_copy(tstart[:], first[:]))
                link(dve.memset(tstart[:].rearrange("q (h i) -> q h i", h=2)[:, :, 0:1], 1.0))
                for h in range(2):
                    s = slice(h * P, (h + 1) * P)
                    dve.tensor_tensor_scan(rank[:, s], ones[:, s], tstart[:, s], -1.0, ALU.mult, ALU.add)
                dve.tensor_scalar(g["startR"][:], first[:], -BIG, None, ALU.mult)
                dve.tensor_scalar(g["endR"][:], lastf[:], -BIG, None, ALU.mult)
                dve.tensor_reduce(anyone[:, 0:1], first[:], AX.X, ALU.max)
                link(dve.tensor_reduce(anyone[:, 1:2], lastf[:], AX.X, ALU.max))
                for k in range(2):
                    dve.tensor_scalar(anyf[:, k, :], ones[:, 0:HEADS], anyone[:, k:k + 1], -BIG, ALU.mult, ALU.mult)
                heads = first[:].rearrange("q (h i) -> q h i", h=2)[:, :, 0]
                dve.tensor_scalar(cont[:], heads, -1.0, 1.0, ALU.mult, ALU.add)
                link(dve.tensor_copy(node0[:], rows["dst"][:].rearrange("q (h i) -> q h i", h=2)[:, :, 0]))
                link(dve.tensor_tensor(rep[:], beforef[:], node0[:], ALU.not_equal))
                link(dve.tensor_tensor(rep[:], rep[:], cont[:], ALU.mult))
                link(dve.tensor_scalar(key[:], node0[:], 1.0, None, ALU.add))
                link(dve.tensor_tensor(key[:], key[:], cont[:], ALU.mult))
                link(dve.tensor_scalar(key[:], key[:], -1.0, None, ALU.add))
                for h in range(2):
                    dve.tensor_scalar(diag[:, h, :], g["ident"][0:EROWS, 0:EROWS], key[:, h:h + 1], None, ALU.mult)
                link(dve.tensor_scalar(beforef[:], rep[:], -float(FAR), float(FAR), ALU.mult, ALU.add))
                link(dve.tensor_tensor(beforef[:], beforef[:], node0[:], ALU.add))
                dve.tensor_copy(idx0[:], beforef[:]).then_inc(turned, 1)
                dve.wait_ge(read, 1)

                def cols(o, k):
                    for h in range(2):
                        last = dve.tensor_copy(o.rearrange("p (q h) -> p h q", h=2)[:, h, :], pc[k][:, h * P:h * P + EROWS])
                    return last
                cols(g["src"][:, 0:ETILES], 0)
                cols(g["dst"][:, 0:ETILES], 1)
                cols(g["rank"][:], 2)
                cols(g["first"][:], 3)
                link(cols(g["ew"][:], 4))
                link(dve.tensor_scalar(rowf[:], g["first"][:], -float(FAR), float(FAR), ALU.mult, ALU.add))
                link(dve.tensor_tensor(rowf[:], rowf[:], g["dst"][:, 0:ETILES], ALU.add))
                link(dve.tensor_copy(fdst[:], rowf[:]))
                dve.wait_ge(bases, 1)
                link(dve.tensor_tensor(rowf[:], tbase[:], g["rank"][:], ALU.add))
                link(dve.tensor_copy(rowid[:], rowf[:]))
                dve.tensor_copy(idx[:], fdst[:, 0:2 * HALF])
                dve.tensor_copy(val[:], rowid[:, 0:2 * HALF]).then_inc(idxed, 2)
                with dve.Fori(0, EITER - 1) as i:
                    for h in range(2):
                        s = slice(h * HALF, (h + 1) * HALF)
                        nxt = bass.ds((i + 1) * 2 * HALF + h * HALF, HALF)
                        dve.wait_ge(scattered[h], (i + 1) * HALF * 16)
                        dve.tensor_copy(idx[:, s], fdst[:, nxt])
                        dve.tensor_copy(val[:, s], rowid[:, nxt]).then_inc(idxed, 1)
                dve.wait_ge(read, 2)
                dve.tensor_copy(g["startrow"][:], pany[0:HEADS, 0, 0:EROWS])
                dve.tensor_copy(g["endrow"][:], pany[0:HEADS, 1, 0:EROWS])
                for h in range(2):
                    for o in range(2):
                        last = dve.tensor_scalar(g["same"][:, h, o, :], prow[0:EROWS, o, 0:EROWS], key[:, h:h + 1],
                                                 cont[:, h:h + 1], ALU.is_equal, ALU.mult)
                link(last)
                for k in range(4):
                    n = min(q4, (E - k * q4 * P) // P)
                    dve.wait_ge(attrs[k], 32 if n < q4 else 16)
                    t = attr[k % 2]
                    link(dve.tensor_tensor(t[:], t[:], spread(aerow[:].rearrange("p (a c) -> p a c", a=1), [P, q4, EDIM]), ALU.mult))
                    dve.tensor_reduce(g["ee"][:, k * q4:(k + 1) * q4], t[:], AX.X, ALU.add).then_inc(attrd, 1)
                dve.wait_ge(ptrs, 16)
                dve.tensor_copy(pieceF[:], pieceR[:]).then_inc(turned, 1)
                dve.wait_ge(read, 3)
                for j in range(4):
                    last = dve.tensor_copy(g["piece"][:, 0:NTILES].rearrange("p (q j) -> p j q", j=4)[:, j, :],
                                           pc[0][:, j * P:j * P + EROWS])
                link(last)


def edge_pass(nc, g, kind, table, beside):
    last_row = table.shape[0] - 1
    slots = 2 * HALF
    with Phase(nc) as ph:
        rows = ph.sb("rows", [P, slots, CW])
        onehot = ph.sb("onehot", [P, slots, P])
        sums = ph.sb("sums", [P, 2, HALF, CW])
        idx = ph.sb("idxs", [P, slots], I32)
        none = ph.sb("none", [1, CW])
        acc = [ph.ps(f"acc{k}", [P, CW]) for k in range(2)]
        passed = ph.sem("passed")
        gathered = [ph.sem(f"gathered{h}") for h in range(2)]
        stored = [ph.sem(f"stored{h}") for h in range(2)]
        (cleared, idx_ready, hot_ready, multiplied, copied, none_ready, none_stored) = (
            ph.sem(n) for n in ("cleared", "idx_ready", "hot_ready", "multiplied", "copied", "none_ready", "none_stored"))
        out = g["pieces"][0:EPAD, :].rearrange("(t r) c -> r t c", r=P)
        with nc.Block() as block:
            @block.gpsimd
            def _(pool):
                pool.wait_ge(cleared, 1)
                with pool.Fori(0, EITER) as i:
                    for h in range(2):
                        pool.wait_ge(idx_ready, 2 * i + h + 1)
                        carry_wait(pool, passed)
                        for j in range(h * HALF, (h + 1) * HALF):
                            pool.indirect_dma_start(rows[:, j, 0:D], None, table,
                                                    bass.IndirectOffsetOnAxis(idx[:, j:j + 1], 0), bounds_check=last_row,
                                                    oob_is_err=False).then_inc(gathered[h], 16)

            @block.vector
            def _(dve):
                dve.memset(rows[:], 0.0)
                dve.memset(none[:], 0.0).then_inc(cleared, 1)
                dve.wait_ge(cleared, 1)
                if kind in ("count", "attention"):
                    dve.memset(rows[:, :, D:D + 1], 1.0)
                dve.memset(none[:, D:D + max(beside, 1)], 1.0 if beside else 0.0).then_inc(none_ready, 1)
                dve.tensor_copy(idx[:], g["src"][:, 0:slots]).then_inc(idx_ready, 2)
                with dve.Fori(0, EITER) as i:
                    for h in range(2):
                        for j in range(h * HALF, (h + 1) * HALF):
                            t = bass.ds(i * slots + j, 1)
                            rank = g["rank"][:, t]
                            dve.wait_ge(multiplied, i * slots + j + 1)
                            if kind in ("attention", "gcn"):
                                w = g["exs"][:, t, 0] if kind == "attention" else g["ew"][:, t]
                                ins = dve.tensor_scalar(onehot[:, j, :], g["iota"][:], rank, w, ALU.is_equal, ALU.mult)
                            else:
                                if kind == "gat" and j % HALF == 0:
                                    dve.wait_ge(gathered[h], (i + 1) * HALF * 16)
                                if kind == "gat":
                                    row = rows[:, j, 0:D].rearrange("p (h c) -> p h c", h=HEADS)
                                    ex = g["exs"][:, t, :].rearrange("p a h -> p (a h)").unsqueeze(2)
                                    dve.tensor_tensor(row, row, ex.to_broadcast([P, HEADS, HID]), ALU.mult)
                                    dve.tensor_copy(rows[:, j, D:CW], g["exd"][:, t, :].rearrange("p a h -> p (a h)"))
                                else:
                                    dve.tensor_copy(rows[:, j, D + 1:D + 2], g["ew"][:, t])
                                ins = dve.tensor_scalar(onehot[:, j, :], g["iota"][:], rank, None, ALU.is_equal)
                            ins.then_inc(hot_ready, 1)
                    for h in range(2):
                        dve.wait_ge(multiplied, (i + 1) * slots + (h + 1) * HALF)
                        s = slice(h * HALF, (h + 1) * HALF)
                        dve.tensor_copy(idx[:, s], g["src"][:, bass.ds((i + 1) * slots + h * HALF, HALF)]).then_inc(idx_ready, 1)

            @block.tensor
            def _(pe):
                pe.sem_inc(multiplied, slots)
                with pe.Fori(0, EITER) as i:
                    for j in range(slots):
                        if j % HALF == 0:
                            pe.wait_ge(gathered[j // HALF], (i + 1) * HALF * 16)
                        pe.wait_ge(hot_ready, i * slots + j + 1)
                        pe.wait_ge(copied, i * slots + j + 1)
                        pe.matmul(acc[j % 2][:], onehot[:, j, :], rows[:, j, :], start=True, stop=True).then_inc(multiplied, 1)

            @block.scalar
            def _(act):
                act.sem_inc(copied, 2)
                with act.Fori(0, EITER) as i:
                    for h in range(2):
                        act.wait_ge(stored[h], (i + 1) * 16)
                        for j in range(h * HALF, (h + 1) * HALF):
                            act.wait_ge(multiplied, (i + 1) * slots + j + 1)
                            act.activation(sums[:, h, j - h * HALF, :], acc[j % 2][:], ACT.Copy).then_inc(copied, 1)

            @block.sync
            def _(sp):
                for h in range(2):
                    sp.dma_start(g["credit"][:, 8 * h:8 * h + 8], g["zero"][:]).then_inc(stored[h], 16)
                sp.wait_ge(none_ready, 1)
                sp.dma_start(g["pieces"][NO_EDGES:NO_EDGES + 1, :], none[:]).then_inc(none_stored, 16)
                with sp.Fori(0, EITER) as i:
                    for h in range(2):
                        sp.wait_ge(copied, i * slots + (h + 1) * HALF + 2)
                        sp.dma_start(out[:, bass.ds(i * slots + h * HALF, HALF), :], sums[:, h, :, :]).then_inc(stored[h], 16)
                sp.wait_ge(none_stored, 16)
                for h in range(2):
                    sp.wait_ge(stored[h], (EITER + 1) * 16)
    merge_pieces(nc, g)


def merge_pieces(nc, g):
    with Phase(nc) as ph:
        firsts = ph.sb("firsts", [EROWS, 2, CW])
        target = ph.sb("targets", [EROWS, 2, CW])
        sums = [ph.ps(f"sums{h}", [P, CW]) for h in range(2)]
        loaded, cleared, summed, added, got, put = (ph.sem(n) for n in ("loaded", "cleared", "summed", "added", "got", "put"))
        with nc.Block() as block:
            @block.sync
            def _(sp):
                sp.dma_start(firsts[:], g["pieces"][0:EPAD, :].rearrange("(q h r) c -> q h r c", h=2, r=P)[:, :, 0, :]).then_inc(loaded, 16)

            @block.gpsimd
            def _(pool):
                pool.wait_ge(cleared, 1)
                for h in range(2):
                    pool.indirect_dma_start(target[:, h, :], None, g["pieces"], bass.IndirectOffsetOnAxis(g["target"][:, h:h + 1], 0),
                                            bounds_check=EPAD - 1, oob_is_err=False).then_inc(got, 16)
                pool.wait_ge(added, 2)
                for h in range(2):
                    pool.indirect_dma_start(g["pieces"], bass.IndirectOffsetOnAxis(g["target"][:, h:h + 1], 0), target[:, h, :], None,
                                            bounds_check=EPAD - 1, oob_is_err=False).then_inc(put, 16)
                pool.wait_ge(put, 32)

            @block.tensor
            def _(pe):
                pe.wait_ge(loaded, 16)
                for o in range(2):
                    for h in range(2):
                        last = pe.matmul(sums[o][0:EROWS, :], g["same"][:, h, o, :], firsts[:, h, :], start=(h == 0), stop=(h == 1))
                    last.then_inc(summed, 1)

            @block.vector
            def _(dve):
                dve.memset(target[:], 0.0).then_inc(cleared, 1)
                dve.wait_ge(got, 32)
                for o in range(2):
                    dve.wait_ge(summed, o + 1)
                    dve.tensor_tensor(target[:, o, :], target[:, o, :], sums[o][0:EROWS, :], ALU.add).then_inc(added, 1)


def edge_scores(nc, g, heads):
    slots = 2 * HALF
    gat = heads > 1
    with Phase(nc) as ph:
        idx = ph.sb("idxs", [P, 2, slots], I32)
        got = ph.sb("got", [P, 2, slots, SCORES])
        both = ph.sb("both", [P, 2, ETILES, SCORES])
        score = ph.sb("score", [P, heads, ETILES])
        selfs = ph.sb("selfs", [P, heads, ETILES])
        most = ph.sb("most", [P, heads, ETILES])
        scoreR, fwd, bwd, zero = (ph.sb(n, [EROWS, heads, 2 * P]) for n in ("scoreR", "fwd", "bwd", "zeroR"))
        ends = ph.sb("ends", [EROWS, 2, HEADS])
        endrow = ph.sb("endsrow", [HEADS, 2, EROWS])
        carryrow = ph.sb("carryrow", [HEADS, 2, EROWS + 1])
        carry = ph.sb("carry", [EROWS, 2, HEADS])
        pr = [ph.ps(f"pr{k}", [P, 2, 2 * P]) for k in range(2)]
        pe_rows = ph.ps("perows", [P, 2, P])
        pcar = ph.ps("pcar", [P, 2, HEADS])
        pcols = [ph.ps(f"pcols{k}", [P, 2, 2 * P]) for k in range(2)]
        passed = ph.sem("passed")
        gathered = [ph.sem(f"gathered{h}") for h in range(2)]
        idx_ready, done, scored, turned, exped, act_done = (
            ph.sem(n) for n in ("idx_ready", "done", "scored", "turned", "exped", "act_done"))
        per = EITER * 4
        with nc.Block() as block:
            @block.gpsimd
            def _(pool):
                with pool.Fori(0, EITER) as i:
                    for h in range(2):
                        pool.wait_ge(idx_ready, 2 * i + h + 1)
                        carry_wait(pool, passed)
                        for j in range(h * HALF, (h + 1) * HALF):
                            for k in range(2):
                                pool.indirect_dma_start(got[:, k, j, :], None, g["scores"],
                                                        bass.IndirectOffsetOnAxis(idx[:, k, j:j + 1], 0), bounds_check=NPAD - 1,
                                                        oob_is_err=False).then_inc(gathered[h], 16)

            @block.vector
            def _(dve):
                link = chain(dve, done)
                for k, name in enumerate(("src", "dst")):
                    last = dve.tensor_copy(idx[:, k, :], g[name][:, 0:slots])
                last.then_inc(idx_ready, 2)
                dve.memset(zero[:], 0.0)
                dve.memset(carryrow[:], -BIG)
                with dve.Fori(0, EITER) as i:
                    for h in range(2):
                        s = slice(h * HALF, (h + 1) * HALF)
                        dve.wait_ge(gathered[h], (i + 1) * 2 * HALF * 16)
                        for k in range(2):
                            dve.tensor_copy(both[:, k, bass.ds(i * slots + h * HALF, HALF), :], got[:, k, s, :])
                        for k, name in enumerate(("src", "dst")):
                            last = dve.tensor_copy(idx[:, k, s], g[name][:, bass.ds((i + 1) * slots + h * HALF, HALF)])
                        last.then_inc(idx_ready, 1)
                dve.wait_ge(idx_ready, 2 * EITER + 2)
                for h in range(heads):
                    last = dve.tensor_tensor(score[:, h, :], both[:, 0, :, h], both[:, 1, :, HEADS + h], ALU.add)
                link(last)
                if gat:
                    for h in range(heads):
                        last = dve.tensor_tensor(selfs[:, h, :], both[:, 1, :, h], both[:, 1, :, HEADS + h], ALU.add)
                    link(last)
                    link(dve.scalar_tensor_tensor(selfs[:], selfs[:], 0.2, selfs[:], ALU.mult, ALU.max))
                else:
                    link(dve.tensor_tensor(score[:, 0, :], score[:, 0, :], g["ee"][:], ALU.add))
                dve.scalar_tensor_tensor(score[:], score[:], 0.2, score[:], ALU.mult, ALU.max).then_inc(scored, 1)
                dve.wait_ge(turned, 1)
                for h in range(heads):
                    last = dve.tensor_copy(scoreR[:, h, :], pr[h // 2][0:EROWS, h % 2, :])
                link(last)

                def scans(start):
                    for h in range(heads):
                        dve.tensor_tensor_scan(fwd[:, h, :], g["startR"][:], scoreR[:, h, :],
                                               -BIG if start is None else start[:, 0, h:h + 1], ALU.add, ALU.max)
                        last = dve.tensor_tensor_scan(bwd[:, h, ::-1], g["endR"][:, ::-1], scoreR[:, h, ::-1],
                                                      -BIG if start is None else start[:, 1, h:h + 1], ALU.add, ALU.max)
                    link(last)
                scans(None)
                dve.tensor_copy(ends[:, 0, 0:heads], fwd[:, :, 2 * P - 1])
                dve.tensor_copy(ends[:, 1, 0:heads], bwd[:, :, 0]).then_inc(scored, 1)
                dve.wait_ge(turned, 2)
                link(dve.tensor_copy(endrow[0:heads, :, :], pe_rows[0:heads, :, 0:EROWS]))
                dve.tensor_tensor_scan(carryrow[0:heads, 0, 1:EROWS + 1], g["startrow"][0:heads, :], endrow[0:heads, 0, :],
                                       -BIG, ALU.add, ALU.max)
                rev = slice(EROWS - 1, None, -1)
                dve.tensor_tensor_scan(carryrow[0:heads, 1, rev], g["endrow"][0:heads, ::-1], endrow[0:heads, 1, ::-1],
                                       -BIG, ALU.add, ALU.max).then_inc(scored, 1)
                dve.wait_ge(turned, 3)
                link(dve.tensor_copy(carry[:, :, 0:heads], pcar[0:EROWS, :, 0:heads]))
                scans(carry)
                dve.tensor_tensor(fwd[:], fwd[:], bwd[:], ALU.max).then_inc(scored, 1)
                dve.wait_ge(turned, 4)
                for h in range(heads):
                    last = dve.tensor_copy(most[:, h, :].rearrange("p (q a) -> p a q", a=2),
                                           pcols[h // 2][:, h % 2, :].rearrange("p (a q) -> p a q", a=2)[:, :, 0:EROWS])
                link(last)
                if gat:
                    link(dve.tensor_tensor(most[:], most[:], selfs[:], ALU.max))
                    dve.tensor_tensor(selfs[:], selfs[:], most[:], ALU.subtract)
                dve.tensor_tensor(score[:], score[:], most[:], ALU.subtract).then_inc(scored, 1)
                dve.wait_ge(exped, 1)
                if gat:
                    for h in range(heads):
                        last = dve.tensor_tensor(selfs[:, h, :], selfs[:, h, :], g["first"][:], ALU.mult)
                    link(last)
                    for h in range(heads):
                        dve.tensor_copy(g["exd"][:, :, HEADS + h], selfs[:, h, :])
                        dve.tensor_tensor(g["exd"][:, :, h], selfs[:, h, :], score[:, h, :], ALU.add)
                for h in range(heads):
                    last = dve.tensor_copy(g["exs"][:, :, h], score[:, h, :])
                link(last)

            @block.tensor
            def _(pe):
                ident = g["ident"]
                pe.wait_ge(scored, 1)
                for h in range(heads):
                    for a in range(2):
                        last = pe.transpose(pr[h // 2][0:EROWS, h % 2, a * P:(a + 1) * P],
                                            score[:, h, :].rearrange("p (q a) -> p a q", a=2)[:, a, :], ident[:])
                last.then_inc(turned, 1)
                pe.wait_ge(scored, 2)
                for k in range(2):
                    last = pe.transpose(pe_rows[0:heads, k, 0:EROWS], ends[:, k, 0:heads], ident[0:EROWS, 0:EROWS])
                last.then_inc(turned, 1)
                pe.wait_ge(scored, 3)
                for k in range(2):
                    last = pe.transpose(pcar[0:EROWS, k, 0:heads], carryrow[0:heads, k, k:k + EROWS], ident[0:heads, 0:heads])
                last.then_inc(turned, 1)
                pe.wait_ge(scored, 4)
                for h in range(heads):
                    for a in range(2):
                        last = pe.transpose(pcols[h // 2][:, h % 2, a * P:a * P + EROWS], fwd[:, h, a * P:(a + 1) * P],
                                            ident[0:EROWS, 0:EROWS])
                last.then_inc(turned, 1)

            @block.scalar
            def _(act):
                act.wait_ge(scored, 5)
                if gat:
                    act.activation(selfs[:], selfs[:], ACT.Exp)
                act.activation(score[:], score[:], ACT.Exp).then_inc(exped, 1)


class Steps:

    def __init__(self, eng, sem):
        self.eng, self.sem, self.base, self.n = eng, sem, 0, 0

    def mark(self, ins):
        self.n += 1
        ins.then_inc(self.sem, 1)
        return self.base + self.n

    def wait(self, mark):
        self.eng.wait_ge(self.sem, mark)

    def link(self, ins):
        self.wait(self.mark(ins))


def in_turn(eng, stages, steps=None, links=0):
    last = max(lag for lag, _ in stages)
    fill = -(-last // SLOTS)

    def step(i, r):
        running = []
        for lag, f in stages:
            if not isinstance(i, int) or 0 <= i * SLOTS + r - lag < NGROUPS:
                running.append(f(i * SLOTS + (r - lag), (r - lag) % SLOTS, i + ((r - lag) // SLOTS + 1)))
        running = [f for f in running if f is not None]
        while running:
            running = [f for f in running if next(f, StopIteration) is not StopIteration]
    for i in range(fill):
        for r in range(SLOTS):
            step(i, r)
    with eng.Fori(fill, NITER) as i:
        if steps:
            before = steps.n
            steps.base, steps.n = before + (i - fill) * (SLOTS * links), 0
        for r in range(SLOTS):
            step(i, r)
        if steps:
            assert steps.n == SLOTS * links, steps.n
    if steps:
        steps.base, steps.n = before + (NITER - fill) * (SLOTS * links), 0
    for r in range(last):
        step(NITER, r)


class Nodes:

    def __init__(self, nc, ph, g, loads, stores, signals):
        self.nc, self.ph, self.g = nc, ph, g
        self.in_bufs = {k: ph.sb(k, [P, SLOTS, GT, D]) for k, *_ in loads}
        self.loads, self.stores = loads, stores
        self.pieces = ph.sb("cb", [P, SLOTS, GT, CW])
        self.idx = ph.sb("idxs", [P, SLOTS * GT], I32)
        self.loaded = {k: [ph.sem(f"loaded_{k}{s}") for s in range(SLOTS)] for k, *_ in loads}
        self.got = [ph.sem(f"got{s}") for s in range(SLOTS)]
        self.stored = {k: [ph.sem(f"stored_{k}{s}") for s in range(SLOTS)] for k, *_ in stores}
        self.idx_ready = ph.sem("idx_ready")
        self.step = ph.sem("vector_step")
        self.passed, self.passed_v = ph.sem("passed"), ph.sem("passed_v")
        self.sig = {k: ph.sem(k) for k in signals}

    def start(self, eng, *signals):
        for k in signals:
            eng.sem_inc(self.sig[k], CREDIT)

    def done(self, ins, signal):
        ins.then_inc(self.sig[signal], 1)

    def need(self, eng, signal, n, back=0):
        eng.wait_ge(self.sig[signal], n + (1 + CREDIT - back))

    def need_load(self, eng, k, turn, s):
        eng.wait_ge(self.loaded[k][s], turn * 16)

    def need_pieces(self, eng, turn, s):
        eng.wait_ge(self.got[s], turn * (16 * GT))

    def need_stored(self, eng, k, turn, s):
        eng.wait_ge(self.stored[k][s], turn * 16)

    def gathers(self, pool):
        def f(n, s, turn):
            pool.wait_ge(self.idx_ready, n + 1)
            carry_wait(pool, self.passed)
            for j in range(GT):
                pool.indirect_dma_start(self.pieces[:, s, j, :], None, self.g["pieces"],
                                        bass.IndirectOffsetOnAxis(self.idx[:, s * GT + j:s * GT + j + 1], 0),
                                        bounds_check=EPAD, oob_is_err=False).then_inc(self.got[s], 16)
        return f

    def gather(self, pool):
        in_turn(pool, [(0, self.gathers(pool))])

    def first_indices(self, dve):
        dve.tensor_copy(self.idx[:], self.g["piece"][:, 0:SLOTS * GT]).then_inc(self.idx_ready, SLOTS)

    def next_indices(self, dve, n, s):
        dve.tensor_copy(self.idx[:, s * GT:(s + 1) * GT],
                        self.g["piece"][:, bass.ds((n + SLOTS) * GT, GT)]).then_inc(self.idx_ready, 1)

    def start_stores(self, sp):
        c = 0
        for k, *_ in self.stores:
            for s in range(SLOTS):
                sp.dma_start(self.g["credit"][:, c:c + 8], self.g["zero"][:]).then_inc(self.stored[k][s], 16)
                c += 8

    def traffic(self, sp):
        self.start_stores(sp)

        def load(k, table, free):
            def f(n, s, turn):
                self.need(sp, free, n, back=SLOTS)
                self.move(sp, n, table, self.in_bufs[k][:, s, :, :], self.loaded[k][s], load=True)
            return f

        def store(k, table, buf, ready):
            def f(n, s, turn):
                self.need(sp, ready, n)
                self.move(sp, n, table, buf[:, s, :, :], self.stored[k][s], load=False)
            return f
        moves = [(lag + 1, load(k, table, free)) for k, table, free, lag in self.loads]
        moves += [(lag + SLOTS + 1, store(*x)) for *x, lag in self.stores]
        in_turn(sp, moves)
        for k, *_ in self.stores:
            for s in range(SLOTS):
                sp.wait_ge(self.stored[k][s], (NITER + 1) * 16)

    @staticmethod
    def partial(table):
        return table.shape[0] != NPAD

    def move(self, sp, n, table, buf, sem, load):
        if isinstance(n, int) and self.partial(table) and (n + 1) * GROUP > N:
            lo = n * GROUP
            assert 0 < N - lo <= P
            dram, chip = table[lo:N, :], buf[0:N - lo, 0, :]
        else:
            dram = table[bass.ds(n * GROUP, GROUP), :].rearrange("(j p) c -> p j c", p=P)
            chip = buf
        sp.dma_start(chip if load else dram, dram if load else chip).then_inc(sem, 16)


def turn(pe, bank, x, ident):
    for c in range(2):
        for j in range(GT):
            last = pe.transpose(bank[:, (c * GT + j) * P:(c * GT + j + 1) * P], x[:, j, c * P:(c + 1) * P], ident[:])
    return last


def times(pe, bank, xT, w, lo, hi, first=True, last=True):
    for j in range(GT):
        for c in range(2):
            ins = pe.matmul(bank[:, j, 0:hi - lo], xT[:, (c * GT + j) * P:(c * GT + j + 1) * P], w[:, c, lo:hi],
                            start=first and c == 0, stop=last and c == 1)
    return ins


def carry_wait(eng, sem):
    eng.sem_inc(sem, 1)


def stats(dve, steps, y, st, mv, n, signal):
    for j in range(GT):
        last = dve.bn_stats(st[:, j, :], y[:, j, :])
    mark = steps.mark(last)
    yield
    steps.wait(mark)
    carry_wait(dve, n.passed_v)
    for j in range(GT):
        last = dve.bn_aggr(mv[:, j, :], st[:, j, :])
    n.done(last, signal)


def normalise(dve, steps, out, y, mv, std, rstd, done):
    mark = steps.mark(dve.reciprocal(rstd, std))
    yield
    steps.wait(mark)
    for j in range(GT):
        last = dve.tensor_scalar(out[:, j, :], y[:, j, :], mv[:, j, 0:1], rstd[:, j:j + 1], ALU.subtract, ALU.mult)
    done(last)


def affine(dve, steps, n, z, x, mv, std, rstd, gain, shift):
    steps.mark(dve.reciprocal(rstd, std))
    for j in range(GT):
        last = dve.scalar_tensor_tensor(z[:, j, :], x[:, j, :], mv[:, j, 0:1], gain[:, j, :], ALU.subtract, ALU.mult)
    mark = steps.mark(last)
    yield
    steps.wait(mark)
    for j in range(GT):
        last = dve.scalar_tensor_tensor(z[:, j, :], z[:, j, :], rstd[:, j:j + 1], shift[:, j, :], ALU.mult, ALU.add)
    n.done(last, "z")


def sage_nodes(nc, g, x):
    with Phase(nc) as ph:
        x1 = ph.sb("x1", [P, SLOTS, GT, D])
        sc = ph.sb("sc", [P, SLOTS, GT, SCORES])
        n = Nodes(nc, ph, g, [("x", x, "sum", 4)], [("x1", g["x1"], x1, "x1", 6), ("sc", g["scores"], sc, "out", 6)],
                  ("mean", "turned", "copied", "product", "relu", "squares", "norm", "y", "std", "x1", "out", "inv", "sum"))
        xb, cb = n.in_bufs["x"], n.pieces
        small = ph.sb("small", [P, SLOTS, 4, GT])
        mean = ph.sb("mean", [P, SLOTS, GT, D])
        xT, mT = (ph.sb(k, [P, SLOTS, 2 * GT * P]) for k in ("xT", "mT"))
        relu, y = (ph.sb(k, [P, SLOTS, GT, D]) for k in ("relu", "y"))
        junk = ph.sb("junk", [P, SLOTS, GT, 2, D])
        sq, norm = (ph.sb(k, [P, SLOTS, GT]) for k in ("sq", "norm"))
        inv, std, rstd = (ph.sb(k, [P, SLOTS, GT]) for k in ("inv", "std", "rstd"))
        st = ph.sb("st", [P, SLOTS, GT, 6])
        mv = ph.sb("mv", [P, SLOTS, GT, 2])
        px = [ph.ps(f"px{k}", [P, 2 * GT * P]) for k in range(2)]
        pm = [ph.ps(f"pm{k}", [P, 2 * GT * P]) for k in range(2)]
        po = [ph.ps(f"po{k}", [P, GT, D]) for k in range(2)]
        with nc.Block() as block:
            @block.sync
            def _(sp):
                n.traffic(sp)

            @block.gpsimd
            def _(pool):
                n.gather(pool)

            @block.tensor
            def _(pe):
                n.start(pe, "turned", "product")

                def transposes(m, s, k):
                    n.need_load(pe, "x", k, s)
                    n.need(pe, "copied", m, back=2)
                    turn(pe, px[s % 2], xb[:, s], g["ident"])
                    n.need(pe, "mean", m)
                    n.done(turn(pe, pm[s % 2], mean[:, s], g["ident"]), "turned")

                def products(m, s, k):
                    n.need(pe, "copied", m)
                    n.need(pe, "relu", m, back=2)
                    for j in range(GT):
                        pe.matmul(po[s % 2][:, j, :], g["ones3"][:], g["b0"][:], start=True, stop=False)
                        for c in range(4):
                            lo = ((c % 2) * GT + j) * P
                            last = pe.matmul(po[s % 2][:, j, :], (xT, mT)[c // 2][:, s, lo:lo + P], g["w0"][:, c, :],
                                             start=False, stop=(c == 3))
                    n.done(last, "product")
                in_turn(pe, [(1, transposes), (2, products)])

            @block.scalar
            def _(act):
                n.start(act, "mean", "copied", "relu", "squares", "norm", "std")

                def means(m, s, k):
                    n.need(act, "inv", m)
                    n.need(act, "turned", m, back=SLOTS)
                    for j in range(GT):
                        last = act.activation(mean[:, s, j, :], cb[:, s, j, 0:D], ACT.Copy, scale=small[:, s, 1, j:j + 1])
                    n.done(last, "mean")

                def copies(m, s, k):
                    n.need(act, "turned", m)
                    n.need(act, "product", m, back=SLOTS)
                    act.activation(xT[:, s, :], px[s % 2][:], ACT.Copy)
                    n.done(act.activation(mT[:, s, :], pm[s % 2][:], ACT.Copy), "copied")

                def relus(m, s, k):
                    n.need(act, "product", m)
                    n.need(act, "x1", m, back=SLOTS)
                    n.done(act.activation(relu[:, s], po[s % 2][:], ACT.Relu), "relu")
                    n.need(act, "relu", m)
                    for j in range(GT):
                        last = act.activation(y[:, s, j, :], relu[:, s, j, :], ACT.Square, accum_out=sq[:, s, j:j + 1])
                    n.done(last, "squares")
                    n.need(act, "squares", m)
                    n.done(act.activation(norm[:, s, :], sq[:, s, :], ACT.Sqrt), "norm")

                def stds(m, s, k):
                    n.need(act, "y", m)
                    n.need(act, "out", m, back=SLOTS)
                    n.done(act.activation(std[:, s, :], mv[:, s, :, 1], ACT.Sqrt, bias=g["eps"][:]), "std")
                in_turn(act, [(1, copies), (3, relus), (5, stds), (0, means)])

            @block.vector
            def _(dve):
                n.start(dve, "inv", "sum", "y", "x1", "out")
                n.first_indices(dve)
                dve.memset(sc[:], 0.0)
                steps = Steps(dve, n.step)

                def invs(m, s, k):
                    n.need_pieces(dve, k, s)
                    n.need(dve, "mean", m, back=SLOTS)
                    mark = steps.mark(dve.tensor_scalar(small[:, s, 0, :], cb[:, s, :, D], 1.0, None, ALU.max))
                    dve.tensor_scalar(g["dis"][:, bass.ds(m * GT, GT)], cb[:, s, :, D + 1], 1.0, None, ALU.add)
                    yield
                    steps.wait(mark)
                    n.done(dve.reciprocal(small[:, s, 1, :], small[:, s, 0, :]), "inv")

                def indices(m, s, k):
                    n.need(dve, "mean", m)
                    n.next_indices(dve, m, s)

                def ys(m, s, k):
                    n.need(dve, "norm", m)
                    n.need_load(dve, "x", k, s)
                    mark = steps.mark(dve.tensor_scalar(small[:, s, 2, :], norm[:, s, :], 1e-12, None, ALU.max))
                    yield
                    steps.wait(mark)
                    mark = steps.mark(dve.reciprocal(inv[:, s, :], small[:, s, 2, :]))
                    yield
                    steps.wait(mark)
                    for j in range(GT):
                        last = dve.scalar_tensor_tensor(y[:, s, j, :], relu[:, s, j, :], inv[:, s, j:j + 1], xb[:, s, j, :], ALU.mult, ALU.add)
                    n.done(last, "sum")
                    yield
                    n.need(dve, "sum", m)
                    yield from stats(dve, steps, y[:, s], st[:, s], mv[:, s], n, "y")

                def outs(m, s, k):
                    n.need(dve, "std", m)
                    n.need_stored(dve, "x1", k, s)
                    n.need_stored(dve, "sc", k, s)
                    yield from normalise(dve, steps, x1[:, s], y[:, s], mv[:, s], std[:, s, :], rstd[:, s],
                                         lambda ins: n.done(ins, "x1"))
                    yield
                    n.need(dve, "x1", m)
                    for j in range(GT):
                        for c, v in enumerate(("vsrc", "vdst")):
                            last = dve.tensor_tensor_reduce(junk[:, s, j, c, :], x1[:, s, j, :], g[v][:], 1.0, 0.0, ALU.mult, ALU.add,
                                                            sc[:, s, j, c * HEADS:c * HEADS + 1])
                    n.done(last, "out")
                in_turn(dve, [(4, ys), (6, outs), (1, indices), (0, invs)], steps, links=5)

    with Phase(nc) as ph:
        root, made = ph.sem("root"), ph.sem("made")
        with nc.Block() as block:
            @block.scalar
            def _(act):
                act.activation(g["dis"][:], g["dis"][:], ACT.Sqrt).then_inc(root, 1)

            @block.vector
            def _(dve):
                dve.wait_ge(root, 1)
                dve.reciprocal(g["dis"][:], g["dis"][:]).then_inc(made, 1)
                dve.wait_ge(made, 1)




def attention_nodes(nc, g):
    with Phase(nc) as ph:
        x2, h = ph.sb("x2", [P, SLOTS, GT, D]), ph.sb("h", [P, SLOTS, GT, D])
        n = Nodes(nc, ph, g, [("x", g["x1"], "sum", 2)], [("x2", g["x2"], x2, "y2", 4), ("h", g["h6"], h, "out", 7)],
                  ("turned", "copied", "product", "sum", "y", "std", "x2", "y2", "std2", "z", "out"))
        xb, cb = n.in_bufs["x"], n.pieces
        small = ph.sb("small", [P, SLOTS, 2, GT])
        y, z = (ph.sb(k, [P, SLOTS, GT, D]) for k in ("y", "z"))
        aT = ph.sb("aT", [P, SLOTS, 2 * GT * P])
        std, rstd = (ph.sb(k, [P, SLOTS, 2, GT]) for k in ("std", "rstd"))
        st = ph.sb("st", [P, SLOTS, GT, 6])
        mv = ph.sb("mv", [P, SLOTS, 2, GT, 2])
        pa = [ph.ps(f"pa{k}", [P, 2 * GT * P]) for k in range(2)]
        po = [ph.ps(f"po{k}", [P, GT, D]) for k in range(2)]
        with nc.Block() as block:
            @block.sync
            def _(sp):
                n.traffic(sp)

            @block.gpsimd
            def _(pool):
                n.gather(pool)

            @block.tensor
            def _(pe):
                n.start(pe, "turned", "product")

                def transposes(m, s, k):
                    n.need_pieces(pe, k, s)
                    n.need(pe, "copied", m, back=2)
                    n.done(turn(pe, pa[s % 2], cb[:, s], g["ident"]), "turned")

                def products(m, s, k):
                    n.need(pe, "copied", m)
                    n.need(pe, "sum", m, back=2)
                    n.done(times(pe, po[s % 2], aT[:, s], g["w1T"], 0, D), "product")
                in_turn(pe, [(0, transposes), (1, products)])

            @block.scalar
            def _(act):
                n.start(act, "copied", "std", "std2", "out")
                def copies(m, s, k):
                    n.need(act, "turned", m)
                    n.need(act, "product", m, back=SLOTS)
                    n.done(act.activation(aT[:, s, :], pa[s % 2][:], ACT.Copy), "copied")

                def stds(c, signal, before):
                    def f(m, s, k):
                        n.need(act, before, m)
                        n.need(act, "z", m, back=SLOTS)
                        n.done(act.activation(std[:, s, c, :], mv[:, s, c, :, 1], ACT.Sqrt, bias=g["eps"][:]), signal)
                    return f

                def scales(m, s, k):
                    n.need(act, "z", m)
                    n.need_stored(act, "h", k, s)
                    for j in range(GT):
                        last = act.activation(h[:, s, j, :], z[:, s, j, :], ACT.Copy,
                                              scale=g["dis"][:, bass.ds(m * GT + j, 1)])
                    n.done(last, "out")
                in_turn(act, [(0, copies), (3, stds(0, "std", "y")), (5, stds(1, "std2", "y2")), (7, scales)])

            @block.vector
            def _(dve):
                n.start(dve, "sum", "y", "x2", "y2", "z")
                n.first_indices(dve)
                steps = Steps(dve, n.step)

                def invs(m, s, k):
                    n.need_pieces(dve, k, s)
                    mark = steps.mark(dve.tensor_scalar(small[:, s, 0, :], cb[:, s, :, D], 0.5, None, ALU.max))
                    yield
                    steps.wait(mark)
                    steps.mark(dve.reciprocal(small[:, s, 1, :], small[:, s, 0, :]))

                def indices(m, s, k):
                    n.need(dve, "turned", m)
                    n.next_indices(dve, m, s)

                def ys(m, s, k):
                    n.need(dve, "product", m)
                    n.need_load(dve, "x", k, s)
                    for j in range(GT):
                        last = dve.scalar_tensor_tensor(y[:, s, j, :], po[s % 2][:, j, :], small[:, s, 1, j:j + 1], xb[:, s, j, :],
                                                        ALU.mult, ALU.add)
                    n.done(last, "sum")
                    yield
                    n.need(dve, "sum", m)
                    yield from stats(dve, steps, y[:, s], st[:, s], mv[:, s, 0], n, "y")

                def x2s(m, s, k):
                    n.need(dve, "std", m)
                    n.need_stored(dve, "x2", k, s)
                    yield from normalise(dve, steps, x2[:, s], y[:, s], mv[:, s, 0], std[:, s, 0, :], rstd[:, s, 0],
                                         lambda ins: n.done(ins, "x2"))
                    yield
                    n.need(dve, "x2", m)
                    yield from stats(dve, steps, x2[:, s], st[:, s], mv[:, s, 1], n, "y2")

                def zs(m, s, k):
                    n.need(dve, "std2", m)
                    n.need(dve, "out", m, back=SLOTS)
                    yield from affine(dve, steps, n, z[:, s], x2[:, s], mv[:, s, 1], std[:, s, 1, :], rstd[:, s, 1], g["ln6g"], g["ln6b"])
                in_turn(dve, [(6, zs), (4, x2s), (2, ys), (1, indices), (0, invs)], steps, links=7)

def gcn_nodes(nc, g, last):
    with Phase(nc) as ph:
        w, bias = (g["w7T"], g["b7"]) if last else (g["w6T"], g["b6"])
        o1, o2 = ph.sb("o1", [P, SLOTS, GT, D]), ph.sb("o2", [P, SLOTS, GT, D])
        sc = ph.sb("sc", [P, SLOTS, GT, SCORES])
        if last:
            loads = [("h", g["h7"], "agg", 0), ("x", g["y6"], "y", 3), ("x2", g["x2"], "v", 6)]
            stores = [("o1", g["x3"], o1, "x3", 8), ("o2", g["p1"], o2, "out", 11), ("sc", g["scores"], sc, "out", 11)]
        else:
            loads = [("h", g["h6"], "agg", 0), ("x", g["x2"], "y", 3)]
            stores = [("o1", g["y6"], o1, "y", 3), ("o2", g["h7"], o2, "out", 6)]
        n = Nodes(nc, ph, g, loads, stores,
                  ("agg", "turned", "copied", "product", "y", "turned2", "copied2", "product2", "v", "std", "z", "x3",
                   "turned3", "copied3", "product3", "out"))
        hb, xb, cb = n.in_bufs["h"], n.in_bufs["x"], n.pieces
        agg, t = (ph.sb(k, [P, SLOTS, GT, D]) for k in ("agg", "t"))
        y = ph.sb("y", [P, SLOTS, GT, D]) if last else o1
        z = ph.sb("z", [P, SLOTS, GT, D])
        aT = ph.sb("aT", [P, SLOTS, 2 * GT * P])
        yT, xT = ((ph.sb(k, [P, SLOTS, 2 * GT * P]) for k in ("yT", "xT")) if last else (None, None))
        std, rstd = (ph.sb(k, [P, SLOTS, GT]) for k in ("std", "rstd"))
        st = ph.sb("st", [P, SLOTS, GT, 6])
        mv = ph.sb("mv", [P, SLOTS, GT, 2])
        pa = ph.ps("pa", [P, 2 * GT * P])
        po = [ph.ps(f"po{k}", [P, GT, D]) for k in range(2)]
        if last:
            py, po2, px, po3 = ph.ps("py", [P, 2 * GT * P]), ph.ps("po2", [P, GT, D]), ph.ps("px", [P, 2 * GT * P]), ph.ps("po3", [P, GT, D])
            psc = ph.ps("psc", [P, GT, SCORES])
        with nc.Block() as block:
            @block.sync
            def _(sp):
                n.traffic(sp)

            @block.gpsimd
            def _(pool):
                n.gather(pool)

            @block.tensor
            def _(pe):
                n.start(pe, "turned", "product", "turned2", "product2", "turned3", "product3")
                def transposes(m, s, k):
                    n.need(pe, "copied", m, back=1)
                    n.need(pe, "agg", m)
                    n.done(turn(pe, pa, agg[:, s], g["ident"]), "turned")

                def products(m, s, k):
                    n.need(pe, "copied", m)
                    n.need(pe, "y", m, back=2)
                    n.done(times(pe, po[s % 2], aT[:, s], w, 0, D), "product")

                def transposes2(m, s, k):
                    n.need(pe, "copied2", m, back=1)
                    n.need(pe, "y", m)
                    n.done(turn(pe, py, y[:, s], g["ident"]), "turned2")

                def products2(m, s, k):
                    n.need(pe, "copied2", m)
                    n.need(pe, "v", m, back=1)
                    for j in range(GT):
                        pe.matmul(po2[:, j, :], g["ones3"][:], g["bp"][:], start=True, stop=False)
                        for c in range(2):
                            ins = pe.matmul(po2[:, j, :], yT[:, s, (c * GT + j) * P:(c * GT + j + 1) * P], g["wpT"][:, c, :],
                                            start=False, stop=(c == 1))
                    n.done(ins, "product2")

                def transposes3(m, s, k):
                    n.need(pe, "copied3", m, back=1)
                    n.need(pe, "x3", m)
                    n.done(turn(pe, px, o1[:, s], g["ident"]), "turned3")

                def products3(m, s, k):
                    n.need(pe, "copied3", m)
                    n.need(pe, "out", m, back=1)
                    times(pe, po3, xT[:, s], g["g1w"], 0, D)
                    n.done(times(pe, psc, xT[:, s], g["g1w"], D, CW), "product3")
                in_turn(pe, [(1, transposes), (2, products)] +
                        ([(4, transposes2), (5, products2), (9, transposes3), (10, products3)] if last else []))

            @block.scalar
            def _(act):
                n.start(act, "copied", "copied2", "copied3", "std", "out")
                def copies(m, s, k):
                    n.need(act, "turned", m)
                    n.need(act, "product", m, back=SLOTS)
                    n.done(act.activation(aT[:, s, :], pa[:], ACT.Copy), "copied")

                def copies2(m, s, k):
                    n.need(act, "turned2", m)
                    n.need(act, "product2", m, back=SLOTS)
                    n.done(act.activation(yT[:, s, :], py[:], ACT.Copy), "copied2")

                def copies3(m, s, k):
                    n.need(act, "turned3", m)
                    n.need(act, "product3", m, back=SLOTS)
                    n.done(act.activation(xT[:, s, :], px[:], ACT.Copy), "copied3")

                def stds(m, s, k):
                    n.need(act, "v" if last else "y", m)
                    n.need(act, "x3" if last else "z", m, back=SLOTS)
                    n.done(act.activation(std[:, s, :], mv[:, s, :, 1], ACT.Sqrt, bias=g["eps"][:]), "std")

                def scales(m, s, k):
                    n.need(act, "z", m)
                    n.need_stored(act, "o2", k, s)
                    for j in range(GT):
                        ins = act.activation(o2[:, s, j, :], z[:, s, j, :], ACT.Copy,
                                             scale=g["dis"][:, bass.ds(m * GT + j, 1)])
                    n.done(ins, "out")

                def rows(m, s, k):
                    n.need(act, "product3", m)
                    n.need_stored(act, "o2", k, s)
                    n.need_stored(act, "sc", k, s)
                    act.activation(o2[:, s], po3[:], ACT.Copy)
                    n.done(act.activation(sc[:, s], psc[:], ACT.Copy), "out")
                if last:
                    in_turn(act, [(1, copies), (11, rows), (4, copies2), (7, stds), (9, copies3)])
                else:
                    in_turn(act, [(1, copies), (4, stds), (6, scales)])

            @block.vector
            def _(dve):
                n.start(dve, "agg", "y", "v", "z", "x3")
                n.first_indices(dve)
                steps = Steps(dve, n.step)

                def aggs(m, s, k):
                    n.need_pieces(dve, k, s)
                    n.need_load(dve, "h", k, s)
                    n.need(dve, "turned", m, back=SLOTS)
                    n.done(dve.tensor_tensor(agg[:, s], cb[:, s, :, 0:D], hb[:, s], ALU.add), "agg")
                    n.next_indices(dve, m, s)

                def ys(m, s, k):
                    n.need(dve, "product", m)
                    n.need_load(dve, "x", k, s)
                    if last:
                        n.need(dve, "turned2", m, back=SLOTS)
                    else:
                        n.need_stored(dve, "o1", k, s)
                    for j in range(GT):
                        ins = dve.scalar_tensor_tensor(t[:, s, j, :], po[s % 2][:, j, :], g["dis"][:, bass.ds(m * GT + j, 1)],
                                                       bias[:], ALU.mult, ALU.add)
                    mark = steps.mark(ins)
                    yield
                    steps.wait(mark)
                    ins = dve.scalar_tensor_tensor(y[:, s], t[:, s], 0.0, xb[:, s], ALU.max, ALU.add)
                    if last:
                        n.done(ins, "y")
                    else:
                        mark = steps.mark(ins)
                        yield
                        steps.wait(mark)
                        yield from stats(dve, steps, y[:, s], st[:, s], mv[:, s], n, "y")

                def zs(m, s, k):
                    n.need(dve, "std", m)
                    n.need(dve, "out", m, back=SLOTS)
                    yield from affine(dve, steps, n, z[:, s], y[:, s], mv[:, s], std[:, s, :], rstd[:, s], g["ln7g"], g["ln7b"])

                def vs(m, s, k):
                    n.need(dve, "product2", m)
                    n.need_load(dve, "x2", k, s)
                    mark = steps.mark(dve.tensor_tensor(z[:, s], po2[:], n.in_bufs["x2"][:, s], ALU.add))
                    yield
                    steps.wait(mark)
                    yield from stats(dve, steps, z[:, s], st[:, s], mv[:, s], n, "v")

                def x3s(m, s, k):
                    n.need(dve, "std", m)
                    n.need_stored(dve, "o1", k, s)
                    n.need(dve, "turned3", m, back=SLOTS)
                    yield from normalise(dve, steps, o1[:, s], z[:, s], mv[:, s], std[:, s, :], rstd[:, s],
                                         lambda ins: n.done(ins, "x3"))
                if last:
                    in_turn(dve, [(8, x3s), (6, vs), (3, ys), (0, aggs)], steps, links=4)
                else:
                    in_turn(dve, [(5, zs), (3, ys), (0, aggs)], steps, links=5)

def gat_nodes(nc, g, last, out):
    with Phase(nc) as ph:
        bias = g["gb2"] if last else g["gb1"]
        o = ph.sb("o", [P, SLOTS, GT, D])
        sc = ph.sb("sc", [P, SLOTS, GT, SCORES])
        if last:
            loads, stores = [("p", g["p2"], "low", 0), ("x3", g["x3"], "sum", 2)], [("o", out, o, "out", 4)]
        else:
            loads, stores = [("p", g["p1"], "low", 0)], [("o", g["p2"], o, "out", 5), ("sc", g["scores"], sc, "out", 5)]
        n = Nodes(nc, ph, g, loads, stores,
                  ("low", "ex", "v", "sum", "turned", "copied", "product", "y", "std", "out"))
        pb, cb = n.in_bufs["p"], n.pieces
        rden = ph.sb("rden", [P, SLOTS, GT, HEADS])
        y = ph.sb("y", [P, SLOTS, GT, D])
        u, low, v = (ph.sb(k, [P, SLOTS, GT, D]) for k in ("u", "low", "v"))
        vT = ph.sb("vT", [P, SLOTS, 2 * GT * P])
        minus = ph.sb("minus", [P, 1])
        std, rstd = (ph.sb(k, [P, SLOTS, GT]) for k in ("std", "rstd"))
        st = ph.sb("st", [P, SLOTS, GT, 6])
        mv = ph.sb("mv", [P, SLOTS, GT, 2])
        pv = [ph.ps(f"pv{k}", [P, 2 * GT * P]) for k in range(2)]
        po = [ph.ps(f"po{k}", [P, GT, D]) for k in range(2)]
        psc = [ph.ps(f"psc{k}", [P, GT, SCORES]) for k in range(2)]
        minus_ready = ph.sem("minus_ready")

        def heads(x):
            return x.rearrange("p j (h c) -> p j h c", h=HEADS)

        def per_head(x):
            return x.unsqueeze(3).to_broadcast([P, GT, HEADS, HID])
        with nc.Block() as block:
            @block.sync
            def _(sp):
                n.traffic(sp)

            @block.gpsimd
            def _(pool):
                n.gather(pool)

            @block.tensor
            def _(pe):
                n.start(pe, "turned", "product")
                if not last:
                    def transposes(m, s, k):
                        n.need(pe, "copied", m, back=2)
                        n.need(pe, "v", m)
                        n.done(turn(pe, pv[s % 2], v[:, s], g["ident"]), "turned")

                    def products(m, s, k):
                        n.need(pe, "copied", m)
                        n.need(pe, "out", m, back=2)
                        times(pe, po[s % 2], vT[:, s], g["g2w"], 0, D)
                        n.done(times(pe, psc[s % 2], vT[:, s], g["g2w"], D, CW), "product")
                    in_turn(pe, [(3, transposes), (4, products)])

            @block.scalar
            def _(act):
                n.start(act, "ex", "copied", "std")
                if not last:
                    n.start(act, "out")
                    act.wait_ge(minus_ready, 1)
                def exps(m, s, k):
                    n.need(act, "low", m)
                    n.done(act.activation(low[:, s], low[:, s], ACT.Exp), "ex")

                def copies(m, s, k):
                    n.need(act, "turned", m)
                    n.need(act, "product", m, back=SLOTS)
                    n.done(act.activation(vT[:, s, :], pv[s % 2][:], ACT.Identity, bias=minus[:]), "copied")

                def rows(m, s, k):
                    n.need(act, "product", m)
                    n.need_stored(act, "o", k, s)
                    n.need_stored(act, "sc", k, s)
                    act.activation(o[:, s], po[s % 2][:], ACT.Copy)
                    n.done(act.activation(sc[:, s], psc[s % 2][:], ACT.Copy), "out")

                def stds(m, s, k):
                    n.need(act, "y", m)
                    n.need(act, "out", m, back=SLOTS)
                    n.done(act.activation(std[:, s, :], mv[:, s, :, 1], ACT.Sqrt, bias=g["eps"][:]), "std")
                if last:
                    in_turn(act, [(3, stds), (1, exps)])
                else:
                    in_turn(act, [(3, copies), (5, rows), (1, exps)])

            @block.vector
            def _(dve):
                n.start(dve, "low", "v", "sum", "y")
                if last:
                    n.start(dve, "out")
                dve.memset(minus[:], -1.0).then_inc(minus_ready, 1)
                n.first_indices(dve)
                steps = Steps(dve, n.step)

                def lows(m, s, k):
                    n.need_pieces(dve, k, s)
                    n.need_load(dve, "p", k, s)
                    dve.reciprocal(rden[:, s], cb[:, s, :, D:D + HEADS])
                    mark = steps.mark(dve.tensor_tensor(heads(u[:, s]), heads(pb[:, s]), per_head(cb[:, s, :, D + HEADS:CW]), ALU.mult))
                    yield
                    steps.wait(mark)
                    mark = steps.mark(dve.tensor_tensor(u[:, s], u[:, s], cb[:, s, :, 0:D], ALU.add))
                    n.next_indices(dve, m, s)
                    yield
                    steps.wait(mark)
                    mark = steps.mark(dve.tensor_tensor(heads(u[:, s]), heads(u[:, s]), per_head(rden[:, s]), ALU.mult))
                    yield
                    steps.wait(mark)
                    mark = steps.mark(dve.tensor_tensor(u[:, s], u[:, s], bias[:], ALU.add))
                    yield
                    steps.wait(mark)
                    n.done(dve.tensor_scalar(low[:, s], u[:, s], 0.0, None, ALU.min), "low")

                def vs(m, s, k):
                    n.need(dve, "ex", m)
                    if not last:
                        n.need(dve, "turned", m, back=SLOTS)
                    ins = dve.scalar_tensor_tensor(v[:, s], u[:, s], 0.0, low[:, s], ALU.max, ALU.add)
                    if not last:
                        n.done(ins, "v")
                        return
                    n.need_load(dve, "x3", k, s)
                    mark = steps.mark(ins)
                    yield
                    steps.wait(mark)
                    n.done(dve.scalar_tensor_tensor(y[:, s], v[:, s], -1.0, n.in_bufs["x3"][:, s], ALU.add, ALU.add), "sum")
                    yield
                    n.need(dve, "sum", m)
                    yield from stats(dve, steps, y[:, s], st[:, s], mv[:, s], n, "y")

                def outs(m, s, k):
                    n.need(dve, "std", m)
                    n.need_stored(dve, "o", k, s)
                    yield from normalise(dve, steps, o[:, s], y[:, s], mv[:, s], std[:, s, :], rstd[:, s],
                                         lambda ins: n.done(ins, "out"))
                in_turn(dve, ([(4, outs)] if last else []) + [(2, vs), (0, lows)], steps, links=7 if last else 4)

_INS = ["x", "src", "dst", "edge_attr_64", "edge_weight", "L0_gnn_W", "L0_gnn_b", "L1_gnn_W", "L1_gnn_A", "L2_gnn_ln6_g",
        "L2_gnn_ln6_b", "L2_gnn_W6", "L2_gnn_b6", "L2_gnn_ln7_g", "L2_gnn_ln7_b", "L2_gnn_W7", "L2_gnn_b7", "L2_gnn_Wp",
        "L2_gnn_bp", "L3_gnn_W1", "L3_gnn_att_src1", "L3_gnn_att_dst1", "L3_gnn_b1", "L3_gnn_W2", "L3_gnn_att_src2",
        "L3_gnn_att_dst2", "L3_gnn_b2"]
_OUTS = [((50000, 256), "float32")]


def kernel(**inputs):
    import numpy as _np
    import concourse.bacc as _bacc
    from concourse import mybir as _mybir
    from concourse.bass_utils import run_bass_kernel_spmd as _run

    nc = _bacc.Bacc("TRN2", target_bir_lowering=False, num_devices=1)
    arrays, args = {}, {}
    for name in _INS:
        a = _np.ascontiguousarray(inputs[name])
        arrays[f"in_{name}_dram"] = a
        args[name] = nc.dram_tensor(f"in_{name}_dram", a.shape, _mybir.dt.from_np(a.dtype), kind="ExternalInput").ap()
    shape, dtype = _OUTS[0]
    out = nc.dram_tensor("out_0_dram", shape, _mybir.dt.from_np(_np.dtype(dtype)), kind="ExternalOutput").ap()
    build(nc, args, out)
    r = _run(nc, [arrays], core_ids=[0])
    return r.results[0]["out_0_dram"]
```

```python
from contextlib import ExitStack

import concourse.bass as bass
from concourse import mybir

F32 = mybir.dt.float32
BF16 = mybir.dt.bfloat16
I32 = mybir.dt.int32
ALU = mybir.AluOpType
ACT = mybir.ActivationFunctionType
AX = mybir.AxisListType

P = 128
D = 256
N = 50000
E = 25000
EDIM = 64
HEADS = 4
HID = D // HEADS

CREDIT = 16
SLOTS = 4
GT = 2
GROUP = GT * P
NGROUPS = -(-N // (GROUP * SLOTS)) * SLOTS
NPAD = NGROUPS * GROUP
NTILES = NPAD // P
NITER = NGROUPS // SLOTS

ETILES = -(-E // (2 * P)) * 2
EPAD = ETILES * P
EROWS = ETILES // 2
HALF = 7
EITER = ETILES // (2 * HALF)
assert EITER * 2 * HALF == ETILES and EROWS <= P and NTILES == 4 * EROWS

SCORES = 2 * HEADS
CW = D + SCORES
NO_EDGES = EPAD
BIG = 1e30
FAR = 1000000
PAD_NODE = 60000
LN_EPS = 1e-5
BANK = 512


def build(nc, a, out):
    ctx = ExitStack()
    with ctx:
        def sb(name, shape, dt=F32):
            return ctx.enter_context(nc.sbuf_tensor(name, shape, dt))

        def dram(name, shape, dt=F32):
            return nc.dram_tensor(name, shape, dt).ap()

        g = {}
        for name in ("x1", "x2", "y6", "x3", "p1", "p2"):
            g[name] = dram("t_" + name, [NPAD, D])
        for name in ("h6", "h7"):
            g[name] = dram("t_" + name, [NPAD, CW])
        g["scores"] = dram("t_scores", [NPAD, SCORES])
        g["pieces"] = dram("t_pieces", [EPAD + 1, CW])
        g["piece_of"] = dram("t_piece_of", [NPAD, 2], I32)
        g["firsts"] = dram("t_firsts", [EPAD, SCORES])
        g["credit"] = dram("t_credit", [P, 32 * 8])

        for name, shape in (("ident", [P, P]), ("iota", [P, P]), ("eps", [P, 1]), ("zero", [P, 8]),
                            ("w0", [P, 4, D]), ("w1T", [P, 2, D]), ("w6T", [P, 2, D]), ("w7T", [P, 2, D]),
                            ("wpT", [P, 2, D]), ("g1w", [P, 2, CW]), ("g2w", [P, 2, CW]),
                            ("vsrc", [P, D]), ("vdst", [P, D]),
                            ("c6", [P, D]), ("c7", [P, D]),
                            ("b6", [P, D]), ("b7", [P, D]), ("gb1", [P, GT, D]), ("gb2", [P, GT, D]),
                            ("rank", [P, ETILES]), ("first", [P, ETILES]), ("ew", [P, ETILES]), ("ee", [P, ETILES]),
                            ("startR", [EROWS, 2 * P]), ("endR", [EROWS, 2 * P]),
                            ("startrow", [HEADS, EROWS]), ("endrow", [HEADS, EROWS]),
                            ("insideR", [EROWS, 2 * P]), ("insiderow", [SCORES, EROWS]),
                            ("same", [EROWS, 2, 2, EROWS]),
                            ("dis", [P, NTILES])):
            g[name] = sb(name, shape)
        g["ones3"] = sb("ones3", [3, P], BF16)
        g["b0"] = sb("b0", [3, D], BF16)
        g["bp"] = sb("bp", [3, D], BF16)
        g["src"] = sb("srcs", [P, ETILES + 2 * HALF], I32)
        g["dst"] = sb("dsts", [P, ETILES + 2 * HALF], I32)
        g["piece"] = sb("piece", [P, NTILES + GT * SLOTS], I32)
        g["slot"] = sb("slot", [P, NTILES], I32)
        g["target"] = sb("target", [EROWS, 2, 2], I32)
        g["exs"] = sb("exs", [P, ETILES, HEADS])
        g["exd"] = sb("exd", [P, ETILES, SCORES])

        weights(nc, a, g)
        edge_tables(nc, a, g)
        edge_pass(nc, g, "count", a["x"], 0)
        sage_nodes(nc, g, a["x"])
        edge_scores(nc, g, 1)
        edge_pass(nc, g, "attention", g["x1"], 1)
        attention_nodes(nc, g)
        edge_pass(nc, g, "gcn", g["h6"], 0)
        gcn_nodes(nc, g, last=False)
        edge_pass(nc, g, "gcn", g["h7"], 0)
        gcn_nodes(nc, g, last=True)
        edge_scores(nc, g, HEADS)
        edge_pass(nc, g, "gat", g["p1"], SCORES)
        gat_nodes(nc, g, last=False, out=None)
        edge_scores(nc, g, HEADS)
        edge_pass(nc, g, "gat", g["p2"], SCORES)
        gat_nodes(nc, g, last=True, out=out)


PHASE = [0]


class Phase:

    def __init__(self, nc):
        self.nc = nc
        self.ctx = ExitStack()
        self.sems = []
        PHASE[0] += 1
        self.tag = f"_{PHASE[0]}"

    def __enter__(self):
        self.ctx.__enter__()
        return self

    def __exit__(self, *e):
        self.nc.clear_and_free_semaphores(self.sems)
        self.nc.all_engine_barrier()
        return self.ctx.__exit__(*e)

    def sb(self, name, shape, dt=F32):
        return self.ctx.enter_context(self.nc.sbuf_tensor(name + self.tag, shape, dt))

    def ps(self, name, shape, dt=F32):
        return self.ctx.enter_context(self.nc.psum_tensor(name + self.tag, shape, dt))

    def sem(self, name):
        s = self.nc.alloc_semaphore(name + self.tag)
        self.sems.append(s)
        return s


def chain(eng, sem):
    n = [0]

    def link(ins):
        n[0] += 1
        ins.then_inc(sem, 1)
        eng.wait_ge(sem, n[0])
    return link


def weights(nc, a, g):
    with Phase(nc) as ph:
        raw = {k: ph.sb("raw_" + k, [P, 2, D]) for k in ("w1", "w6", "w7", "wp")}
        acol = ph.sb("acol", [P, 2, 2])
        lncol = ph.sb("lncol", [P, 4, 2])
        brow = ph.sb("brow", [P, 2, 2, P])
        arow = ph.sb("arow", [P, 2, 2, P])
        att = ph.sb("att", [P, 4, D])
        prod = ph.sb("prod", [P, 2, 4, D])
        bias = ph.sb("bias", [1, 2, D])
        parts = ph.sb("parts", [1, 2, 3, D], BF16)
        rest = ph.sb("rest", [1, 2, 2, D])
        pt = [ph.ps(f"pt{k}", [P, 2 * D]) for k in range(4)]
        pv = ph.ps("pv", [P, 2, D])
        pb = ph.ps("pb", [P, 2, D])
        loaded, zeroed, done, transposed, vecs = (ph.sem(n) for n in ("loaded", "zeroed", "done", "transposed", "vecs"))
        moved, split = ph.sem("moved"), ph.sem("split")
        names = (("w1", "L1_gnn_W", "w1T"), ("w6", "L2_gnn_W6", "w6T"), ("w7", "L2_gnn_W7", "w7T"), ("wp", "L2_gnn_Wp", "wpT"))
        loads = [0]
        with nc.Block() as block:
            @block.sync
            def _(sp):
                def load(o, i):
                    sp.dma_start(o, i).then_inc(loaded, 16)
                    loads[0] += 1
                for k, name, _ in names:
                    load(raw[k][:], a[name].rearrange("(c p) k -> p c k", p=P))
                load(g["w0"][:], a["L0_gnn_W"].rearrange("(c p) k -> p c k", p=P))
                load(g["g1w"][:, :, 0:D], a["L3_gnn_W1"].rearrange("(c p) k -> p c k", p=P))
                load(g["g2w"][:, :, 0:D], a["L3_gnn_W2"].rearrange("(c p) k -> p c k", p=P))
                with nc.allow_non_contiguous_dma(reason="1536 scattered words, once"):
                    for k in range(2):
                        for c in range(2):
                            load(acol[:, k, c:c + 1], a["L1_gnn_A"][0:1, k * D + c * P:k * D + (c + 1) * P].rearrange("a p -> p a"))
                    for k, name in enumerate(("ln6_g", "ln7_g", "ln6_b", "ln7_b")):
                        load(lncol[:, k, :], a["L2_gnn_" + name].rearrange("(c p) -> p c", p=P))
                for k, name in enumerate(("L3_gnn_att_src1", "L3_gnn_att_dst1", "L3_gnn_att_src2", "L3_gnn_att_dst2")):
                    load(att[:, k, :], a[name].rearrange("(a h) c -> a (h c)", a=1).to_broadcast([P, D]))
                for k, name in (("gb1", "L3_gnn_b1"), ("gb2", "L3_gnn_b2")):
                    for j in range(GT):
                        load(g[k][:, j, :], a[name].rearrange("(a c) -> a c", a=1).to_broadcast([P, D]))
                for k, name in (("b6", "L2_gnn_b6"), ("b7", "L2_gnn_b7")):
                    load(g[k][:], a[name].rearrange("(a c) -> a c", a=1).to_broadcast([P, D]))
                for k, name in enumerate(("L0_gnn_b", "L2_gnn_bp")):
                    load(bias[:, k, :], a[name].rearrange("(a c) -> a c", a=1))
                sp.wait_ge(split, 1)
                for k, name in enumerate(("b0", "bp")):
                    for part in range(3):
                        sp.dma_start(g[name][part:part + 1, :], parts[:, k, part, :]).then_inc(moved, 16)
                sp.wait_ge(moved, 6 * 16)

            @block.gpsimd
            def _(pool):
                pool.memset(g["ident"][:], 0.0).then_inc(zeroed, 1)
                pool.wait_ge(zeroed, 1)
                pool.affine_select(out=g["ident"][:], in_=g["ident"][:], compare_op=ALU.not_equal, fill=1.0, base=0,
                                   pattern=[[-1, P]], channel_multiplier=1).then_inc(zeroed, 1)
                pool.iota(g["iota"][:], [[1, P]], base=0, channel_multiplier=0,
                          allow_small_or_imprecise_dtypes=True).then_inc(zeroed, 1)

            @block.tensor
            def _(pe):
                pe.wait_ge(zeroed, 3)
                pe.wait_ge(loaded, 16 * loads[0])
                for n, (k, _, _) in enumerate(names):
                    for ci in range(2):
                        for co in range(2):
                            last = pe.transpose(pt[n][:, ci * D + co * P:ci * D + (co + 1) * P],
                                                raw[k][:, co, ci * P:(ci + 1) * P], g["ident"][:])
                    last.then_inc(transposed, 1)
                pe.wait_ge(vecs, 1)
                for k in range(2):
                    for c in range(2):
                        last = pe.matmul(pv[:, k, :], arow[:, k, c, :], raw["w1"][:, c, :], start=(c == 0), stop=(c == 1))
                last.then_inc(transposed, 1)
                pe.wait_ge(vecs, 2)
                for k, w in enumerate(("w6T", "w7T")):
                    for c in range(2):
                        last = pe.matmul(pb[:, k, :], brow[:, k, c, :], g[w][:, c, :], start=(c == 0), stop=(c == 1))
                last.then_inc(transposed, 1)

            @block.vector
            def _(dve):
                link = chain(dve, done)
                dve.memset(g["eps"][:], LN_EPS)
                dve.memset(brow[:], 1.0)
                dve.memset(g["ones3"][:], 1.0)
                dve.memset(g["zero"][:], 0.0)
                link(dve.memset(arow[:], 1.0))
                dve.wait_ge(loaded, 16 * loads[0])
                for k in range(2):
                    for c in range(2):
                        last = dve.tensor_scalar(arow[:, k, c, :], arow[:, k, c, :], acol[:, k, c:c + 1], None, ALU.mult)
                last.then_inc(vecs, 1)
                for k in range(2):
                    for c in range(2):
                        last = dve.tensor_scalar(brow[:, k, c, :], brow[:, k, c, :], lncol[:, 2 + k, c:c + 1], None, ALU.mult)
                link(last)
                for w, base in ((g["g1w"], 0), (g["g2w"], 2)):
                    for k in range(2):
                        for c in range(2):
                            last = dve.tensor_tensor(prod[:, c, base + k, :], w[:, c, 0:D], att[:, base + k, :], ALU.mult)
                link(last)
                for w, base in ((g["g1w"], 0), (g["g2w"], 2)):
                    for k in range(2):
                        for c in range(2):
                            last = dve.tensor_reduce(w[:, c, D + k * HEADS:D + (k + 1) * HEADS],
                                                     prod[:, c, base + k, :].rearrange("p (h c) -> p h c", h=HEADS),
                                                     AX.X, ALU.add)
                link(last)
                link(dve.tensor_copy(parts[:, :, 0, :], bias[:]))
                link(dve.tensor_tensor(rest[:, :, 0, :], bias[:], parts[:, :, 0, :], ALU.subtract))
                link(dve.tensor_copy(parts[:, :, 1, :], rest[:, :, 0, :]))
                link(dve.tensor_tensor(rest[:, :, 1, :], rest[:, :, 0, :], parts[:, :, 1, :], ALU.subtract))
                dve.tensor_copy(parts[:, :, 2, :], rest[:, :, 1, :]).then_inc(split, 1)
                for n, (_, _, k) in enumerate(names):
                    dve.wait_ge(transposed, n + 1)
                    dve.tensor_copy(g[k][:], pt[n][:].rearrange("p (c k) -> p c k", c=2))
                dve.wait_ge(transposed, len(names) + 1)
                dve.tensor_copy(g["vsrc"][:], pv[:, 0, :])
                dve.tensor_copy(g["vdst"][:], pv[:, 1, :]).then_inc(vecs, 1)
                dve.wait_ge(transposed, len(names) + 2)
                for k, (c, w) in enumerate((("c6", "w6T"), ("c7", "w7T"))):
                    dve.tensor_copy(g[c][:], pb[:, k, :])
                    for i in range(2):
                        last = dve.tensor_scalar(g[w][:, i, :], g[w][:, i, :], lncol[:, k, i:i + 1], None, ALU.mult)
                link(last)


def edge_tables(nc, a, g):
    full = E // (2 * P)
    tail = E - full * 2 * P
    with Phase(nc) as ph:
        names = ("src", "dst", "prev", "next")
        ints = {k: ph.sb("i_" + k, [EROWS, 2 * P], I32) for k in names}
        rows = {k: ph.sb("r_" + k, [EROWS, 2 * P]) for k in names}
        ewR = ph.sb("ewR", [EROWS, 2 * P])
        before = ph.sb("before", [EROWS, 2], I32)
        beforef = ph.sb("beforef", [EROWS, 2])
        first, lastf, tstart, rank, ones = (ph.sb(n, [EROWS, 2 * P]) for n in ("firstR", "lastR", "tstart", "rankR", "onesR"))
        anyf = ph.sb("anyf", [EROWS, 3, SCORES])
        anyone = ph.sb("anyone", [EROWS, 2])
        cont, key, rep, node0 = (ph.sb(n, [EROWS, 2]) for n in ("cont", "key", "rep", "node0"))
        idx0 = ph.sb("idx0", [EROWS, 2], I32)
        diag = ph.sb("diag", [EROWS, 2, EROWS])
        fdst = ph.sb("fdst", [P, ETILES], I32)
        rowid = ph.sb("rowid", [P, ETILES], I32)
        rowf = ph.sb("rowf", [P, ETILES])
        tbase = ph.sb("tbase", [P, ETILES])
        attr = [ph.sb(f"attr{k}", [P, ETILES // 4, EDIM]) for k in range(2)]
        aerow = ph.sb("aerow", [P, EDIM])
        idx = ph.sb("idxs", [P, 2 * HALF], I32)
        val = ph.sb("vals", [P, 2 * HALF, 2], I32)
        fill = ph.sb("fill", [EROWS, 4 * P, 2], I32)
        zeros = ph.sb("zeros", [EROWS, 2 * P * SCORES])
        edgeid = ph.sb("edgeid", [P, ETILES], I32)
        pieceR = ph.sb("pieceR", [EROWS, 4 * P, 2], I32)
        pieceF = ph.sb("pieceF", [EROWS, 2, 4 * P])
        pc = [ph.ps(f"pc{k}", [P, 512]) for k in range(5)]
        prow = ph.ps("prow", [P, 2, P])
        pany = ph.ps("pany", [P, 3, P])
        (ready, loaded, done, turned, filled, idxed, told, read, ptrs, attrd, bases) = (
            ph.sem(n) for n in ("ready", "loaded", "done", "turned", "filled", "idxed", "told", "read",
                                "ptrs", "attrd", "bases"))
        passed = ph.sem("passed")
        attrs = [ph.sem(f"attrs{k}") for k in range(4)]
        scattered = [ph.sem(f"scattered{h}") for h in range(2)]
        q4 = ETILES // 4
        nloads = [0]
        with nc.Block() as block:
            @block.sync
            def _(sp):
                sp.wait_ge(ready, 1)
                nloads[0] = 0

                def load(o, i):
                    sp.dma_start(o, i).then_inc(loaded, 16)
                    nloads[0] += 1
                flat = {"src": a["src"], "dst": a["dst"], "prev": a["dst"], "next": a["dst"]}

                def rowsof(k, lo, n):
                    return flat[k][lo:lo + n * 2 * P].rearrange("(q i) -> q i", i=2 * P)

                def one(k, lo, n):
                    return flat[k][lo:lo + n].rearrange("(q i) -> q i", q=1)
                for k in ("src", "dst"):
                    load(ints[k][0:full, :], rowsof(k, 0, full))
                    load(ints[k][full:full + 1, 0:tail], one(k, full * 2 * P, tail))
                load(ints["prev"][0:1, 1:2 * P], one("prev", 0, 2 * P - 1))
                load(ints["prev"][1:full, :], rowsof("prev", 2 * P - 1, full - 1))
                load(ints["prev"][full:full + 1, 0:tail + 1], one("prev", full * 2 * P - 1, tail + 1))
                load(ints["next"][0:full, :], rowsof("next", 1, full))
                load(ints["next"][full:full + 1, 0:tail - 1], one("next", full * 2 * P + 1, tail - 1))
                load(ewR[0:full, :], a["edge_weight"][0:full * 2 * P].rearrange("(q i) -> q i", i=2 * P))
                load(ewR[full:full + 1, 0:tail], a["edge_weight"][full * 2 * P:E].rearrange("(q i) -> q i", q=1))
                with nc.allow_non_contiguous_dma(reason="97 words, once"):
                    load(before[1:EROWS, 0:1], rowsof("dst", 0, EROWS - 1)[:, P - 1:P])
                load(aerow[:], a["L1_gnn_A"][0:1, 2 * D:2 * D + EDIM].to_broadcast([P, EDIM]))
                sp.dma_start(g["piece_of"].rearrange("(q i) a -> q i a", q=EROWS), fill[:]).then_inc(filled, 16)
                sp.dma_start(g["firsts"].rearrange("(q i) c -> q (i c)", q=EROWS), zeros[:]).then_inc(filled, 16)
                for k in range(4):
                    lo = k * q4 * P
                    n = min(q4, (E - lo) // P)
                    if k >= 2:
                        sp.wait_ge(attrd, k - 1)
                    if n < q4:
                        sp.dma_start(attr[k % 2][0:E - lo - n * P, n, :], a["edge_attr_64"][lo + n * P:E, :]).then_inc(attrs[k], 16)
                    sp.dma_start(attr[k % 2][:, 0:n, :],
                                 a["edge_attr_64"][lo:lo + n * P, :].rearrange("(t p) c -> p t c", p=P)).then_inc(attrs[k], 16)
                for h in range(2):
                    sp.wait_ge(scattered[h], EITER * HALF * 16)
                sp.dma_start(pieceR[:], g["piece_of"].rearrange("(q i) a -> q i a", q=EROWS)).then_inc(ptrs, 16)

            @block.gpsimd
            def _(pool):
                pool.iota(tbase[:], [[P, ETILES]], base=0, channel_multiplier=0,
                          allow_small_or_imprecise_dtypes=True).then_inc(bases, 1)
                pool.iota(edgeid[:], [[P, ETILES]], base=0, channel_multiplier=1).then_inc(bases, 1)
                pool.wait_ge(filled, 32)
                with pool.Fori(0, EITER) as i:
                    for h in range(2):
                        pool.wait_ge(idxed, 2 * i + h + 1)
                        carry_wait(pool, passed)
                        for j in range(h * HALF, (h + 1) * HALF):
                            pool.indirect_dma_start(g["piece_of"], bass.IndirectOffsetOnAxis(idx[:, j:j + 1], 0),
                                                    val[:, j, :], None, bounds_check=NPAD - 1,
                                                    oob_is_err=False).then_inc(scattered[h], 16)
                for h in range(2):
                    pool.wait_ge(scattered[h], EITER * HALF * 16)
                for h in range(2):
                    pool.indirect_dma_start(g["target"][:, h, :], None, g["piece_of"],
                                            bass.IndirectOffsetOnAxis(idx0[:, h:h + 1], 0), bounds_check=NPAD - 1,
                                            oob_is_err=False).then_inc(told, 16)
                pool.wait_ge(told, 32)

            @block.tensor
            def _(pe):
                pe.wait_ge(turned, 1)
                for k, r in enumerate((rows["src"], rows["dst"], rank, first, ewR)):
                    for h in range(2):
                        last = pe.transpose(pc[k][:, h * P:h * P + EROWS], r[:, h * P:(h + 1) * P], g["ident"][0:EROWS, 0:EROWS])
                last.then_inc(read, 1)
                for k in range(3):
                    last = pe.matmul(pany[0:SCORES, k, 0:EROWS], anyf[:, k, :], g["ident"][0:EROWS, 0:EROWS], start=True, stop=True)
                for h in range(2):
                    last = pe.matmul(prow[0:EROWS, h, 0:EROWS], ones[:, 0:EROWS], diag[:, h, :], start=True, stop=True)
                last.then_inc(read, 1)
                pe.wait_ge(turned, 2)
                for k in range(2):
                    for j in range(4):
                        last = pe.transpose(pc[k][:, j * P:j * P + EROWS], pieceF[:, k, j * P:(j + 1) * P], g["ident"][0:EROWS, 0:EROWS])
                last.then_inc(read, 1)

            @block.vector
            def _(dve):
                link = chain(dve, done)
                for k, v in (("src", 0), ("dst", PAD_NODE), ("prev", PAD_NODE), ("next", -5)):
                    dve.memset(ints[k][:], v)
                dve.memset(before[:], -1)
                dve.memset(ewR[:], 0.0)
                dve.memset(ones[:], 1.0)
                dve.memset(fill[:, :, 0:1], NO_EDGES)
                dve.memset(fill[:, :, 1:2], FAR)
                dve.memset(zeros[:], 0.0)
                dve.memset(g["target"][:], FAR)
                dve.memset(g["src"][:], 0)
                dve.memset(g["dst"][:], 0)
                dve.memset(g["piece"][:], NO_EDGES)
                link(dve.memset(attr[1][:, q4 - 1, :], 0.0))
                dve.memset(ints["prev"][0:1, 0:1], -1).then_inc(ready, 1)
                dve.wait_ge(loaded, 16 * nloads[0])
                for k in names:
                    last = dve.tensor_copy(rows[k][:], ints[k][:])
                link(last)
                link(dve.tensor_copy(beforef[:], before[:]))
                link(dve.tensor_copy(beforef[:, 1:2], rows["prev"][:, 0:1]))
                dve.tensor_tensor(first[:], rows["dst"][:], rows["prev"][:], ALU.not_equal)
                link(dve.tensor_tensor(lastf[:], rows["dst"][:], rows["next"][:], ALU.not_equal))
                link(dve.tensor_copy(tstart[:], first[:]))
                link(dve.memset(tstart[:].rearrange("q (h i) -> q h i", h=2)[:, :, 0:1], 1.0))
                for h in range(2):
                    s = slice(h * P, (h + 1) * P)
                    dve.tensor_tensor_scan(rank[:, s], ones[:, s], tstart[:, s], -1.0, ALU.mult, ALU.add)
                dve.tensor_scalar(g["startR"][:], first[:], -BIG, None, ALU.mult)
                dve.tensor_scalar(g["endR"][:], lastf[:], -BIG, None, ALU.mult)
                dve.tensor_reduce(anyone[:, 0:1], first[:], AX.X, ALU.max)
                link(dve.tensor_reduce(anyone[:, 1:2], lastf[:], AX.X, ALU.max))
                for k in range(2):
                    dve.tensor_scalar(anyf[:, k, :], ones[:, 0:SCORES], anyone[:, k:k + 1], -BIG, ALU.mult, ALU.mult)
                dve.tensor_scalar(anyf[:, 2, :], ones[:, 0:SCORES], anyone[:, 0:1], 1.0, ALU.not_equal, ALU.mult)
                dve.tensor_scalar(g["insideR"][:], first[:], -1.0, 1.0, ALU.mult, ALU.add)
                heads = first[:].rearrange("q (h i) -> q h i", h=2)[:, :, 0]
                dve.tensor_scalar(cont[:], heads, -1.0, 1.0, ALU.mult, ALU.add)
                link(dve.tensor_copy(node0[:], rows["dst"][:].rearrange("q (h i) -> q h i", h=2)[:, :, 0]))
                link(dve.tensor_tensor(rep[:], beforef[:], node0[:], ALU.not_equal))
                link(dve.tensor_tensor(rep[:], rep[:], cont[:], ALU.mult))
                link(dve.tensor_scalar(key[:], node0[:], 1.0, None, ALU.add))
                link(dve.tensor_tensor(key[:], key[:], cont[:], ALU.mult))
                link(dve.tensor_scalar(key[:], key[:], -1.0, None, ALU.add))
                for h in range(2):
                    dve.tensor_scalar(diag[:, h, :], g["ident"][0:EROWS, 0:EROWS], key[:, h:h + 1], None, ALU.mult)
                link(dve.tensor_scalar(beforef[:], rep[:], -float(FAR), float(FAR), ALU.mult, ALU.add))
                link(dve.tensor_tensor(beforef[:], beforef[:], node0[:], ALU.add))
                dve.tensor_copy(idx0[:], beforef[:]).then_inc(turned, 1)
                dve.wait_ge(read, 1)

                def cols(o, k):
                    for h in range(2):
                        last = dve.tensor_copy(o.rearrange("p (q h) -> p h q", h=2)[:, h, :], pc[k][:, h * P:h * P + EROWS])
                    return last
                cols(g["src"][:, 0:ETILES], 0)
                cols(g["dst"][:, 0:ETILES], 1)
                cols(g["rank"][:], 2)
                cols(g["first"][:], 3)
                link(cols(g["ew"][:], 4))
                link(dve.tensor_scalar(rowf[:], g["first"][:], -float(FAR), float(FAR), ALU.mult, ALU.add))
                link(dve.tensor_tensor(rowf[:], rowf[:], g["dst"][:, 0:ETILES], ALU.add))
                link(dve.tensor_copy(fdst[:], rowf[:]))
                dve.wait_ge(bases, 2)
                link(dve.tensor_tensor(rowf[:], tbase[:], g["rank"][:], ALU.add))
                link(dve.tensor_copy(rowid[:], rowf[:]))
                dve.tensor_copy(idx[:], fdst[:, 0:2 * HALF])
                dve.tensor_copy(val[:, :, 0], rowid[:, 0:2 * HALF])
                dve.tensor_copy(val[:, :, 1], edgeid[:, 0:2 * HALF]).then_inc(idxed, 2)
                with dve.Fori(0, EITER - 1) as i:
                    for h in range(2):
                        s = slice(h * HALF, (h + 1) * HALF)
                        nxt = bass.ds((i + 1) * 2 * HALF + h * HALF, HALF)
                        dve.wait_ge(scattered[h], (i + 1) * HALF * 16)
                        dve.tensor_copy(idx[:, s], fdst[:, nxt])
                        dve.tensor_copy(val[:, s, 0], rowid[:, nxt])
                        dve.tensor_copy(val[:, s, 1], edgeid[:, nxt]).then_inc(idxed, 1)
                dve.wait_ge(read, 2)
                dve.tensor_copy(g["startrow"][:], pany[0:HEADS, 0, 0:EROWS])
                dve.tensor_copy(g["endrow"][:], pany[0:HEADS, 1, 0:EROWS])
                dve.tensor_copy(g["insiderow"][:], pany[0:SCORES, 2, 0:EROWS])
                for h in range(2):
                    for o in range(2):
                        last = dve.tensor_scalar(g["same"][:, h, o, :], prow[0:EROWS, o, 0:EROWS], key[:, h:h + 1],
                                                 cont[:, h:h + 1], ALU.is_equal, ALU.mult)
                link(last)
                for k in range(4):
                    n = min(q4, (E - k * q4 * P) // P)
                    dve.wait_ge(attrs[k], 32 if n < q4 else 16)
                    t = attr[k % 2]
                    link(dve.tensor_tensor(t[:], t[:], aerow[:].rearrange("p (a c) -> p a c", a=1).to_broadcast([P, q4, EDIM]), ALU.mult))
                    dve.tensor_reduce(g["ee"][:, k * q4:(k + 1) * q4], t[:], AX.X, ALU.add).then_inc(attrd, 1)
                dve.wait_ge(ptrs, 16)
                dve.tensor_copy(pieceF[:, 0, :], pieceR[:, :, 0])
                dve.tensor_copy(pieceF[:, 1, :], pieceR[:, :, 1]).then_inc(turned, 1)
                dve.wait_ge(read, 3)
                for k, name in enumerate(("piece", "slot")):
                    for j in range(4):
                        last = dve.tensor_copy(g[name][:, 0:NTILES].rearrange("p (q j) -> p j q", j=4)[:, j, :],
                                               pc[k][:, j * P:j * P + EROWS])
                link(last)


def edge_pass(nc, g, kind, table, beside):
    last_row, width = table.shape[0] - 1, table.shape[1]
    slots = 2 * HALF
    with Phase(nc) as ph:
        rows = ph.sb("rows", [P, slots, CW])
        onehot = ph.sb("onehot", [P, slots, P])
        sums = ph.sb("sums", [P, 2, HALF, CW])
        idx = ph.sb("idxs", [P, slots], I32)
        none = ph.sb("none", [1, CW])
        acc = [ph.ps(f"acc{k}", [P, CW]) for k in range(2)]
        passed = ph.sem("passed")
        gathered = [ph.sem(f"gathered{h}") for h in range(2)]
        stored = [ph.sem(f"stored{h}") for h in range(2)]
        (cleared, idx_ready, hot_ready, multiplied, copied, none_ready, none_stored) = (
            ph.sem(n) for n in ("cleared", "idx_ready", "hot_ready", "multiplied", "copied", "none_ready", "none_stored"))
        out = g["pieces"][0:EPAD, :].rearrange("(t r) c -> r t c", r=P)
        with nc.Block() as block:
            @block.gpsimd
            def _(pool):
                pool.wait_ge(cleared, 1)
                with pool.Fori(0, EITER) as i:
                    for h in range(2):
                        pool.wait_ge(idx_ready, 2 * i + h + 1)
                        carry_wait(pool, passed)
                        for j in range(h * HALF, (h + 1) * HALF):
                            pool.indirect_dma_start(rows[:, j, 0:width], None, table,
                                                    bass.IndirectOffsetOnAxis(idx[:, j:j + 1], 0), bounds_check=last_row,
                                                    oob_is_err=False).then_inc(gathered[h], 16)

            @block.vector
            def _(dve):
                dve.memset(rows[:], 0.0)
                dve.memset(none[:], 0.0).then_inc(cleared, 1)
                dve.wait_ge(cleared, 1)
                if kind in ("count", "attention"):
                    dve.memset(rows[:, :, D:D + 1], 1.0)
                dve.memset(none[:, D:D + max(beside, 1)], 1.0 if beside else 0.0).then_inc(none_ready, 1)
                dve.tensor_copy(idx[:], g["src"][:, 0:slots]).then_inc(idx_ready, 2)
                with dve.Fori(0, EITER) as i:
                    for h in range(2):
                        for j in range(h * HALF, (h + 1) * HALF):
                            t = bass.ds(i * slots + j, 1)
                            rank = g["rank"][:, t]
                            dve.wait_ge(multiplied, i * slots + j + 1)
                            if kind in ("attention", "gcn"):
                                w = g["exs"][:, t, 0] if kind == "attention" else g["ew"][:, t]
                                ins = dve.tensor_scalar(onehot[:, j, :], g["iota"][:], rank, w, ALU.is_equal, ALU.mult)
                            else:
                                if kind == "gat" and j % HALF == 0:
                                    dve.wait_ge(gathered[h], (i + 1) * HALF * 16)
                                if kind == "gat":
                                    row = rows[:, j, 0:D].rearrange("p (h c) -> p h c", h=HEADS)
                                    ex = g["exs"][:, t, :].rearrange("p a h -> p (a h)").unsqueeze(2)
                                    dve.tensor_tensor(row, row, ex.to_broadcast([P, HEADS, HID]), ALU.mult)
                                    dve.tensor_copy(rows[:, j, D:CW], g["exd"][:, t, :].rearrange("p a h -> p (a h)"))
                                else:
                                    dve.tensor_copy(rows[:, j, D + 1:D + 2], g["ew"][:, t])
                                ins = dve.tensor_scalar(onehot[:, j, :], g["iota"][:], rank, None, ALU.is_equal)
                            ins.then_inc(hot_ready, 1)
                    for h in range(2):
                        dve.wait_ge(multiplied, (i + 1) * slots + (h + 1) * HALF)
                        s = slice(h * HALF, (h + 1) * HALF)
                        dve.tensor_copy(idx[:, s], g["src"][:, bass.ds((i + 1) * slots + h * HALF, HALF)]).then_inc(idx_ready, 1)

            @block.tensor
            def _(pe):
                pe.sem_inc(multiplied, slots)
                with pe.Fori(0, EITER) as i:
                    for j in range(slots):
                        if j % HALF == 0:
                            pe.wait_ge(gathered[j // HALF], (i + 1) * HALF * 16)
                        pe.wait_ge(hot_ready, i * slots + j + 1)
                        pe.wait_ge(copied, i * slots + j + 1)
                        pe.matmul(acc[j % 2][:], onehot[:, j, :], rows[:, j, :], start=True, stop=True).then_inc(multiplied, 1)

            @block.scalar
            def _(act):
                act.sem_inc(copied, 2)
                with act.Fori(0, EITER) as i:
                    for h in range(2):
                        act.wait_ge(stored[h], (i + 1) * 16)
                        for j in range(h * HALF, (h + 1) * HALF):
                            act.wait_ge(multiplied, (i + 1) * slots + j + 1)
                            act.activation(sums[:, h, j - h * HALF, :], acc[j % 2][:], ACT.Copy).then_inc(copied, 1)

            @block.sync
            def _(sp):
                for h in range(2):
                    sp.dma_start(g["credit"][:, 8 * h:8 * h + 8], g["zero"][:]).then_inc(stored[h], 16)
                sp.wait_ge(none_ready, 1)
                sp.dma_start(g["pieces"][NO_EDGES:NO_EDGES + 1, :], none[:]).then_inc(none_stored, 16)
                with sp.Fori(0, EITER) as i:
                    for h in range(2):
                        sp.wait_ge(copied, i * slots + (h + 1) * HALF + 2)
                        sp.dma_start(out[:, bass.ds(i * slots + h * HALF, HALF), :], sums[:, h, :, :]).then_inc(stored[h], 16)
                sp.wait_ge(none_stored, 16)
                for h in range(2):
                    sp.wait_ge(stored[h], (EITER + 1) * 16)
    merge_pieces(nc, g)


def merge_pieces(nc, g):
    with Phase(nc) as ph:
        firsts = ph.sb("firsts", [EROWS, 2, CW])
        target = ph.sb("targets", [EROWS, 2, CW])
        sums = [ph.ps(f"sums{h}", [P, CW]) for h in range(2)]
        loaded, cleared, summed, added, got, put = (ph.sem(n) for n in ("loaded", "cleared", "summed", "added", "got", "put"))
        with nc.Block() as block:
            @block.sync
            def _(sp):
                sp.dma_start(firsts[:], g["pieces"][0:EPAD, :].rearrange("(q h r) c -> q h r c", h=2, r=P)[:, :, 0, :]).then_inc(loaded, 16)

            @block.gpsimd
            def _(pool):
                pool.wait_ge(cleared, 1)
                for h in range(2):
                    pool.indirect_dma_start(target[:, h, :], None, g["pieces"], bass.IndirectOffsetOnAxis(g["target"][:, h, 0:1], 0),
                                            bounds_check=EPAD - 1, oob_is_err=False).then_inc(got, 16)
                pool.wait_ge(added, 2)
                for h in range(2):
                    pool.indirect_dma_start(g["pieces"], bass.IndirectOffsetOnAxis(g["target"][:, h, 0:1], 0), target[:, h, :], None,
                                            bounds_check=EPAD - 1, oob_is_err=False).then_inc(put, 16)
                pool.wait_ge(put, 32)

            @block.tensor
            def _(pe):
                pe.wait_ge(loaded, 16)
                for o in range(2):
                    for h in range(2):
                        last = pe.matmul(sums[o][0:EROWS, :], g["same"][:, h, o, :], firsts[:, h, :], start=(h == 0), stop=(h == 1))
                    last.then_inc(summed, 1)

            @block.vector
            def _(dve):
                dve.memset(target[:], 0.0).then_inc(cleared, 1)
                dve.wait_ge(got, 32)
                for o in range(2):
                    dve.wait_ge(summed, o + 1)
                    dve.tensor_tensor(target[:, o, :], target[:, o, :], sums[o][0:EROWS, :], ALU.add).then_inc(added, 1)


def edge_scores(nc, g, heads):
    slots = 2 * HALF
    gat = heads > 1
    with Phase(nc) as ph:
        columns = range(SCORES) if gat else (HEADS,)
        ncols = len(columns)
        idx = ph.sb("idxs", [P, slots], I32)
        got = ph.sb("got", [P, slots, SCORES])
        srcs = ph.sb("srcs", [P, ETILES, SCORES])
        dsts = ph.sb("dsts", [P, ncols, ETILES])
        firstR = ph.sb("firstR", [EROWS, 2 * P, SCORES])
        dstR = ph.sb("dstR", [EROWS, ncols, 2 * P])
        dend = ph.sb("dend", [EROWS, ncols])
        drow = ph.sb("drow", [ncols, EROWS])
        dcarry = ph.sb("dcarry", [ncols, EROWS + 1])
        dstart = ph.sb("dstart", [EROWS, ncols])
        score = ph.sb("score", [P, heads, ETILES])
        selfs = ph.sb("selfs", [P, heads, ETILES])
        most = ph.sb("most", [P, heads, ETILES])
        scoreR, fwd, bwd = (ph.sb(n, [EROWS, heads, 2 * P]) for n in ("scoreR", "fwd", "bwd"))
        ends = ph.sb("ends", [EROWS, 2, HEADS])
        endrow = ph.sb("endsrow", [HEADS, 2, EROWS])
        carryrow = ph.sb("carryrow", [HEADS, 2, EROWS + 1])
        carry = ph.sb("carry", [EROWS, 2, HEADS])
        pr = [ph.ps(f"pr{k}", [P, 2, 2 * P]) for k in range(2)]
        pe_rows = ph.ps("perows", [P, 2, P])
        pcar = ph.ps("pcar", [P, 2, HEADS])
        pcols = [ph.ps(f"pcols{k}", [P, 2, 2 * P]) for k in range(2)]
        passed = ph.sem("passed")
        gathered = [ph.sem(f"gathered{h}") for h in range(2)]
        banks = pr + pcols
        idx_ready, done, scored, turned, exped, loaded, spread, spread_turned = (
            ph.sem(n) for n in ("idx_ready", "done", "scored", "turned", "exped", "loaded", "spread", "spread_turned"))
        with nc.Block() as block:
            @block.sync
            def _(sp):
                sp.dma_start(firstR[:], g["firsts"].rearrange("(q i) c -> q i c", q=EROWS)).then_inc(loaded, 16)

            @block.gpsimd
            def _(pool):
                with pool.Fori(0, EITER) as i:
                    for h in range(2):
                        pool.wait_ge(idx_ready, 2 * i + h + 1)
                        carry_wait(pool, passed)
                        for j in range(h * HALF, (h + 1) * HALF):
                            pool.indirect_dma_start(got[:, j, :], None, g["scores"],
                                                    bass.IndirectOffsetOnAxis(idx[:, j:j + 1], 0), bounds_check=NPAD - 1,
                                                    oob_is_err=False).then_inc(gathered[h], 16)

            @block.vector
            def _(dve):
                link = chain(dve, done)
                dve.tensor_copy(idx[:], g["src"][:, 0:slots]).then_inc(idx_ready, 2)
                dve.memset(carryrow[:], -BIG)
                dve.memset(dcarry[:], 0.0)
                dve.wait_ge(loaded, 16)

                def spreads(start):
                    for n, c in enumerate(columns):
                        last = dve.tensor_tensor_scan(dstR[:, n, :], g["insideR"][:], firstR[:, :, c],
                                                      0.0 if start is None else start[:, n:n + 1], ALU.mult, ALU.add)
                    return last
                link(spreads(None))
                dve.tensor_copy(dend[:], dstR[:, :, 2 * P - 1]).then_inc(spread, 1)
                dve.wait_ge(spread_turned, 1)
                link(dve.tensor_copy(drow[:], pe_rows[0:ncols, 0, 0:EROWS]))
                dve.tensor_tensor_scan(dcarry[:, 1:EROWS + 1], g["insiderow"][0:ncols, :], drow[:], 0.0,
                                       ALU.mult, ALU.add).then_inc(spread, 1)
                dve.wait_ge(spread_turned, 2)
                link(dve.tensor_copy(dstart[:], pe_rows[0:EROWS, 1, 0:ncols]))
                spreads(dstart).then_inc(spread, 1)
                with dve.Fori(0, EITER) as i:
                    for h in range(2):
                        s = slice(h * HALF, (h + 1) * HALF)
                        dve.wait_ge(gathered[h], (i + 1) * HALF * 16)
                        dve.tensor_copy(srcs[:, bass.ds(i * slots + h * HALF, HALF), :], got[:, s, :])
                        dve.tensor_copy(idx[:, s], g["src"][:, bass.ds((i + 1) * slots + h * HALF, HALF)]).then_inc(idx_ready, 1)
                dve.wait_ge(spread_turned, 3)
                for n in range(ncols):
                    last = dve.tensor_copy(dsts[:, n, :].rearrange("p (q a) -> p a q", a=2),
                                           banks[n // 2][:, n % 2, :].rearrange("p (a q) -> p a q", a=2)[:, :, 0:EROWS])
                link(last)
                for h in range(heads):
                    last = dve.tensor_tensor(score[:, h, :], srcs[:, :, h], dsts[:, ncols - heads + h, :], ALU.add)
                link(last)
                if gat:
                    link(dve.tensor_tensor(selfs[:], dsts[:, 0:HEADS, :], dsts[:, HEADS:SCORES, :], ALU.add))
                    link(dve.scalar_tensor_tensor(selfs[:], selfs[:], 0.2, selfs[:], ALU.mult, ALU.max))
                else:
                    link(dve.tensor_tensor(score[:, 0, :], score[:, 0, :], g["ee"][:], ALU.add))
                dve.scalar_tensor_tensor(score[:], score[:], 0.2, score[:], ALU.mult, ALU.max).then_inc(scored, 1)
                dve.wait_ge(turned, 1)
                for h in range(heads):
                    last = dve.tensor_copy(scoreR[:, h, :], pr[h // 2][0:EROWS, h % 2, :])
                link(last)

                def scans(start):
                    for h in range(heads):
                        dve.tensor_tensor_scan(fwd[:, h, :], g["startR"][:], scoreR[:, h, :],
                                               -BIG if start is None else start[:, 0, h:h + 1], ALU.add, ALU.max)
                        last = dve.tensor_tensor_scan(bwd[:, h, ::-1], g["endR"][:, ::-1], scoreR[:, h, ::-1],
                                                      -BIG if start is None else start[:, 1, h:h + 1], ALU.add, ALU.max)
                    link(last)
                scans(None)
                dve.tensor_copy(ends[:, 0, 0:heads], fwd[:, :, 2 * P - 1])
                dve.tensor_copy(ends[:, 1, 0:heads], bwd[:, :, 0]).then_inc(scored, 1)
                dve.wait_ge(turned, 2)
                link(dve.tensor_copy(endrow[0:heads, :, :], pe_rows[0:heads, :, 0:EROWS]))
                dve.tensor_tensor_scan(carryrow[0:heads, 0, 1:EROWS + 1], g["startrow"][0:heads, :], endrow[0:heads, 0, :],
                                       -BIG, ALU.add, ALU.max)
                rev = slice(EROWS - 1, None, -1)
                dve.tensor_tensor_scan(carryrow[0:heads, 1, rev], g["endrow"][0:heads, ::-1], endrow[0:heads, 1, ::-1],
                                       -BIG, ALU.add, ALU.max).then_inc(scored, 1)
                dve.wait_ge(turned, 3)
                link(dve.tensor_copy(carry[:, :, 0:heads], pcar[0:EROWS, :, 0:heads]))
                scans(carry)
                dve.tensor_tensor(fwd[:], fwd[:], bwd[:], ALU.max).then_inc(scored, 1)
                dve.wait_ge(turned, 4)
                for h in range(heads):
                    last = dve.tensor_copy(most[:, h, :].rearrange("p (q a) -> p a q", a=2),
                                           pcols[h // 2][:, h % 2, :].rearrange("p (a q) -> p a q", a=2)[:, :, 0:EROWS])
                link(last)
                if gat:
                    link(dve.tensor_tensor(most[:], most[:], selfs[:], ALU.max))
                    dve.tensor_tensor(selfs[:], selfs[:], most[:], ALU.subtract)
                dve.tensor_tensor(score[:], score[:], most[:], ALU.subtract).then_inc(scored, 1)
                dve.wait_ge(exped, 1)
                if gat:
                    for h in range(heads):
                        last = dve.tensor_tensor(selfs[:, h, :], selfs[:, h, :], g["first"][:], ALU.mult)
                    link(last)
                    for h in range(heads):
                        dve.tensor_copy(g["exd"][:, :, HEADS + h], selfs[:, h, :])
                        dve.tensor_tensor(g["exd"][:, :, h], selfs[:, h, :], score[:, h, :], ALU.add)
                for h in range(heads):
                    last = dve.tensor_copy(g["exs"][:, :, h], score[:, h, :])
                link(last)

            @block.tensor
            def _(pe):
                ident = g["ident"]
                pe.wait_ge(spread, 1)
                pe.transpose(pe_rows[0:ncols, 0, 0:EROWS], dend[:], ident[0:EROWS, 0:EROWS]).then_inc(spread_turned, 1)
                pe.wait_ge(spread, 2)
                pe.transpose(pe_rows[0:EROWS, 1, 0:ncols], dcarry[:, 0:EROWS], ident[0:ncols, 0:ncols]).then_inc(spread_turned, 1)
                pe.wait_ge(spread, 3)
                for n in range(ncols):
                    for a in range(2):
                        last = pe.transpose(banks[n // 2][:, n % 2, a * P:a * P + EROWS], dstR[:, n, a * P:(a + 1) * P],
                                            ident[0:EROWS, 0:EROWS])
                last.then_inc(spread_turned, 1)
                pe.wait_ge(scored, 1)
                for h in range(heads):
                    for a in range(2):
                        last = pe.transpose(pr[h // 2][0:EROWS, h % 2, a * P:(a + 1) * P],
                                            score[:, h, :].rearrange("p (q a) -> p a q", a=2)[:, a, :], ident[:])
                last.then_inc(turned, 1)
                pe.wait_ge(scored, 2)
                for k in range(2):
                    last = pe.transpose(pe_rows[0:heads, k, 0:EROWS], ends[:, k, 0:heads], ident[0:EROWS, 0:EROWS])
                last.then_inc(turned, 1)
                pe.wait_ge(scored, 3)
                for k in range(2):
                    last = pe.transpose(pcar[0:EROWS, k, 0:heads], carryrow[0:heads, k, k:k + EROWS], ident[0:heads, 0:heads])
                last.then_inc(turned, 1)
                pe.wait_ge(scored, 4)
                for h in range(heads):
                    for a in range(2):
                        last = pe.transpose(pcols[h // 2][:, h % 2, a * P:a * P + EROWS], fwd[:, h, a * P:(a + 1) * P],
                                            ident[0:EROWS, 0:EROWS])
                last.then_inc(turned, 1)

            @block.scalar
            def _(act):
                act.wait_ge(scored, 5)
                if gat:
                    act.activation(selfs[:], selfs[:], ACT.Exp)
                act.activation(score[:], score[:], ACT.Exp).then_inc(exped, 1)


class Steps:

    def __init__(self, eng, sem):
        self.eng, self.sem, self.base, self.n = eng, sem, 0, 0

    def mark(self, ins):
        self.n += 1
        ins.then_inc(self.sem, 1)
        return self.base + self.n

    def wait(self, mark):
        self.eng.wait_ge(self.sem, mark)

    def link(self, ins):
        self.wait(self.mark(ins))


def in_turn(eng, stages, steps=None, links=0):
    last = max(lag for lag, _ in stages)
    fill = -(-last // SLOTS)

    def step(i, r):
        running = []
        for lag, f in stages:
            if not isinstance(i, int) or 0 <= i * SLOTS + r - lag < NGROUPS:
                running.append(f(i * SLOTS + (r - lag), (r - lag) % SLOTS, i + ((r - lag) // SLOTS + 1)))
        running = [f for f in running if f is not None]
        while running:
            running = [f for f in running if next(f, StopIteration) is not StopIteration]
    for i in range(fill):
        for r in range(SLOTS):
            step(i, r)
    with eng.Fori(fill, NITER) as i:
        if steps:
            before = steps.n
            steps.base, steps.n = before + (i - fill) * (SLOTS * links), 0
        for r in range(SLOTS):
            step(i, r)
        if steps:
            assert steps.n == SLOTS * links, steps.n
    if steps:
        steps.base, steps.n = before + (NITER - fill) * (SLOTS * links), 0
    for r in range(last):
        step(NITER, r)


class Nodes:

    def __init__(self, nc, ph, g, loads, stores, signals):
        self.nc, self.ph, self.g = nc, ph, g
        self.in_bufs = {k: ph.sb(k, [P, SLOTS, GT, table.shape[1]]) for k, table, *_ in loads}
        self.loads, self.stores = loads, stores
        self.pieces = ph.sb("cb", [P, SLOTS, GT, CW])
        self.idx = ph.sb("idxs", [P, SLOTS * GT], I32)
        self.loaded = {k: [ph.sem(f"loaded_{k}{s}") for s in range(SLOTS)] for k, *_ in loads}
        self.got = [ph.sem(f"got{s}") for s in range(SLOTS)]
        self.stored = {k: [ph.sem(f"stored_{k}{s}") for s in range(SLOTS)] for k, *_ in stores}
        self.idx_ready = ph.sem("idx_ready")
        self.slots = ph.sb("slots", [P, SLOTS * GT], I32)
        self.slots_ready = ph.sem("slots_ready")
        self.scattered = [ph.sem(f"scattered{s}") for s in range(SLOTS)]
        self.step = ph.sem("vector_step")
        self.passed, self.passed_v = ph.sem("passed"), ph.sem("passed_v")
        self.sig = {k: ph.sem(k) for k in signals}

    def start(self, eng, *signals):
        for k in signals:
            eng.sem_inc(self.sig[k], CREDIT)

    def done(self, ins, signal):
        ins.then_inc(self.sig[signal], 1)

    def need(self, eng, signal, n, back=0):
        eng.wait_ge(self.sig[signal], n + (1 + CREDIT - back))

    def need_load(self, eng, k, turn, s):
        eng.wait_ge(self.loaded[k][s], turn * 16)

    def need_pieces(self, eng, turn, s):
        eng.wait_ge(self.got[s], turn * (16 * GT))

    def need_stored(self, eng, k, turn, s):
        eng.wait_ge(self.stored[k][s], turn * 16)

    def gathers(self, pool):
        def f(n, s, turn):
            pool.wait_ge(self.idx_ready, n + 1)
            carry_wait(pool, self.passed)
            for j in range(GT):
                pool.indirect_dma_start(self.pieces[:, s, j, :], None, self.g["pieces"],
                                        bass.IndirectOffsetOnAxis(self.idx[:, s * GT + j:s * GT + j + 1], 0),
                                        bounds_check=EPAD, oob_is_err=False).then_inc(self.got[s], 16)
        return f

    def scatters(self, pool, sc):
        def indices(n, s, turn):
            pool.wait_ge(self.scattered[s], turn * (16 * GT))
            pool.tensor_copy(self.slots[:, s * GT:(s + 1) * GT],
                             self.g["slot"][:, bass.ds(n * GT, GT)]).then_inc(self.slots_ready, 1)

        def scatter(n, s, turn):
            pool.wait_ge(self.slots_ready, n + 1)
            self.need(pool, "out", n)
            carry_wait(pool, self.passed)
            for j in range(GT):
                pool.indirect_dma_start(self.g["firsts"], bass.IndirectOffsetOnAxis(self.slots[:, s * GT + j:s * GT + j + 1], 0),
                                        sc[:, s, j, :], None, bounds_check=EPAD - 1,
                                        oob_is_err=False).then_inc(self.scattered[s], 16)
        return indices, scatter

    def need_scattered(self, eng, turn, s):
        eng.wait_ge(self.scattered[s], turn * (16 * GT))

    def gather(self, pool, sc=None, lag=0):
        if sc is None:
            in_turn(pool, [(0, self.gathers(pool))])
            return
        for k in range(SLOTS * GT):
            c = (16 + k) * SCORES
            pool.dma_start(self.g["credit"][:, c:c + SCORES], self.g["zero"][:]).then_inc(self.scattered[k // GT], 16)
        indices, scatter = self.scatters(pool, sc)
        in_turn(pool, [(lag, scatter), (0, self.gathers(pool)), (lag - 1, indices)])
        for s in range(SLOTS):
            pool.wait_ge(self.scattered[s], (NITER + 1) * 16 * GT)

    def first_indices(self, dve):
        dve.tensor_copy(self.idx[:], self.g["piece"][:, 0:SLOTS * GT]).then_inc(self.idx_ready, SLOTS)

    def next_indices(self, dve, n, s):
        dve.tensor_copy(self.idx[:, s * GT:(s + 1) * GT],
                        self.g["piece"][:, bass.ds((n + SLOTS) * GT, GT)]).then_inc(self.idx_ready, 1)

    def start_stores(self, sp):
        c = 0
        for k, *_ in self.stores:
            for s in range(SLOTS):
                sp.dma_start(self.g["credit"][:, c:c + 8], self.g["zero"][:]).then_inc(self.stored[k][s], 16)
                c += 8

    def traffic(self, sp):
        self.start_stores(sp)

        def load(k, table, free):
            def f(n, s, turn):
                self.need(sp, free, n, back=SLOTS)
                self.move(sp, n, table, self.in_bufs[k][:, s, :, :], self.loaded[k][s], load=True)
            return f

        def store(k, table, buf, ready):
            def f(n, s, turn):
                self.need(sp, ready, n)
                self.move(sp, n, table, buf[:, s, :, :], self.stored[k][s], load=False)
            return f
        moves = [(lag + 1, load(k, table, free)) for k, table, free, lag in self.loads]
        moves += [(lag + SLOTS + 1, store(*x)) for *x, lag in self.stores]
        in_turn(sp, moves)
        for k, *_ in self.stores:
            for s in range(SLOTS):
                sp.wait_ge(self.stored[k][s], (NITER + 1) * 16)

    @staticmethod
    def partial(table):
        return table.shape[0] != NPAD

    def move(self, sp, n, table, buf, sem, load):
        if isinstance(n, int) and self.partial(table) and (n + 1) * GROUP > N:
            lo = n * GROUP
            assert 0 < N - lo <= P
            dram, chip = table[lo:N, :], buf[0:N - lo, 0, :]
        else:
            dram = table[bass.ds(n * GROUP, GROUP), :].rearrange("(j p) c -> p j c", p=P)
            chip = buf
        sp.dma_start(chip if load else dram, dram if load else chip).then_inc(sem, 16)


def turn(pe, bank, x, ident):
    for c in range(2):
        for j in range(GT):
            last = pe.transpose(bank[:, (c * GT + j) * P:(c * GT + j + 1) * P], x[:, j, c * P:(c + 1) * P], ident[:])
    return last


def times(pe, bank, xT, w, lo, hi):
    for j in range(GT):
        for c in range(2):
            ins = pe.matmul(bank[:, j, 0:hi - lo], xT[:, (c * GT + j) * P:(c * GT + j + 1) * P], w[:, c, lo:hi],
                            start=(c == 0), stop=(c == 1))
    return ins


def carry_wait(eng, sem):
    eng.sem_inc(sem, 1)


def stats(dve, steps, y, st, mv, n, signal):
    for j in range(GT):
        last = dve.bn_stats(st[:, j, :], y[:, j, :])
    mark = steps.mark(last)
    yield
    steps.wait(mark)
    carry_wait(dve, n.passed_v)
    for j in range(GT):
        last = dve.bn_aggr(mv[:, j, :], st[:, j, :])
    n.done(last, signal)


def normalise(dve, steps, out, y, mv, std, rstd, done):
    mark = steps.mark(dve.reciprocal(rstd, std))
    yield
    steps.wait(mark)
    for j in range(GT):
        last = dve.tensor_scalar(out[:, j, :], y[:, j, :], mv[:, j, 0:1], rstd[:, j:j + 1], ALU.subtract, ALU.mult)
    done(last)


def scaled(dve, steps, n, h, mv, std, small, dis):
    mark = steps.mark(dve.reciprocal(small[:, 0], std))
    dve.tensor_copy(h[:, :, D], dis)
    yield
    steps.wait(mark)
    mark = steps.mark(dve.tensor_tensor(small[:, 1], small[:, 0], dis, ALU.mult))
    yield
    steps.wait(mark)
    n.done(dve.scalar_tensor_tensor(small[:, 2], mv[:, :, 0], -1.0, small[:, 1], ALU.mult, ALU.mult), "z")


def sage_nodes(nc, g, x):
    with Phase(nc) as ph:
        x1 = ph.sb("x1", [P, SLOTS, GT, D])
        sc = ph.sb("sc", [P, SLOTS, GT, SCORES])
        n = Nodes(nc, ph, g, [("x", x, "sum", 4)], [("x1", g["x1"], x1, "x1", 6), ("sc", g["scores"], sc, "out", 6)],
                  ("mean", "turned", "copied", "product", "relu", "squares", "norm", "y", "std", "x1", "out", "inv", "sum"))
        xb, cb = n.in_bufs["x"], n.pieces
        small = ph.sb("small", [P, SLOTS, 4, GT])
        mean = ph.sb("mean", [P, SLOTS, GT, D])
        xT, mT = (ph.sb(k, [P, SLOTS, 2 * GT * P]) for k in ("xT", "mT"))
        relu, y = (ph.sb(k, [P, SLOTS, GT, D]) for k in ("relu", "y"))
        junk = ph.sb("junk", [P, SLOTS, GT, 2, D])
        sq, norm = (ph.sb(k, [P, SLOTS, GT]) for k in ("sq", "norm"))
        inv, std, rstd = (ph.sb(k, [P, SLOTS, GT]) for k in ("inv", "std", "rstd"))
        st = ph.sb("st", [P, SLOTS, GT, 6])
        mv = ph.sb("mv", [P, SLOTS, GT, 2])
        px = [ph.ps(f"px{k}", [P, 2 * GT * P]) for k in range(2)]
        pm = [ph.ps(f"pm{k}", [P, 2 * GT * P]) for k in range(2)]
        po = [ph.ps(f"po{k}", [P, GT, D]) for k in range(2)]
        with nc.Block() as block:
            @block.sync
            def _(sp):
                n.traffic(sp)

            @block.gpsimd
            def _(pool):
                n.gather(pool, sc, 6 + SLOTS + 1)

            @block.tensor
            def _(pe):
                n.start(pe, "turned", "product")

                def transposes(m, s, k):
                    n.need_load(pe, "x", k, s)
                    n.need(pe, "copied", m, back=2)
                    turn(pe, px[s % 2], xb[:, s], g["ident"])
                    n.need(pe, "mean", m)
                    n.done(turn(pe, pm[s % 2], mean[:, s], g["ident"]), "turned")

                def products(m, s, k):
                    n.need(pe, "copied", m)
                    n.need(pe, "relu", m, back=2)
                    for j in range(GT):
                        pe.matmul(po[s % 2][:, j, :], g["ones3"][:], g["b0"][:], start=True, stop=False)
                        for c in range(4):
                            lo = ((c % 2) * GT + j) * P
                            last = pe.matmul(po[s % 2][:, j, :], (xT, mT)[c // 2][:, s, lo:lo + P], g["w0"][:, c, :],
                                             start=False, stop=(c == 3))
                    n.done(last, "product")
                in_turn(pe, [(1, transposes), (2, products)])

            @block.scalar
            def _(act):
                n.start(act, "mean", "copied", "relu", "squares", "norm", "std")

                def means(m, s, k):
                    n.need(act, "inv", m)
                    n.need(act, "turned", m, back=SLOTS)
                    for j in range(GT):
                        last = act.activation(mean[:, s, j, :], cb[:, s, j, 0:D], ACT.Copy, scale=small[:, s, 1, j:j + 1])
                    n.done(last, "mean")

                def copies(m, s, k):
                    n.need(act, "turned", m)
                    n.need(act, "product", m, back=SLOTS)
                    act.activation(xT[:, s, :], px[s % 2][:], ACT.Copy)
                    n.done(act.activation(mT[:, s, :], pm[s % 2][:], ACT.Copy), "copied")

                def relus(m, s, k):
                    n.need(act, "product", m)
                    n.need(act, "x1", m, back=SLOTS)
                    n.done(act.activation(relu[:, s], po[s % 2][:], ACT.Relu), "relu")
                    n.need(act, "relu", m)
                    for j in range(GT):
                        last = act.activation(y[:, s, j, :], relu[:, s, j, :], ACT.Square, accum_out=sq[:, s, j:j + 1])
                    n.done(last, "squares")
                    n.need(act, "squares", m)
                    n.done(act.activation(norm[:, s, :], sq[:, s, :], ACT.Sqrt), "norm")

                def stds(m, s, k):
                    n.need(act, "y", m)
                    n.need(act, "out", m, back=SLOTS)
                    n.done(act.activation(std[:, s, :], mv[:, s, :, 1], ACT.Sqrt, bias=g["eps"][:]), "std")
                in_turn(act, [(1, copies), (3, relus), (5, stds), (0, means)])

            @block.vector
            def _(dve):
                n.start(dve, "inv", "sum", "y", "x1", "out")
                n.first_indices(dve)
                dve.memset(sc[:], 0.0)
                steps = Steps(dve, n.step)

                def invs(m, s, k):
                    n.need_pieces(dve, k, s)
                    n.need(dve, "mean", m, back=SLOTS)
                    mark = steps.mark(dve.tensor_scalar(small[:, s, 0, :], cb[:, s, :, D], 1.0, None, ALU.max))
                    dve.tensor_scalar(g["dis"][:, bass.ds(m * GT, GT)], cb[:, s, :, D + 1], 1.0, None, ALU.add)
                    yield
                    steps.wait(mark)
                    n.done(dve.reciprocal(small[:, s, 1, :], small[:, s, 0, :]), "inv")

                def indices(m, s, k):
                    n.need(dve, "mean", m)
                    n.next_indices(dve, m, s)

                def ys(m, s, k):
                    n.need(dve, "norm", m)
                    n.need_load(dve, "x", k, s)
                    mark = steps.mark(dve.tensor_scalar(small[:, s, 2, :], norm[:, s, :], 1e-12, None, ALU.max))
                    yield
                    steps.wait(mark)
                    mark = steps.mark(dve.reciprocal(inv[:, s, :], small[:, s, 2, :]))
                    yield
                    steps.wait(mark)
                    for j in range(GT):
                        last = dve.scalar_tensor_tensor(y[:, s, j, :], relu[:, s, j, :], inv[:, s, j:j + 1], xb[:, s, j, :], ALU.mult, ALU.add)
                    n.done(last, "sum")
                    yield
                    n.need(dve, "sum", m)
                    yield from stats(dve, steps, y[:, s], st[:, s], mv[:, s], n, "y")

                def outs(m, s, k):
                    n.need(dve, "std", m)
                    n.need_stored(dve, "x1", k, s)
                    n.need_stored(dve, "sc", k, s)
                    n.need_scattered(dve, k, s)
                    yield from normalise(dve, steps, x1[:, s], y[:, s], mv[:, s], std[:, s, :], rstd[:, s],
                                         lambda ins: n.done(ins, "x1"))
                    yield
                    n.need(dve, "x1", m)
                    for j in range(GT):
                        for c, v in enumerate(("vsrc", "vdst")):
                            last = dve.tensor_tensor_reduce(junk[:, s, j, c, :], x1[:, s, j, :], g[v][:], 1.0, 0.0, ALU.mult, ALU.add,
                                                            sc[:, s, j, c * HEADS:c * HEADS + 1])
                    n.done(last, "out")
                in_turn(dve, [(4, ys), (6, outs), (1, indices), (0, invs)], steps, links=5)

    with Phase(nc) as ph:
        root, made = ph.sem("root"), ph.sem("made")
        with nc.Block() as block:
            @block.scalar
            def _(act):
                act.activation(g["dis"][:], g["dis"][:], ACT.Sqrt).then_inc(root, 1)

            @block.vector
            def _(dve):
                dve.wait_ge(root, 1)
                dve.reciprocal(g["dis"][:], g["dis"][:]).then_inc(made, 1)
                dve.wait_ge(made, 1)


def attention_nodes(nc, g):
    with Phase(nc) as ph:
        x2, h = ph.sb("x2", [P, SLOTS, GT, D]), ph.sb("h", [P, SLOTS, GT, CW])
        n = Nodes(nc, ph, g, [("x", g["x1"], "sum", 2)], [("x2", g["x2"], x2, "y2", 4), ("h", g["h6"], h, "out", 7)],
                  ("turned", "copied", "product", "sum", "y", "std", "x2", "y2", "std2", "z", "out"))
        xb, cb = n.in_bufs["x"], n.pieces
        small = ph.sb("small", [P, SLOTS, 2, GT])
        y = ph.sb("y", [P, SLOTS, GT, D])
        coef = ph.sb("coef", [P, SLOTS, 3, GT])
        aT = ph.sb("aT", [P, SLOTS, 2 * GT * P])
        std, rstd = (ph.sb(k, [P, SLOTS, 2, GT]) for k in ("std", "rstd"))
        st = ph.sb("st", [P, SLOTS, GT, 6])
        mv = ph.sb("mv", [P, SLOTS, 2, GT, 2])
        pa = [ph.ps(f"pa{k}", [P, 2 * GT * P]) for k in range(2)]
        po = [ph.ps(f"po{k}", [P, GT, D]) for k in range(2)]
        with nc.Block() as block:
            @block.sync
            def _(sp):
                n.traffic(sp)

            @block.gpsimd
            def _(pool):
                n.gather(pool)

            @block.tensor
            def _(pe):
                n.start(pe, "turned", "product")

                def transposes(m, s, k):
                    n.need_pieces(pe, k, s)
                    n.need(pe, "copied", m, back=2)
                    n.done(turn(pe, pa[s % 2], cb[:, s], g["ident"]), "turned")

                def products(m, s, k):
                    n.need(pe, "copied", m)
                    n.need(pe, "sum", m, back=2)
                    n.done(times(pe, po[s % 2], aT[:, s], g["w1T"], 0, D), "product")
                in_turn(pe, [(0, transposes), (1, products)])

            @block.scalar
            def _(act):
                n.start(act, "copied", "std", "std2", "out")
                def copies(m, s, k):
                    n.need(act, "turned", m)
                    n.need(act, "product", m, back=SLOTS)
                    n.done(act.activation(aT[:, s, :], pa[s % 2][:], ACT.Copy), "copied")

                def stds(c, signal, before):
                    def f(m, s, k):
                        n.need(act, before, m)
                        n.need(act, "z", m, back=SLOTS)
                        n.done(act.activation(std[:, s, c, :], mv[:, s, c, :, 1], ACT.Sqrt, bias=g["eps"][:]), signal)
                    return f

                def scales(m, s, k):
                    n.need(act, "z", m)
                    n.need_stored(act, "h", k, s)
                    for j in range(GT):
                        last = act.activation(h[:, s, j, 0:D], x2[:, s, j, :], ACT.Identity,
                                              scale=coef[:, s, 1, j:j + 1], bias=coef[:, s, 2, j:j + 1])
                    n.done(last, "out")
                in_turn(act, [(0, copies), (3, stds(0, "std", "y")), (5, stds(1, "std2", "y2")), (7, scales)])

            @block.vector
            def _(dve):
                n.start(dve, "sum", "y", "x2", "y2", "z")
                n.first_indices(dve)
                dve.memset(h[:], 0.0)
                steps = Steps(dve, n.step)

                def invs(m, s, k):
                    n.need_pieces(dve, k, s)
                    mark = steps.mark(dve.tensor_scalar(small[:, s, 0, :], cb[:, s, :, D], 0.5, None, ALU.max))
                    yield
                    steps.wait(mark)
                    steps.mark(dve.reciprocal(small[:, s, 1, :], small[:, s, 0, :]))

                def indices(m, s, k):
                    n.need(dve, "turned", m)
                    n.next_indices(dve, m, s)

                def ys(m, s, k):
                    n.need(dve, "product", m)
                    n.need_load(dve, "x", k, s)
                    for j in range(GT):
                        last = dve.scalar_tensor_tensor(y[:, s, j, :], po[s % 2][:, j, :], small[:, s, 1, j:j + 1], xb[:, s, j, :],
                                                        ALU.mult, ALU.add)
                    n.done(last, "sum")
                    yield
                    n.need(dve, "sum", m)
                    yield from stats(dve, steps, y[:, s], st[:, s], mv[:, s, 0], n, "y")

                def x2s(m, s, k):
                    n.need(dve, "std", m)
                    n.need_stored(dve, "x2", k, s)
                    n.need(dve, "out", m, back=SLOTS)
                    yield from normalise(dve, steps, x2[:, s], y[:, s], mv[:, s, 0], std[:, s, 0, :], rstd[:, s, 0],
                                         lambda ins: n.done(ins, "x2"))
                    yield
                    n.need(dve, "x2", m)
                    yield from stats(dve, steps, x2[:, s], st[:, s], mv[:, s, 1], n, "y2")

                def zs(m, s, k):
                    n.need(dve, "std2", m)
                    n.need(dve, "out", m, back=SLOTS)
                    n.need_stored(dve, "h", k, s)
                    yield from scaled(dve, steps, n, h[:, s], mv[:, s, 1], std[:, s, 1, :], coef[:, s],
                                      g["dis"][:, bass.ds(m * GT, GT)])
                in_turn(dve, [(6, zs), (4, x2s), (2, ys), (1, indices), (0, invs)], steps, links=7)

def gcn_nodes(nc, g, last):
    with Phase(nc) as ph:
        w, bias = (g["w7T"], g["b7"]) if last else (g["w6T"], g["b6"])
        shift = g["c7"] if last else g["c6"]
        o1, o2 = ph.sb("o1", [P, SLOTS, GT, D]), ph.sb("o2", [P, SLOTS, GT, D if last else CW])
        sc = ph.sb("sc", [P, SLOTS, GT, SCORES])
        if last:
            loads = [("h", g["h7"], "agg", 0), ("x", g["y6"], "y", 3), ("x2", g["x2"], "v", 6)]
            stores = [("o1", g["x3"], o1, "x3", 8), ("o2", g["p1"], o2, "out", 11), ("sc", g["scores"], sc, "out", 11)]
        else:
            loads = [("h", g["h6"], "agg", 0), ("x", g["x2"], "y", 3)]
            stores = [("o1", g["y6"], o1, "y", 3), ("o2", g["h7"], o2, "out", 6)]
        n = Nodes(nc, ph, g, loads, stores,
                  ("agg", "turned", "copied", "product", "y", "turned2", "copied2", "product2", "v", "std", "z", "x3",
                   "turned3", "copied3", "product3", "out"))
        hb, xb, cb = n.in_bufs["h"], n.in_bufs["x"], n.pieces
        agg = ph.sb("agg", [P, SLOTS, GT, CW])
        t, add = (ph.sb(k, [P, SLOTS, GT, D]) for k in ("t", "add"))
        share = ph.sb("share", [P, SLOTS, GT])
        coef = ph.sb("coef", [P, SLOTS, 3, GT])
        y = ph.sb("y", [P, SLOTS, GT, D]) if last else o1
        z = ph.sb("z", [P, SLOTS, GT, D]) if last else None
        aT = ph.sb("aT", [P, SLOTS, 2 * GT * P])
        yT, xT = ((ph.sb(k, [P, SLOTS, 2 * GT * P]) for k in ("yT", "xT")) if last else (None, None))
        std, rstd = (ph.sb(k, [P, SLOTS, GT]) for k in ("std", "rstd"))
        st = ph.sb("st", [P, SLOTS, GT, 6])
        mv = ph.sb("mv", [P, SLOTS, GT, 2])
        pa = ph.ps("pa", [P, 2 * GT * P])
        po = [ph.ps(f"po{k}", [P, GT, D]) for k in range(2)]
        if last:
            py, po2, px = ph.ps("py", [P, 2 * GT * P]), ph.ps("po2", [P, GT, D]), ph.ps("px", [P, 2 * GT * P])
            po3 = ph.ps("po3", [P, GT, BANK])
        with nc.Block() as block:
            @block.sync
            def _(sp):
                n.traffic(sp)

            @block.gpsimd
            def _(pool):
                n.gather(pool, *((sc, 11 + SLOTS + 1) if last else ()))

            @block.tensor
            def _(pe):
                n.start(pe, "turned", "product", "turned2", "product2", "turned3", "product3")
                def transposes(m, s, k):
                    n.need(pe, "copied", m, back=1)
                    n.need(pe, "agg", m)
                    n.done(turn(pe, pa, agg[:, s, :, 0:D], g["ident"]), "turned")

                def products(m, s, k):
                    n.need(pe, "copied", m)
                    n.need(pe, "y", m, back=2)
                    n.done(times(pe, po[s % 2], aT[:, s], w, 0, D), "product")

                def transposes2(m, s, k):
                    n.need(pe, "copied2", m, back=1)
                    n.need(pe, "y", m)
                    n.done(turn(pe, py, y[:, s], g["ident"]), "turned2")

                def products2(m, s, k):
                    n.need(pe, "copied2", m)
                    n.need(pe, "v", m, back=1)
                    for j in range(GT):
                        pe.matmul(po2[:, j, :], g["ones3"][:], g["bp"][:], start=True, stop=False)
                        for c in range(2):
                            ins = pe.matmul(po2[:, j, :], yT[:, s, (c * GT + j) * P:(c * GT + j + 1) * P], g["wpT"][:, c, :],
                                            start=False, stop=(c == 1))
                    n.done(ins, "product2")

                def transposes3(m, s, k):
                    n.need(pe, "copied3", m, back=1)
                    n.need(pe, "x3", m)
                    n.done(turn(pe, px, o1[:, s], g["ident"]), "turned3")

                def products3(m, s, k):
                    n.need(pe, "copied3", m)
                    n.need(pe, "out", m, back=1)
                    n.done(times(pe, po3, xT[:, s], g["g1w"], 0, CW), "product3")
                in_turn(pe, [(1, transposes), (2, products)] +
                        ([(4, transposes2), (5, products2), (9, transposes3), (10, products3)] if last else []))

            @block.scalar
            def _(act):
                n.start(act, "copied", "copied2", "copied3", "std", "out")
                def copies(m, s, k):
                    n.need(act, "turned", m)
                    n.need(act, "product", m, back=SLOTS)
                    n.done(act.activation(aT[:, s, :], pa[:], ACT.Copy), "copied")

                def copies2(m, s, k):
                    n.need(act, "turned2", m)
                    n.need(act, "product2", m, back=SLOTS)
                    n.done(act.activation(yT[:, s, :], py[:], ACT.Copy), "copied2")

                def copies3(m, s, k):
                    n.need(act, "turned3", m)
                    n.need(act, "product3", m, back=SLOTS)
                    n.done(act.activation(xT[:, s, :], px[:], ACT.Copy), "copied3")

                def stds(m, s, k):
                    n.need(act, "v" if last else "y", m)
                    n.need(act, "x3" if last else "z", m, back=SLOTS)
                    n.done(act.activation(std[:, s, :], mv[:, s, :, 1], ACT.Sqrt, bias=g["eps"][:]), "std")

                def scales(m, s, k):
                    n.need(act, "z", m)
                    n.need_stored(act, "o2", k, s)
                    for j in range(GT):
                        ins = act.activation(o2[:, s, j, 0:D], y[:, s, j, :], ACT.Identity,
                                             scale=coef[:, s, 1, j:j + 1], bias=coef[:, s, 2, j:j + 1])
                    n.done(ins, "out")

                def rows(m, s, k):
                    n.need(act, "product3", m)
                    n.need_stored(act, "o2", k, s)
                    n.need_stored(act, "sc", k, s)
                    n.need_scattered(act, k, s)
                    act.activation(o2[:, s], po3[:, :, 0:D], ACT.Copy)
                    n.done(act.activation(sc[:, s], po3[:, :, D:CW], ACT.Copy), "out")
                if last:
                    in_turn(act, [(1, copies), (11, rows), (4, copies2), (7, stds), (9, copies3)])
                else:
                    in_turn(act, [(1, copies), (4, stds), (6, scales)])

            @block.vector
            def _(dve):
                n.start(dve, "agg", "y", "v", "z", "x3")
                n.first_indices(dve)
                if not last:
                    dve.memset(o2[:], 0.0)
                steps = Steps(dve, n.step)

                def aggs(m, s, k):
                    n.need_pieces(dve, k, s)
                    n.need_load(dve, "h", k, s)
                    n.need(dve, "turned", m, back=SLOTS)
                    n.done(dve.tensor_tensor(agg[:, s], cb[:, s], hb[:, s], ALU.add), "agg")
                    n.next_indices(dve, m, s)
                    yield
                    n.need(dve, "agg", m)
                    mark = steps.mark(dve.tensor_tensor(share[:, s, :], agg[:, s, :, D], g["dis"][:, bass.ds(m * GT, GT)], ALU.mult))
                    yield
                    steps.wait(mark)
                    for j in range(GT):
                        ins = dve.scalar_tensor_tensor(add[:, s, j, :], shift[:], share[:, s, j:j + 1], bias[:], ALU.mult, ALU.add)
                    steps.mark(ins)

                def ys(m, s, k):
                    n.need(dve, "product", m)
                    n.need_load(dve, "x", k, s)
                    if last:
                        n.need(dve, "turned2", m, back=SLOTS)
                    else:
                        n.need_stored(dve, "o1", k, s)
                        n.need(dve, "out", m, back=SLOTS)
                    for j in range(GT):
                        ins = dve.scalar_tensor_tensor(t[:, s, j, :], po[s % 2][:, j, :], g["dis"][:, bass.ds(m * GT + j, 1)],
                                                       add[:, s, j, :], ALU.mult, ALU.add)
                    mark = steps.mark(ins)
                    yield
                    steps.wait(mark)
                    ins = dve.scalar_tensor_tensor(y[:, s], t[:, s], 0.0, xb[:, s], ALU.max, ALU.add)
                    if last:
                        n.done(ins, "y")
                    else:
                        mark = steps.mark(ins)
                        yield
                        steps.wait(mark)
                        yield from stats(dve, steps, y[:, s], st[:, s], mv[:, s], n, "y")

                def zs(m, s, k):
                    n.need(dve, "std", m)
                    n.need(dve, "out", m, back=SLOTS)
                    n.need_stored(dve, "o2", k, s)
                    yield from scaled(dve, steps, n, o2[:, s], mv[:, s], std[:, s, :], coef[:, s],
                                      g["dis"][:, bass.ds(m * GT, GT)])

                def vs(m, s, k):
                    n.need(dve, "product2", m)
                    n.need_load(dve, "x2", k, s)
                    mark = steps.mark(dve.tensor_tensor(z[:, s], po2[:], n.in_bufs["x2"][:, s], ALU.add))
                    yield
                    steps.wait(mark)
                    yield from stats(dve, steps, z[:, s], st[:, s], mv[:, s], n, "v")

                def x3s(m, s, k):
                    n.need(dve, "std", m)
                    n.need_stored(dve, "o1", k, s)
                    n.need(dve, "turned3", m, back=SLOTS)
                    yield from normalise(dve, steps, o1[:, s], z[:, s], mv[:, s], std[:, s, :], rstd[:, s],
                                         lambda ins: n.done(ins, "x3"))
                if last:
                    in_turn(dve, [(8, x3s), (6, vs), (3, ys), (0, aggs)], steps, links=6)
                else:
                    in_turn(dve, [(5, zs), (3, ys), (0, aggs)], steps, links=7)

def gat_nodes(nc, g, last, out):
    with Phase(nc) as ph:
        bias = g["gb2"] if last else g["gb1"]
        o = ph.sb("o", [P, SLOTS, GT, D])
        sc = ph.sb("sc", [P, SLOTS, GT, SCORES])
        if last:
            loads, stores = [("p", g["p2"], "low", 0), ("x3", g["x3"], "sum", 5)], [("o", out, o, "out", 8)]
        else:
            loads, stores = [("p", g["p1"], "low", 0)], [("o", g["p2"], o, "out", 5), ("sc", g["scores"], sc, "out", 5)]
        n = Nodes(nc, ph, g, loads, stores,
                  ("low", "ex", "v", "sum", "turned", "copied", "product", "y", "std", "out", "shared", "biased"))
        pb, cb = n.in_bufs["p"], n.pieces
        rden = ph.sb("rden", [P, SLOTS, GT, HEADS])
        y = ph.sb("y", [P, SLOTS, GT, D])
        u, low, v = (ph.sb(k, [P, SLOTS, GT, D]) for k in ("u", "low", "v"))
        if last:
            biased, above = (ph.sb(k, [P, SLOTS, GT, D]) for k in ("biased", "above"))
        vT = ph.sb("vT", [P, SLOTS, 2 * GT * P])
        minus = ph.sb("minus", [P, 1])
        std, rstd = (ph.sb(k, [P, SLOTS, GT]) for k in ("std", "rstd"))
        st = ph.sb("st", [P, SLOTS, GT, 6])
        mv = ph.sb("mv", [P, SLOTS, GT, 2])
        pv = [ph.ps(f"pv{k}", [P, 2 * GT * P]) for k in range(2)]
        po = [ph.ps(f"po{k}", [P, GT, BANK]) for k in range(2)]
        minus_ready = ph.sem("minus_ready")

        def heads(x):
            return x.rearrange("p j (h c) -> p j h c", h=HEADS)

        def per_head(x):
            return x.unsqueeze(3).to_broadcast([P, GT, HEADS, HID])
        with nc.Block() as block:
            @block.sync
            def _(sp):
                n.traffic(sp)

            @block.gpsimd
            def _(pool):
                n.gather(pool, *(() if last else (sc, 5 + SLOTS + 1)))

            @block.tensor
            def _(pe):
                n.start(pe, "turned", "product")
                if not last:
                    def transposes(m, s, k):
                        n.need(pe, "copied", m, back=2)
                        n.need(pe, "v", m)
                        n.done(turn(pe, pv[s % 2], v[:, s], g["ident"]), "turned")

                    def products(m, s, k):
                        n.need(pe, "copied", m)
                        n.need(pe, "out", m, back=2)
                        n.done(times(pe, po[s % 2], vT[:, s], g["g2w"], 0, CW), "product")
                    in_turn(pe, [(3, transposes), (4, products)])

            @block.scalar
            def _(act):
                n.start(act, "ex", "copied", "std")
                if not last:
                    n.start(act, "out")
                    act.wait_ge(minus_ready, 1)
                if last:
                    n.start(act, "shared")

                def shares(m, s, k):
                    n.need(act, "low", m)
                    n.need(act, "biased", m, back=SLOTS)
                    for j in range(GT):
                        for h in range(HEADS):
                            ins = act.activation(low[:, s, j, h * HID:(h + 1) * HID], u[:, s, j, h * HID:(h + 1) * HID],
                                                 ACT.Copy, scale=rden[:, s, j, h:h + 1])
                    n.done(ins, "shared")

                def elus(m, s, k):
                    n.need(act, "biased", m)
                    n.need(act, "sum", m, back=SLOTS)
                    act.activation(v[:, s], biased[:, s], ACT.Exp)
                    n.done(act.activation(above[:, s], biased[:, s], ACT.Relu), "ex")

                def exps(m, s, k):
                    n.need(act, "low", m)
                    n.done(act.activation(low[:, s], low[:, s], ACT.Exp), "ex")

                def copies(m, s, k):
                    n.need(act, "turned", m)
                    n.need(act, "product", m, back=SLOTS)
                    n.done(act.activation(vT[:, s, :], pv[s % 2][:], ACT.Identity, bias=minus[:]), "copied")

                def rows(m, s, k):
                    n.need(act, "product", m)
                    n.need_stored(act, "o", k, s)
                    n.need_stored(act, "sc", k, s)
                    n.need_scattered(act, k, s)
                    act.activation(o[:, s], po[s % 2][:, :, 0:D], ACT.Copy)
                    n.done(act.activation(sc[:, s], po[s % 2][:, :, D:CW], ACT.Copy), "out")

                def stds(m, s, k):
                    if s % 2 == 0:
                        return
                    n.need(act, "y", m)
                    n.need(act, "out", m, back=SLOTS)
                    act.activation(std[:, s - 1:s + 1, :], mv[:, s - 1:s + 1, :, 1], ACT.Sqrt,
                                   bias=g["eps"][:]).then_inc(n.sig["std"], 2)
                if last:
                    in_turn(act, [(6, stds), (4, elus), (2, shares)])
                else:
                    in_turn(act, [(3, copies), (5, rows), (1, exps)])

            @block.vector
            def _(dve):
                n.start(dve, "low", "v", "sum", "y")
                if last:
                    n.start(dve, "out", "biased")
                dve.memset(minus[:], -1.0).then_inc(minus_ready, 1)
                n.first_indices(dve)
                steps = Steps(dve, n.step)

                def lows(m, s, k):
                    n.need_pieces(dve, k, s)
                    n.need_load(dve, "p", k, s)
                    if last:
                        n.need(dve, "shared", m, back=SLOTS)
                    dve.reciprocal(rden[:, s], cb[:, s, :, D:D + HEADS])
                    mark = steps.mark(dve.tensor_tensor(heads(u[:, s]), heads(pb[:, s]), per_head(cb[:, s, :, D + HEADS:CW]), ALU.mult))
                    yield
                    steps.wait(mark)
                    ins = dve.tensor_tensor(u[:, s], u[:, s], cb[:, s, :, 0:D], ALU.add)
                    if last:
                        n.done(ins, "low")
                        n.next_indices(dve, m, s)
                        return
                    mark = steps.mark(ins)
                    n.next_indices(dve, m, s)
                    yield
                    steps.wait(mark)
                    mark = steps.mark(dve.tensor_tensor(heads(u[:, s]), heads(u[:, s]), per_head(rden[:, s]), ALU.mult))
                    yield
                    steps.wait(mark)
                    mark = steps.mark(dve.tensor_tensor(u[:, s], u[:, s], bias[:], ALU.add))
                    yield
                    steps.wait(mark)
                    n.done(dve.tensor_scalar(low[:, s], u[:, s], 0.0, None, ALU.min), "low")

                def biases(m, s, k):
                    n.need(dve, "shared", m)
                    n.need(dve, "ex", m, back=SLOTS)
                    n.done(dve.tensor_tensor(biased[:, s], low[:, s], bias[:], ALU.add), "biased")

                def vs(m, s, k):
                    n.need(dve, "ex", m)
                    n.need(dve, "turned", m, back=SLOTS)
                    n.done(dve.scalar_tensor_tensor(v[:, s], u[:, s], 0.0, low[:, s], ALU.max, ALU.add), "v")

                def ys(m, s, k):
                    n.need(dve, "ex", m)
                    n.need_load(dve, "x3", k, s)
                    mark = steps.mark(dve.scalar_tensor_tensor(y[:, s], v[:, s], 1.0, above[:, s], ALU.min, ALU.add))
                    yield
                    steps.wait(mark)
                    n.done(dve.scalar_tensor_tensor(y[:, s], y[:, s], -1.0, n.in_bufs["x3"][:, s], ALU.add, ALU.add), "sum")
                    yield
                    n.need(dve, "sum", m)
                    yield from stats(dve, steps, y[:, s], st[:, s], mv[:, s], n, "y")

                def outs(m, s, k):
                    n.need(dve, "std", m)
                    n.need_stored(dve, "o", k, s)
                    yield from normalise(dve, steps, o[:, s], y[:, s], mv[:, s], std[:, s, :], rstd[:, s],
                                         lambda ins: n.done(ins, "out"))
                if last:
                    in_turn(dve, [(8, outs), (5, ys), (3, biases), (0, lows)], steps, links=4)
                else:
                    in_turn(dve, [(2, vs), (0, lows)], steps, links=4)

_INS = ["x", "src", "dst", "edge_attr_64", "edge_weight", "L0_gnn_W", "L0_gnn_b", "L1_gnn_W", "L1_gnn_A", "L2_gnn_ln6_g",
        "L2_gnn_ln6_b", "L2_gnn_W6", "L2_gnn_b6", "L2_gnn_ln7_g", "L2_gnn_ln7_b", "L2_gnn_W7", "L2_gnn_b7", "L2_gnn_Wp",
        "L2_gnn_bp", "L3_gnn_W1", "L3_gnn_att_src1", "L3_gnn_att_dst1", "L3_gnn_b1", "L3_gnn_W2", "L3_gnn_att_src2",
        "L3_gnn_att_dst2", "L3_gnn_b2"]
_OUTS = [((50000, 256), "float32")]


def kernel(**inputs):
    import numpy as _np
    import concourse.bacc as _bacc
    from concourse import mybir as _mybir
    from concourse.bass_utils import run_bass_kernel_spmd as _run

    nc = _bacc.Bacc("TRN2", target_bir_lowering=False, num_devices=1)
    arrays, args = {}, {}
    for name in _INS:
        a = _np.ascontiguousarray(inputs[name])
        arrays[f"in_{name}_dram"] = a
        args[name] = nc.dram_tensor(f"in_{name}_dram", a.shape, _mybir.dt.from_np(a.dtype), kind="ExternalInput").ap()
    shape, dtype = _OUTS[0]
    out = nc.dram_tensor("out_0_dram", shape, _mybir.dt.from_np(_np.dtype(dtype)), kind="ExternalOutput").ap()
    build(nc, args, out)
    r = _run(nc, [arrays], core_ids=[0])
    return r.results[0]["out_0_dram"]
```
